# Optimizing a Trainium2 kernel written in Bass

```python
import numpy as np
import jax
import jax.numpy as jnp

def _softmax(x, axis=-1):
    return jax.nn.softmax(x, axis=axis)

def _gelu(x):
    return jax.nn.gelu(x, approximate=True)

def _silu(x):
    return jax.nn.silu(x)

def _sigmoid(x):
    return jax.nn.sigmoid(x)

def _layernorm(x, axis=-1, eps=1e-05):
    m = jnp.mean(x, axis=axis, keepdims=True)
    v = jnp.var(x, axis=axis, keepdims=True)
    return (x - m) / jnp.sqrt(v + eps)

def _scatter_add(tgt, idx, src, axis=0):
    return tgt.at[idx].add(src)

def _segment_sum(src, seg, n):
    return jax.ops.segment_sum(src, seg, n)
kernel_name = 'mk_gnn_ffn_d1_gnn_r32_4f9da9'

def setup_inputs(seed: int=0):
    np.random.seed(seed)
    _w = jnp.asarray

    def _rec_inputs():
        import jax
        import jax.numpy as jnp
        _gk = jax.random.key(seed)
        x = -0.0003713 + 1 * jax.random.normal(jax.random.fold_in(_gk, 1), (3125, 256), jnp.float32)
        _s = jax.random.randint(jax.random.fold_in(_gk, 2), (25000,), 0, 3125, jnp.int32)
        _d = jax.random.randint(jax.random.fold_in(_gk, 3), (25000,), 0, 3125, jnp.int32)
        _loop = jnp.arange(3125, dtype=jnp.int32)
        src = jnp.concatenate([_s, _d, _loop])
        dst = jnp.concatenate([_d, _s, _loop])
        _o = jnp.argsort(dst, stable=True)
        src = src[_o]
        dst = dst[_o]
        return (x, src, dst)
    x, src, dst = _rec_inputs()

    def _L0_gnn_setup():
        import jax, jax.numpy as jnp
        import numpy as np
        N_NODES = 50000
        N_EDGES = 25000
        D_IN = 256
        D_OUT = 256
        key = jax.random.key(seed)
        k_feat, k_src, k_dst, k_ws, k_wn, k_b = jax.random.split(key, 6)
        feat = jax.random.normal(k_feat, (N_NODES, D_IN), dtype=jnp.float32)
        src = jax.random.randint(k_src, (N_EDGES,), 0, N_NODES)
        dst = jax.random.randint(k_dst, (N_EDGES,), 0, N_NODES)
        scale = 1.0 / np.sqrt(D_IN)
        W_self = jax.random.normal(k_ws, (D_IN, D_OUT), dtype=jnp.float32) * scale
        W_neigh = jax.random.normal(k_wn, (D_IN, D_OUT), dtype=jnp.float32) * scale
        b = jnp.zeros((D_OUT,), dtype=jnp.float32)
        return {'feat': feat, 'W_self': W_self, 'W_neigh': W_neigh, 'b': b, 'src': src, 'dst': dst}
    _L0_gnn_all = _L0_gnn_setup()
    _L0_gnn_in = {k: v for k, v in _L0_gnn_all.items() if k in ('W_self', 'W_neigh', 'b')}
    del _L0_gnn_all

    def _L0_ffn_setup():
        import jax, jax.numpy as jnp
        import numpy as np
        B, S, H, F, E, K = (8, 128, 256, 512, 16, 2)
        EPS = 1e-05
        key = jax.random.key(seed)
        ks = jax.random.split(key, 9)
        sc = 0.02
        return {'x': jax.random.normal(ks[0], (B, S, H), dtype=jnp.float32), 'gate_w': jax.random.normal(ks[1], (H, E), dtype=jnp.float32) * sc, 'gate_b': jnp.zeros((E,), dtype=jnp.float32), 'w1': jax.random.normal(ks[2], (E, H, F), dtype=jnp.float32) * sc, 'b1': jnp.zeros((E, F), dtype=jnp.float32), 'w2': jax.random.normal(ks[3], (E, F, H), dtype=jnp.float32) * sc, 'b2': jnp.zeros((E, H), dtype=jnp.float32), 'gamma': jnp.ones((H,), dtype=jnp.float32), 'beta': jnp.zeros((H,), dtype=jnp.float32)}
    _L0_ffn_all = _L0_ffn_setup()
    _L0_ffn_in = {k: v for k, v in _L0_ffn_all.items() if k in ('gate_w', 'gate_b', 'w1', 'b1', 'w2', 'b2', 'gamma', 'beta')}
    del _L0_ffn_all
    return {'x': x, 'src': src, 'dst': dst, 'L0_gnn_W_self': _L0_gnn_in['W_self'], 'L0_gnn_W_neigh': _L0_gnn_in['W_neigh'], 'L0_gnn_b': _L0_gnn_in['b'], 'L0_ffn_gate_w': _L0_ffn_in['gate_w'], 'L0_ffn_gate_b': _L0_ffn_in['gate_b'], 'L0_ffn_w1': _L0_ffn_in['w1'], 'L0_ffn_b1': _L0_ffn_in['b1'], 'L0_ffn_w2': _L0_ffn_in['w2'], 'L0_ffn_b2': _L0_ffn_in['b2'], 'L0_ffn_gamma': _L0_ffn_in['gamma'], 'L0_ffn_beta': _L0_ffn_in['beta']}

def reference(x, src, dst, L0_gnn_W_self, L0_gnn_W_neigh, L0_gnn_b, L0_ffn_gate_w, L0_ffn_gate_b, L0_ffn_w1, L0_ffn_b1, L0_ffn_w2, L0_ffn_b2, L0_ffn_gamma, L0_ffn_beta):
    import jax
    import jax.numpy as jnp

    def _L0_gnn_ref(feat, W_self, W_neigh, b, src, dst):
        import jax, jax.numpy as jnp
        import numpy as np
        N_NODES = 50000
        N_EDGES = 25000
        D_IN = 256
        D_OUT = 256
        n = feat.shape[0]
        msg = feat[src]
        agg = jax.ops.segment_sum(msg, dst, num_segments=n)
        deg = jax.ops.segment_sum(jnp.ones_like(dst, dtype=feat.dtype), dst, num_segments=n)
        h_neigh = agg / jnp.maximum(deg, 1.0)[:, None]
        out = feat @ W_self + h_neigh @ W_neigh + b
        return out

    def _L0_ffn_ref(x, gate_w, gate_b, w1, b1, w2, b2, gamma, beta):
        import jax, jax.numpy as jnp
        import numpy as np
        B, S, H, F, E, K = (8, 128, 256, 512, 16, 2)
        EPS = 1e-05
        gate_logits = x @ gate_w + gate_b
        topk_vals, topk_idx = jax.lax.top_k(gate_logits, K)
        topk_w = jax.nn.softmax(topk_vals, axis=-1)
        h = jax.nn.relu(jnp.einsum('bsh,ehf->bsef', x, w1) + b1)
        expert_out = jnp.einsum('bsef,efh->bseh', h, w2) + b2
        sel = jnp.take_along_axis(expert_out, topk_idx[:, :, :, None], axis=2)
        moe = jnp.sum(topk_w[..., None] * sel, axis=2)
        y = x + moe
        mu = jnp.mean(y, axis=-1, keepdims=True)
        var = jnp.var(y, axis=-1, keepdims=True)
        return (y - mu) / jnp.sqrt(var + EPS) * gamma + beta
    x = x + _L0_gnn_ref(_layernorm(x, axis=-1), L0_gnn_W_self, L0_gnn_W_neigh, L0_gnn_b, src, dst)
    x = x + _L0_ffn_ref(_layernorm(x, axis=-1)[None], L0_ffn_gate_w, L0_ffn_gate_b, L0_ffn_w1, L0_ffn_b1, L0_ffn_w2, L0_ffn_b2, L0_ffn_gamma, L0_ffn_beta)[0]
    return x

_drawn_inputs = setup_inputs


def setup_inputs(seed=0):
    import zlib

    import numpy as np

    out = dict(_drawn_inputs(seed))
    spreads = {'L0_gnn_b': (0.0, 0.1),
     'L0_ffn_gate_b': (0.0, 0.286),
     'L0_ffn_b1': (0.0, 0.8),
     'L0_ffn_b2': (0.0, 0.269),
     'L0_ffn_gamma': (1.0, 0.2),
     'L0_ffn_beta': (0.0, 0.1)}
    factors = {}
    for name, (base, spread) in spreads.items():
        noise = np.random.default_rng([zlib.crc32(name.encode()), seed]).standard_normal(out[name].shape)
        drawn = base * np.exp(spread * noise) if base else spread * noise
        out[name] = jnp.asarray(drawn.astype(out[name].dtype))
    for name, factor in factors.items():
        out[name] = (out[name] * factor).astype(out[name].dtype)
    return out
```

```python
import concourse.bass as bass
from concourse import mybir
from contextlib import ExitStack

N = 3125
D = 256
E = 53125
NEXP = 16
F = 512
EPS = 1e-5

P = 128
KC = D // P
FC = F // P
BT = 125
NB = N // BT
GB = 5
NG = NB // GB
GT = GB * BT

ET = -(-E // P)
TPR = 8
ER = ET // TPR
ETP = ET + 8
QT = 4
QR = 4
RING = QT * QR
NIT = ET // RING
AGGW = N + P + 11
FAR = 1.0e6
NWIN = -(-N // P)

WSS = 16.0
WS1 = 16.0
WS2 = 64.0
REG = 26 * P
DUMMY = NEXP * REG
ROW = D + 2
NITEM = NEXP + (2 * N - NEXP) // P
SKIP = 1 << 20
ARENA = 7440
NTHR = -(-N // P)


def build(nc, x, src, dst, w_self, w_neigh, gnn_b, gate_w, gate_b, w1, b1, w2, b2, gamma, beta, out):
    f32, f16, i32, u32 = mybir.dt.float32, mybir.dt.float16, mybir.dt.int32, mybir.dt.uint32
    ALU = mybir.AluOpType
    ACT = mybir.ActivationFunctionType
    AX = mybir.AxisListType

    ctx = ExitStack()
    with ctx:
        def sb(name, shape, dt=f32):
            return ctx.enter_context(nc.sbuf_tensor(name, shape, dt))

        def sem(name):
            return ctx.enter_context(nc.semaphore(name))

        def dram(name, shape, dt=f32):
            return nc.dram_tensor(name, shape, dt, kind="Internal").ap()

        h_tab = dram("h_tab", [N, 2 * D], f16)
        s_tab = dram("s_tab", [N, D])
        xx_tab = dram("xx_tab", [N, 2 * D])
        xs = dram("xs", [DUMMY + P, ROW])
        z_tab = dram("z_tab", [2 * N, D])

        W1 = sb("W1", [P, NEXP, 2, KC, F], f16)
        W2 = sb("W2", [P, NEXP, 2, FC, D], f16)
        AGG = sb("AGG", [P, KC + 1, AGGW])
        ident = sb("ident", [P, P])
        ident16 = sb("ident16", [P, P], f16)
        iota = sb("iota", [P, P])
        iotap = sb("iotap", [P, 1])
        iota16 = sb("iota16", [P, P], f16)
        ones = sb("ones", [P, P])
        ones16 = sb("ones16", [P, P], f16)
        bias_one = sb("bias_one", [1, BT])
        ones_row = ones[0:1, 0:BT]
        lower = sb("lower", [BT, BT])
        ws = sb("ws", [P, 2, KC, D], f16)
        wn = sb("wn", [P, KC, D])
        gw = sb("gw", [P, KC, NEXP])
        brow = sb("brow", [1, D])
        gbrow = sb("gbrow", [1, NEXP])
        gamma_b = sb("gamma_b", [BT, D])
        beta_b = sb("beta_b", [BT, D])
        b2s = sb("b2s", [NEXP, D])
        b1T = sb("b1T", [P, NEXP * FC])
        acc = sb("acc", [BT, NEXP])
        ebase = sb("ebase", [BT, NEXP])
        tok2 = sb("tok2", [BT, GB, 2])
        items = sb("items", [1, 2, NITEM], i32)
        irregular = sb("irregular", [1, 1], i32)
        padrow = sb("padrow", [1, NEXP], i32)
        arena = sb("arena", [P, ARENA])

        at = [0]

        def part(words):
            a = at[0]
            at[0] += words
            assert at[0] <= ARENA, at[0]
            return arena[:, a:a + words]

        pro = W2[:, :, :, :, :].rearrange("p e s c f -> p (e s c f)").bitcast(f32)
        X = pro[0:BT, 0:NB * D].rearrange("p (b d) -> p b d", d=D)
        H = pro[0:BT, NB * D:2 * NB * D].rearrange("p (b d) -> p b d", d=D)
        pr1 = W1[:, :, :, :, :].rearrange("p e s c f -> p (e s c f)").bitcast(f32)
        H16 = pr1[0:BT, 0:NB * D].bitcast(f16).rearrange("p (b a d) -> p b a d", a=2, d=D)
        o = NB * D
        L = TPR * P
        srow = pr1[0:ER, o:o + L].bitcast(i32)
        drow = pr1[0:ER, o + L:o + 2 * L].bitcast(i32)
        drow2 = pr1[0:ER, o + 2 * L:o + 3 * L].bitcast(i32)
        srowf = pr1[0:ER, o + 3 * L:o + 4 * L]
        drowf = pr1[0:ER, o + 4 * L:o + 5 * L]
        drowf2 = pr1[0:ER, o + 5 * L:o + 6 * L]
        o += 6 * L
        wsf = pr1[:, o:o + KC * D].rearrange("p (k d) -> p k d", d=D)
        b1rows = pr1[0:NEXP * FC, o + KC * D:o + KC * D + P]
        o += KC * D + P
        stats0 = pr1[0:BT, o:o + NB * 6].rearrange("p (b s) -> p b s", s=6)
        mv0 = pr1[0:BT, o + 200:o + 200 + NB * 2].rearrange("p (b s) -> p b s", s=2)
        rstd0 = pr1[0:BT, o + 260:o + 260 + NB]
        tmp0 = [pr1[0:BT, a:a + NB] for a in (o + 290, o + 320)]
        bmin = pr1[0:ER, o + 350:o + 351]
        bmax = pr1[0:ER, o + 351:o + 352]
        bad = pr1[0:ER, o + 352:o + 353]
        badf = pr1[0:1, o + 353:o + 354]
        assert o + 354 <= NEXP * 2 * KC * F // 2

        msg = part(RING * D).bitcast(f16).rearrange("p (q u a d) -> p q u a d", u=QT, a=2, d=D)
        oh = part(2 * QT * P // 2).bitcast(f16).rearrange("p (h u c) -> p h u c", u=QT, c=P)
        wstg = part(KC * F)
        srcT = part(ETP)
        relT = part(ETP)
        base_row = part(ER).bitcast(i32)
        stage = part(RING).bitcast(i32).rearrange("p (h u) -> p h u", u=QT)
        hx_h = part(D).bitcast(f16).rearrange("p (a d) -> p a d", d=D)
        hx_x = part(D)
        hT = part(2 * KC * P // 2).bitcast(f16).rearrange("p (a k t) -> p a k t", a=2, k=KC)
        at[0] = 0
        XX = part(GB * 2 * D).rearrange("p (b a d) -> p b a d", a=2, d=D)
        xtT_w = part(GB * KC * P)
        xtT = xtT_w.rearrange("p (b k t) -> p b k t", k=KC, t=P)
        hn = xtT_w[:, 0:KC * GT].rearrange("p (k t) -> p k t", t=GT)
        GT_sb = xtT_w[:, 0:GB * P].rearrange("p (b t) -> p b t", t=P)
        pay_w = part(GB * 2 * ROW)
        pay = pay_w.rearrange("p (b k w) -> p b k w", k=2, w=ROW)
        pay_i = pay_w.bitcast(i32).rearrange("p (b k w) -> p b k w", k=2, w=ROW)
        pay_h = pay_w.bitcast(f16).rearrange("p (b k w) -> p b k w", k=2, w=2 * ROW)
        m8 = part(GB * 8).rearrange("p (b m) -> p b m", m=8)
        i8 = part(GB * 8).bitcast(u32).rearrange("p (b m) -> p b m", m=8)
        stats = part(GB * 6).rearrange("p (b s) -> p b s", s=6)
        mv = part(GB * 2).rearrange("p (b s) -> p b s", s=2)
        rstd = part(GB)
        tmp = [part(GB)[0:BT, :] for _ in range(2)]
        wt = part(GB * 2).rearrange("p (b k) -> p b k", k=2)
        dl = part(GB)
        e1 = part(GB)
        idxf = part(GB * 2).rearrange("p (b k) -> p b k", k=2)
        oh2 = part(GB * 2 * NEXP).rearrange("p (b k e) -> p b k e", k=2, e=NEXP)
        ohs = part(GB * NEXP).rearrange("p (b e) -> p b e", e=NEXP)
        posb = part(GB * NEXP).rearrange("p (b e) -> p b e", e=NEXP)
        prod = part(GB * 2 * NEXP).rearrange("p (b k e) -> p b k e", k=2, e=NEXP)
        gates4 = part(GB * 2 * NEXP)[0:BT, :].rearrange("p (b k e) -> p b k e", k=2, e=NEXP)
        gates = part(GB * NEXP).rearrange("p (b e) -> p b e", e=NEXP)
        slotf = part(GB * 2).rearrange("p (b k) -> p b k", k=2)
        sloti = part(GB * 2).bitcast(i32).rearrange("p (b k) -> p b k", k=2)
        gsum = part(NEXP)
        cnt = part(NEXP)
        ntile = part(NEXP)
        pincl = part(NEXP)
        cmp2 = part(NEXP)
        scr = part(16)
        padt = xtT_w[:, 0:ROW]
        thr = xtT_w[:, ROW:ROW + NTHR]
        cmp1 = xtT_w[:, 2 * ROW:2 * ROW + NEXP * NTHR].rearrange("p (e k) -> p e k", k=NTHR)
        at[0] = 0
        xsr = part(4 * ROW).rearrange("p (s w) -> p s w", w=ROW)
        xT = part(2 * 2 * KC * P // 2).bitcast(f16).rearrange("p (s a k t) -> p s a k t", s=2, a=2, k=KC)
        meta = part(4 * 2).rearrange("p (s w) -> p s w", w=2)
        b1e = part(2 * FC).rearrange("p (s c) -> p s c", c=FC)
        hr = part(2 * F).rearrange("p (s t) -> p s t", t=F)
        hh = part(2 * F // 2).bitcast(f16).rearrange("p (s t) -> p s t", t=F)
        hl = part(2 * F // 2).bitcast(f16).rearrange("p (s t) -> p s t", t=F)
        yo = part(4 * D).rearrange("p (s d) -> p s d", d=D)
        agg_w = AGG[:, :, :].rearrange("p k c -> p (k c)").bitcast(f16)
        w1e = agg_w[:, 0:4 * KC * F].rearrange("p (s a k f) -> p s a k f", s=2, a=2, k=KC)
        w2e = agg_w[:, 4 * KC * F:4 * (KC * F + FC * D)].rearrange("p (s a c d) -> p s a c d", s=2, a=2, c=FC)
        agg_f = AGG[:, :, :].rearrange("p k c -> p (k c)")
        at[0] = 0
        XX3 = [part(GB * 2 * D).rearrange("p (b a d) -> p b a d", a=2, d=D) for _ in range(2)]
        Z = [agg_f[:, s * GB * 2 * D:(s + 1) * GB * 2 * D].rearrange("p (b k d) -> p b k d", k=2, d=D) for s in range(2)]
        assert 2 * GB * 2 * D <= (KC + 1) * AGGW
        Y = [agg_f[:, (4 + s) * GB * D:(5 + s) * GB * D].rearrange("p (b d) -> p b d", d=D) for s in range(2)]
        stats3 = part(GB * 6).rearrange("p (b s) -> p b s", s=6)
        mv3 = [part(GB * 2)[0:BT, :].rearrange("p (b s) -> p b s", s=2) for _ in range(2)]
        rstd3 = [part(GB)[0:BT, :] for _ in range(2)]
        nmr3 = [part(GB)[0:BT, :] for _ in range(2)]
        tmp3 = [part(GB)[0:BT, :] for _ in range(2)]

        PS = ctx.enter_context(nc.psum_tensor("PS", [P, 8, 512], f32))
        p_agg = [PS[:, b * (KC + 1):(b + 1) * (KC + 1), 0:P] for b in range(2)]
        p_hT = PS[:, 6, 0:KC * P].bitcast(f16).rearrange("p (a k t) -> p a k t", a=2, k=KC)
        p_s = PS[0:BT, 7, 0:D]
        p_n = PS[0:BT, 0:3, :].rearrange("p n (h d) -> p (n h) d", d=D)
        p_xT = PS[:, 3:6, :].rearrange("p n (h t) -> p (n h) t", t=P)
        p_lg = PS[0:BT, 6, 0:GB * NEXP].rearrange("p (b e) -> p b e", e=NEXP)
        p_pos = PS[0:BT, 7, 0:GB * NEXP].rearrange("p (b e) -> p b e", e=NEXP)
        p_gT = PS[0:NEXP, 6:8, :].rearrange("p n (h t) -> p (n h) t", t=P)
        p_cnt = PS[:, 0, 0:NEXP]
        p_item = PS[0:1, 1, 0:2 * P].rearrange("p (a t) -> p a t", t=P)
        p_x16 = [PS[:, s, 0:256].bitcast(f16).rearrange("p (a k t) -> p a k t", a=2, k=KC) for s in range(2)]
        p_h = [PS[:, 2 + s, :] for s in range(2)]
        p_y = [PS[:, 4 + s, 0:D] for s in range(2)]
        p_sum = [PS[0:BT, 3 * s:3 * s + 3, :].rearrange("p n (h d) -> p (n h) d", d=D) for s in range(2)]

        const_loaded = sem("const_loaded")
        consts_made = sem("consts_made")
        edges_loaded = sem("edges_loaded")
        edge_pads = sem("edge_pads")
        x_loaded = [sem(f"x_loaded{c}") for c in range(NG)]
        h_made = sem("h_made")
        h_hi = sem("h_hi")
        h_lo = sem("h_lo")
        flag_ready = sem("flag_ready")
        fb_staged = sem("fb_staged")
        fb_gathered = [sem(f"fb_gathered{u}") for u in range(TPR)]
        fb_oh = sem("fb_oh")
        fb_sums = sem("fb_sums")
        fb_done = sem("fb_done")
        fb_moved = sem("fb_moved")
        h_stored = sem("h_stored")
        dve_step = sem("dve_step")
        waits_passed = sem("waits_passed")
        rows_ready = sem("rows_ready")
        edge_T = sem("edge_T")
        edge_out = sem("edge_out")
        stage_ready = sem("stage_ready")
        gathered = [sem(f"gathered{u}") for u in range(QR)]
        oh_ready = sem("oh_ready")
        quads_done = sem("quads_done")
        adds_done = sem("adds_done")
        hx_loaded = sem("hx_loaded")
        hT_made = sem("hT_made")
        hT_copied = sem("hT_copied")
        self_done = sem("self_done")
        sout_ready = sem("sout_ready")
        s_stored = sem("s_stored")
        w_loaded = sem("w_loaded")
        w_hi = sem("w_hi")
        w_lo = sem("w_lo")
        s_back = sem("s_back")
        agg_norm = sem("agg_norm")
        neigh_done = sem("neigh_done")
        xt_made = sem("xt_made")
        xtT_made = sem("xtT_made")
        xtT_copied = sem("xtT_copied")
        logits = sem("logits")
        delta = sem("delta")
        expd = sem("expd")
        ohs_made = sem("ohs_made")
        pos_made = sem("pos_made")
        hi_made = sem("hi_made")
        lo_made = sem("lo_made")
        rows_made = sem("rows_made")
        meta_made = sem("meta_made")
        gates_made = sem("gates_made")
        gT_made = sem("gT_made")
        gT_copied = sem("gT_copied")
        b2_made = sem("b2_made")
        xx_ready = sem("xx_ready")
        xx_stored = sem("xx_stored")
        scattered = sem("scattered")
        rows_free = sem("rows_free")
        counted = sem("counted")
        item_cols = sem("item_cols")
        item_T = sem("item_T")
        items_ready = sem("items_ready")
        padded = sem("padded")
        xs_in = [sem(f"xs_in{s}") for s in range(4)]
        x16_made = sem("x16_made")
        x16_copied = sem("x16_copied")
        meta_taken = sem("meta_taken")
        w1_copied = sem("w1_copied")
        w2_copied = sem("w2_copied")
        l1_done = sem("l1_done")
        relu_done = sem("relu_done")
        hi_split = sem("hi_split")
        h_split = sem("h_split")
        l2_done = sem("l2_done")
        yo_ready = sem("yo_ready")
        yo_out = [sem(f"yo_out{s}") for s in range(4)]
        zx_loaded = [sem(f"zx_loaded{s}") for s in range(2)]
        summed = sem("summed")
        stats_made = sem("stats_made")
        normed = sem("normed")
        out_ready = sem("out_ready")
        out_stored = sem("out_stored")

        out_b = out.rearrange("(c b p) d -> c p b d", p=BT, b=GB)
        HT = TPR // 2

        x_b = x.rearrange("(c b p) d -> c p b d", p=BT, b=GB)
        h_b = h_tab.rearrange("(c b p) d -> c p b d", p=BT, b=GB)
        DMA = 16

        def carry(engine):
            engine.sem_inc(waits_passed, 1)

        def counted_link(engine, signal, base):
            n = [0]

            def link(ins, alone=False):
                n[0] += 1
                ins.then_inc(signal, 1)
                engine.wait_ge(signal, base + n[0])
                if alone:
                    carry(engine)
            return link, n

        def rsqrt(v, link, var, tmp, y):
            link(v.tensor_scalar(tmp[0], var, EPS, None, ALU.add))
            link(v.tensor_scalar(tmp[1].bitcast(i32), tmp[0].bitcast(i32), 1, None, ALU.logical_shift_right))
            link(v.tensor_scalar(y.bitcast(i32), tmp[1].bitcast(i32), -1.0, float(0x5F3759DF), ALU.mult, ALU.add))
            for _ in range(3):
                link(v.scalar_tensor_tensor(tmp[1], y, -0.5, y, ALU.mult, ALU.mult))
                link(v.tensor_tensor(tmp[1], tmp[1], tmp[0], ALU.mult))
                link(v.scalar_tensor_tensor(y, tmp[1], 1.5, y, ALU.add, ALU.mult))

        block = ctx.enter_context(nc.Block())

        SPANS = [(0, NEXP, True, True), (NEXP, NB, True, False), (NB, NIT, False, False)]

        @block.sync
        def _(sp):
            full = ER - 1
            rest = E - full * L
            sp.wait_ge(edge_pads, 3)
            for t, a in ((srow, src), (drow, dst), (drow2, dst)):
                sp.dma_start(t[0:full, :], a[0:full * L].rearrange("(r c) -> r c", c=L)).then_inc(edges_loaded, DMA)
                sp.dma_start(t[full:ER, 0:rest], a[full * L:E].rearrange("(r c) -> r c", r=1)).then_inc(edges_loaded, DMA)
            for c in range(NG):
                sp.dma_start(X[:, c * GB:(c + 1) * GB, :], x_b[c]).then_inc(x_loaded[c], DMA)
            for t, a in ((wsf, w_self.rearrange("(k p) d -> p k d", p=P)),
                         (wn[:, :, :], w_neigh.rearrange("(k p) d -> p k d", p=P)),
                         (gw[:, :, :], gate_w.rearrange("(k p) e -> p k e", p=P)),
                         (brow[:, :], gnn_b.rearrange("(a d) -> a d", a=1)),
                         (gbrow[:, :], gate_b.rearrange("(a d) -> a d", a=1)),
                         (gamma_b[:, :], gamma.rearrange("(a d) -> a d", a=1).to_broadcast([BT, D])),
                         (beta_b[:, :], beta.rearrange("(a d) -> a d", a=1).to_broadcast([BT, D])),
                         (b2s[:, :], b2),
                         (b1rows, b1.rearrange("e (c f) -> (e c) f", f=P))):
                sp.dma_start(t, a).then_inc(const_loaded, DMA)
            for c in range(NG):
                sp.wait_ge(h_lo, c + 1)
                sp.dma_start(h_b[c], H16[:, c * GB:(c + 1) * GB, :, :].rearrange("p b a d -> p b (a d)")).then_inc(h_stored, DMA)
            sp.wait_ge(h_stored, NG * DMA)
            sp.wait_ge(edge_out, 7)
            sp.sem_inc(w_lo, 1)
            sp.sem_inc(s_stored, DMA)
            sp.sem_inc(xx_stored, DMA)

            for lo, hi, own, experts in SPANS:
                with sp.Fori(lo, hi) as i:
                    if experts:
                        sp.wait_ge(w_lo, 2 * i + 1)
                        sp.dma_start(wstg.rearrange("p (k f) -> p k f", f=F),
                                     w1[bass.ds(i, 1), :, :].rearrange("e (k p) f -> p (e k) f", p=P)).then_inc(w_loaded, DMA)
                    if own:
                        sp.wait_ge(s_stored, DMA * (i + 1))
                        sp.dma_start(hx_h[0:BT, :, :], h_tab[bass.ds(i * BT, BT), :].rearrange("p (a d) -> p a d", a=2)).then_inc(hx_loaded, DMA)
                        sp.dma_start(hx_x[0:BT, :], x[bass.ds(i * BT, BT), :]).then_inc(hx_loaded, DMA)
                    if experts:
                        sp.wait_ge(w_lo, 2 * i + 2)
                        sp.dma_start(wstg.rearrange("p (c d) -> p c d", d=D),
                                     w2[bass.ds(i, 1), :, :].rearrange("e (c p) d -> p (e c) d", p=P)).then_inc(w_loaded, DMA)
                    if own:
                        sp.wait_ge(sout_ready, i + 2)
                        sp.dma_start(s_tab[bass.ds(i * BT, BT), :], hx_x[0:BT, :]).then_inc(s_stored, DMA)

            sp.wait_ge(s_stored, (NB + 1) * DMA)
            sp.wait_ge(adds_done, ER + 2)
            with sp.Fori(0, NG) as q:
                sp.wait_ge(xx_stored, (q + 1) * DMA)
                sp.dma_start(XX[0:BT, :, 0, :],
                             s_tab[bass.ds(q * GT, GT), :].rearrange("(b p) d -> p b d", p=BT)).then_inc(s_back, DMA)
                sp.wait_ge(xx_ready, q + 1)
                sp.dma_start(xx_tab[bass.ds(q * GT, GT), :].rearrange("(b p) (a d) -> p b a d", p=BT, a=2),
                             XX[0:BT, :, :, :]).then_inc(xx_stored, DMA)

            sp.wait_ge(items_ready, 1)
            with sp.Fori(0, NEXP) as e:
                row = sp.value_load(padrow[0:1, bass.ds(e, 1)], min_val=0, max_val=NEXP * REG - P)
                sp.dma_start(xs[bass.ds(row, P), :], padt).then_inc(padded, DMA)
            sp.dma_start(xs[DUMMY:DUMMY + P, :], padt).then_inc(padded, DMA)
            sp.wait_ge(padded, (NEXP + 1) * DMA)
            sp.wait_ge(scattered, NB * 2 * DMA)
            sp.wait_ge(xx_stored, (NG + 1) * DMA)

            with sp.Fori(0, NITEM // 4) as m:
                for s in range(4):
                    row = sp.value_load(items[0:1, 1, bass.ds(4 * m + s, 1)], min_val=0, max_val=DUMMY)
                    sp.wait_ge(x16_copied, 4 * m + s + 1)
                    sp.wait_ge(meta_taken, 4 * m + s + 1)
                    sp.dma_start(xsr[:, s, :], xs[bass.ds(row, P), :]).then_inc(xs_in[s], DMA)

            for s in range(4):
                sp.wait_ge(yo_out[s], NITEM // 4 * DMA)
            for q in range(NG):
                s = q % 2
                if q >= 2:
                    sp.wait_ge(out_stored, (q - 1) * DMA)
                sp.dma_start(XX3[s][0:BT, :, :, :],
                             xx_tab[q * GT:(q + 1) * GT, :].rearrange("(b p) (a d) -> p b a d", p=BT, a=2)).then_inc(zx_loaded[s], DMA)
                sp.dma_start(Z[s][0:BT, :, :, :],
                             z_tab[2 * q * GT:2 * (q + 1) * GT, :].rearrange("(b p k) d -> p b k d", p=BT, k=2)).then_inc(zx_loaded[s], DMA)
                if q >= 1:
                    sp.wait_ge(out_ready, q)
                    sp.dma_start(out_b[q - 1], Y[1 - s][0:BT, :, :]).then_inc(out_stored, DMA)
            sp.wait_ge(out_ready, NG)
            sp.dma_start(out_b[NG - 1], Y[(NG - 1) % 2][0:BT, :, :]).then_inc(out_stored, DMA)
            sp.wait_ge(out_stored, NG * DMA)

        @block.gpsimd
        def _(pool):
            g = nc.gpsimd
            g.iota(iota[:, :], [[1, P]], base=0, channel_multiplier=0, allow_small_or_imprecise_dtypes=True).then_inc(consts_made, 1)
            g.iota(iotap[:, :], [[0, 1]], base=0, channel_multiplier=1, allow_small_or_imprecise_dtypes=True).then_inc(consts_made, 1)
            g.iota(ebase[:, :], [[REG, NEXP]], base=0, channel_multiplier=0, allow_small_or_imprecise_dtypes=True).then_inc(consts_made, 1)
            g.iota(tok2[:, :, :], [[2 * BT, GB], [1, 2]], base=0, channel_multiplier=2, allow_small_or_imprecise_dtypes=True).then_inc(consts_made, 1)
            g.memset(ident[:, :], 0.0).then_inc(consts_made, 1)
            g.memset(lower[:, :], 0.0).then_inc(consts_made, 1)
            g.memset(ones[:, :], 1.0).then_inc(consts_made, 1)
            g.memset(acc[:, :], 0.0).then_inc(consts_made, 1)
            g.memset(ones16[:, :], 1.0).then_inc(consts_made, 1)
            g.memset(bias_one[:, :], WSS).then_inc(consts_made, 1)
            pool.wait_ge(consts_made, 10)
            g.affine_select(out=ident[:, :], in_=ident[:, :], compare_op=ALU.not_equal, fill=1.0,
                            base=0, pattern=[[-1, P]], channel_multiplier=1).then_inc(consts_made, 1)
            g.affine_select(out=lower[:, :], in_=lower[:, :], compare_op=ALU.is_ge, fill=1.0,
                            base=0, pattern=[[-1, BT]], channel_multiplier=1).then_inc(consts_made, 1)
            g.tensor_copy(iota16[:, :], iota[:, :]).then_inc(consts_made, 1)
            pool.wait_ge(consts_made, 13)
            g.tensor_copy(ident16[:, :], ident[:, :]).then_inc(consts_made, 1)
            for c in range(NG):
                bs = slice(c * GB, (c + 1) * GB)
                pool.wait_ge(h_hi, c + 1)
                g.tensor_tensor(H16[:, bs, 1, :], H[:, bs, :], H16[:, bs, 0, :], ALU.subtract).then_inc(h_lo, 1)

            pool.wait_ge(h_stored, NG * DMA)
            pool.wait_ge(flag_ready, 1)
            flag = pool.value_load(irregular[0:1, 0:1], min_val=0, max_val=1)
            with pool.If(flag == 1):
                with pool.Fori(0, NWIN) as w:
                    with pool.Fori(0, ER) as r:
                        pool.wait_ge(fb_staged, ER * w + r + 1)
                        carry(pool)
                        for j in range(TPR):
                            g.indirect_dma_start(msg[:, j // QT, j % QT, :, :].rearrange("p a d -> p (a d)"), None, h_tab[:, :],
                                                 bass.IndirectOffsetOnAxis(ap=stage[:, j // QT, j % QT:j % QT + 1], axis=0)
                                                 ).then_inc(fb_gathered[j], DMA)
            with pool.Fori(0, NIT) as i:
                for s in range(QR):
                    pool.wait_ge(stage_ready, QR * i + s + 1)
                    carry(pool)
                    for u in range(QT):
                        g.indirect_dma_start(msg[:, s, u, :, :].rearrange("p a d -> p (a d)"), None, h_tab[:, :],
                                             bass.IndirectOffsetOnAxis(ap=stage[:, s, u:u + 1], axis=0)
                                             ).then_inc(gathered[s], DMA)

            with pool.Fori(0, NG) as q:
                pool.wait_ge(rows_made, q + 1)
                pool.wait_ge(meta_made, q + 1)
                carry(pool)
                for b in range(GB):
                    for k in range(2):
                        g.indirect_dma_start(xs[:, :], bass.IndirectOffsetOnAxis(ap=sloti[0:BT, b, k:k + 1], axis=0),
                                             pay[0:BT, b, k, :], None).then_inc(scattered, DMA)
                pool.wait_ge(scattered, GB * 2 * DMA * (q + 1))
                pool.sem_inc(rows_free, 1)

            with pool.Fori(0, NITEM // 4) as m:
                for s in range(4):
                    pool.wait_ge(yo_ready, 4 * m + s + 3)
                    carry(pool)
                    g.indirect_dma_start(z_tab[:, :], bass.IndirectOffsetOnAxis(ap=meta[:, s, 0:1].bitcast(i32), axis=0),
                                         yo[:, s, :], None, bounds_check=2 * N - 1, oob_is_err=False).then_inc(yo_out[s], DMA)

        @block.scalar
        def _(act):
            a = nc.scalar
            for c in range(NG):
                bs = slice(c * GB, (c + 1) * GB)
                act.wait_ge(h_made, c + 1)
                a.activation(H16[:, bs, 0, :], H[:, bs, :], ACT.Copy).then_inc(h_hi, 1)
            act.wait_ge(edge_out, 7)
            act.wait_ge(h_stored, NG * DMA)
            flag = act.value_load(irregular[0:1, 0:1], min_val=0, max_val=1)
            with act.If(flag == 1):
                with act.Fori(0, NWIN) as w:
                    with act.Fori(0, ER) as r:
                        act.wait_ge(fb_done, ER * w + r + 1)
                        a.activation(stage[:, 0:2, :], srcT[:, bass.ds(TPR * r, TPR)].rearrange("p (h u) -> p h u", u=QT),
                                     ACT.Copy).then_inc(fb_staged, 1)
                act.wait_ge(fb_done, ER * NWIN + 1)

            def stage_quad(i, s):
                act.wait_ge(quads_done, QR * i + s + 1)
                a.activation(stage[:, s, :], srcT[:, bass.ds(RING * i + QT * s, QT)], ACT.Copy).then_inc(stage_ready, 1)

            for lo, hi, own, experts in SPANS:
                with act.Fori(lo, hi) as i:
                    stage_quad(i, 0)
                    stage_quad(i, 1)
                    if experts:
                        act.wait_ge(w_loaded, DMA * (2 * i + 1))
                        a.activation(W1[:, bass.ds(i, 1), 0, :, :].rearrange("p e k f -> p (e k f)"), wstg, ACT.Copy, scale=WS1).then_inc(w_hi, 1)
                    stage_quad(i, 2)
                    if own:
                        act.wait_ge(hT_made, i + 1)
                        a.activation(hT[:, :, :, 0:BT], p_hT[:, :, :, 0:BT], ACT.Copy).then_inc(hT_copied, 1)
                    stage_quad(i, 3)
                    if experts:
                        act.wait_ge(w_loaded, DMA * (2 * i + 2))
                        a.activation(W2[:, bass.ds(i, 1), 0, :, :].rearrange("p e c d -> p (e c d)"), wstg, ACT.Copy, scale=WS2).then_inc(w_hi, 1)

            with act.Fori(0, NG) as q:
                act.wait_ge(xtT_made, q + 1)
                a.activation(xtT[:, :, :, 0:BT], p_xT[:, 0:GB * KC, 0:BT].rearrange("p (b k) t -> p b k t", k=KC), ACT.Copy).then_inc(xtT_copied, 1)
                act.wait_ge(rows_free, q + 1)
                for k in range(2):
                    ins = a.activation(pay_h[0:BT, :, k, 0:D], XX[0:BT, :, 1, :], ACT.Copy)
                ins.then_inc(hi_made, 1)
                act.wait_ge(delta, q + 1)
                a.activation(e1[0:BT, :], dl[0:BT, :], ACT.Exp).then_inc(expd, 1)
                act.wait_ge(lo_made, q + 1)
                a.activation(pay_h[0:BT, :, 1, D:2 * D], pay_h[0:BT, :, 0, D:2 * D], ACT.Copy).then_inc(rows_made, 1)
                act.wait_ge(gT_made, q + 1)
                a.activation(GT_sb[0:NEXP, :, 0:BT], p_gT[:, 0:GB, 0:BT], ACT.Copy).then_inc(gT_copied, 1)

            def x_out(s, m):
                n = 4 * m + s
                act.wait_ge(x16_made, n + 1)
                act.wait_ge(l1_done, n + 1)
                a.activation(xT[:, s % 2, :, :, :], p_x16[s % 2], ACT.Copy).then_inc(x16_copied, 1)

            def relu(s, m):
                n = 4 * m + s
                act.wait_ge(l1_done, n + 3)
                act.wait_ge(w1_copied, n + 1)
                act.wait_ge(h_split, n + 1)
                for c in range(FC):
                    ins = a.activation(hr[:, s % 2, c * P:(c + 1) * P], p_h[s % 2][:, c * P:(c + 1) * P], ACT.Relu,
                                       bias=b1e[:, s % 2, c:c + 1], scale=1.0 / WS1)
                ins.then_inc(relu_done, 1)

            def weigh(s, m):
                n = 4 * m + s
                act.wait_ge(l2_done, n + 3)
                act.wait_ge(meta_taken, n + 5)
                if not (isinstance(m, int) and m == 0):
                    act.wait_ge(yo_out[s], DMA * m)
                a.activation(yo[:, s, :], p_y[s % 2], ACT.Copy, scale=meta[:, s, 1:2]).then_inc(yo_ready, 1)

            act.wait_ge(items_ready, 1)
            act.sem_inc(relu_done, 2)
            act.sem_inc(yo_ready, 2)
            act.sem_inc(x16_copied, 4)
            x_out(0, 0)
            x_out(1, 0)
            relu(0, 0)

            def act_items(m):
                for s in range(4):
                    x_out((s + 2) % 4, m + (s + 2) // 4)
                    relu((s + 1) % 4, m + (s + 1) // 4)
                    weigh(s, m)

            act_items(0)
            with act.Fori(1, NITEM // 4 - 1) as m:
                act_items(m)
            last = NITEM // 4 - 1
            for s in range(4):
                if s < 2:
                    x_out(s + 2, last)
                if s < 3:
                    relu(s + 1, last)
                weigh(s, last)

            for q in range(NG):
                act.wait_ge(stats_made, q + 1)
                if q >= 2:
                    act.wait_ge(out_stored, (q - 1) * DMA)
                for b in range(GB):
                    ins = a.activation(Y[q % 2][0:BT, b, :], p_sum[q % 2][:, b, :], ACT.Identity,
                                       bias=nmr3[q % 2][:, b:b + 1], scale=rstd3[q % 2][:, b:b + 1])
                ins.then_inc(normed, 1)

        @block.tensor
        def _(pe):
            t = nc.tensor
            pe.wait_ge(consts_made, 14)
            pe.wait_ge(rows_ready, 2)
            for j in range(TPR):
                t.transpose(PS[:, j, 0:ER], srowf[:, j * P:(j + 1) * P], ident[0:ER, 0:ER])
                t.transpose(PS[:, j, P:P + ER], drowf[:, j * P:(j + 1) * P], ident[0:ER, 0:ER])
            t.transpose(PS[0:1, 0, 2 * P:2 * P + ER], bmin, ident[0:ER, 0:ER])
            t.transpose(PS[0:1, 1, 2 * P:2 * P + ER], bad, ident[0:ER, 0:ER])
            pe.wait_ge(const_loaded, 9 * DMA)
            ins = t.transpose(PS[:, 2, 2 * P:2 * P + NEXP * FC], b1rows, ident[0:NEXP * FC, 0:NEXP * FC])
            ins.then_inc(edge_T, 1)
            pe.wait_ge(edge_out, 7)
            pe.sem_inc(quads_done, QR)
            pe.sem_inc(sout_ready, 1)

            def tile_sums(bank, s, u, h, first, last):
                p = p_agg[bank]
                for k in range(KC):
                    for a in range(2):
                        t.matmul(p[:, k, :], msg[:, s, u, a, k * P:(k + 1) * P], oh[:, h, u, :],
                                 start=(first and a == 0), stop=(last and a == 1))
                return t.matmul(p[:, KC, :], ones16[:, :], oh[:, h, u, :], start=first, stop=last)

            pe.wait_ge(flag_ready, 1)
            flag = pe.value_load(irregular[0:1, 0:1], min_val=0, max_val=1)
            with pe.If(flag == 1):
                with pe.Fori(0, NWIN) as w:
                    with pe.Fori(0, ER) as r:
                        pe.wait_ge(fb_oh, 2 * (ER * w + r + 1))
                        pe.wait_ge(fb_done, ER * w + r + 1)
                        for j in range(TPR):
                            pe.wait_ge(fb_gathered[j], DMA * (ER * w + r + 1))
                            ins = tile_sums(0, j // QT, j % QT, j // QT, j == 0, j == TPR - 1)
                        ins.then_inc(fb_sums, 1)

            for lo, hi, own, experts in SPANS:
                with pe.Fori(lo, hi) as i:
                    for s in range(QR):
                        if s % 2 == 0:
                            pe.wait_ge(adds_done, 2 * i + s // 2 + 1)
                        pe.wait_ge(oh_ready, QR * i + s + 1)
                        pe.wait_ge(gathered[s], QT * DMA * (i + 1))
                        for u in range(QT):
                            ins = tile_sums(s // 2, s, u, s % 2, s % 2 == 0 and u == 0, s % 2 == 1 and u == QT - 1)
                        ins.then_inc(quads_done, 1)
                        if own and s == 1:
                            pe.wait_ge(hx_loaded, 2 * DMA * (i + 1))
                            for a in range(2):
                                for k in range(KC):
                                    ins = t.transpose(p_hT[:, a, k, 0:BT], hx_h[0:BT, a, k * P:(k + 1) * P], ident16[0:BT, 0:BT])
                            ins.then_inc(hT_made, 1)
                        if own and s == 2:
                            pe.wait_ge(hT_copied, i + 1)
                            pe.wait_ge(sout_ready, i + 1)
                            t.matmul(p_s, bias_one[:, :], brow[:, :], start=True, stop=False)
                            for n, (ha, wa, k) in enumerate([(ha, wa, k) for ha, wa in ((0, 0), (1, 0), (0, 1)) for k in range(KC)]):
                                ins = t.matmul(p_s, hT[:, ha, k, 0:BT], ws[:, wa, k, :], start=False, stop=(n == 3 * KC - 1))
                            ins.then_inc(self_done, 1)

            with pe.Fori(0, NG) as q:
                pe.wait_ge(agg_norm, q + 1)
                for b in range(GB):
                    for k in range(KC):
                        ins = t.matmul(p_n[:, b, :], hn[:, k, b * BT:(b + 1) * BT], wn[:, k, :], start=(k == 0), stop=(k == KC - 1))
                ins.then_inc(neigh_done, 1)
                pe.wait_ge(xt_made, q + 1)
                for b in range(GB):
                    for k in range(KC):
                        ins = t.transpose(p_xT[:, b * KC + k, 0:BT], XX[0:BT, b, 1, k * P:(k + 1) * P], ident[0:BT, 0:BT])
                ins.then_inc(xtT_made, 1)
                pe.wait_ge(xtT_copied, q + 1)
                for b in range(GB):
                    for k in range(KC):
                        t.matmul(p_lg[:, b, :], xtT[:, b, k, 0:BT], gw[:, k, :], start=(k == 0), stop=False)
                    ins = t.matmul(p_lg[:, b, :], ones_row, gbrow[:, :], start=False, stop=True)
                ins.then_inc(logits, 1)
                pe.wait_ge(ohs_made, q + 1)
                for b in range(GB):
                    t.matmul(p_pos[:, b, :], lower[:, :], ohs[0:BT, b, :], start=True, stop=False)
                    for c in range(b):
                        t.matmul(p_pos[:, b, :], ones[0:BT, 0:BT], ohs[0:BT, c, :], start=False, stop=False)
                    ins = t.matmul(p_pos[:, b, :], ones[0:BT, 0:BT], acc[:, :], start=False, stop=True)
                ins.then_inc(pos_made, 1)
                pe.wait_ge(gates_made, q + 1)
                for b in range(GB):
                    ins = t.transpose(p_gT[:, b, 0:BT], gates[0:BT, b, :], ident[0:BT, 0:BT])
                ins.then_inc(gT_made, 1)
                pe.wait_ge(gT_copied, q + 1)
                for b in range(GB):
                    ins = t.matmul(p_n[:, b, :], GT_sb[0:NEXP, b, 0:BT], b2s[:, :], start=True, stop=True)
                ins.then_inc(b2_made, 1)

            pe.wait_ge(xx_ready, NG)
            t.matmul(p_cnt, ones[0:BT, :], acc[:, :], start=True, stop=True).then_inc(counted, 1)
            pe.wait_ge(item_cols, 1)
            for c in range(2):
                ins = t.transpose(p_item[:, c, 0:NITEM], scr[0:NITEM, c:c + 1], ident[0:NITEM, 0:NITEM])
            ins.then_inc(item_T, 1)

            def turn(s, m):
                n = 4 * m + s
                pe.wait_ge(xs_in[s], DMA * (m + 1))
                pe.wait_ge(x16_copied, n + 3)
                v = xsr[:, s, 0:D].bitcast(f16).rearrange("p (a k h) -> p a k h", a=2, k=KC)
                for h in range(2):
                    for k in range(KC):
                        ins = t.transpose(p_x16[s % 2][:, h, k, :], v[:, h, k, :], ident16[:, :])
                ins.then_inc(x16_made, 1)

            def up(s, m):
                n = 4 * m + s
                pe.wait_ge(w1_copied, n + 1)
                pe.wait_ge(x16_copied, n + 5)
                pe.wait_ge(relu_done, n + 1)
                for c in range(FC):
                    terms = [(wa, xa, k) for wa, xa in ((0, 0), (0, 1), (1, 0)) for k in range(KC)]
                    for y, (wa, xa, k) in enumerate(terms):
                        ins = t.matmul(p_h[s % 2][:, c * P:(c + 1) * P], w1e[:, s % 2, wa, k, c * P:(c + 1) * P],
                                       xT[:, s % 2, xa, k, :], start=(y == 0), stop=(y == len(terms) - 1))
                ins.then_inc(l1_done, 1)

            def down(s, m):
                n = 4 * m + s
                pe.wait_ge(w2_copied, n + 1)
                pe.wait_ge(h_split, n + 3)
                pe.wait_ge(yo_ready, n + 1)
                terms = [(h, wa, c) for h, wa in ((hh, 0), (hh, 1), (hl, 0)) for c in range(FC)]
                for y, (h, wa, c) in enumerate(terms):
                    ins = t.matmul(p_y[s % 2], h[:, s % 2, c * P:(c + 1) * P], w2e[:, s % 2, wa, c, :],
                                   start=(y == 0), stop=(y == len(terms) - 1))
                ins.then_inc(l2_done, 1)

            pe.wait_ge(items_ready, 1)
            pe.sem_inc(l1_done, 2)
            pe.sem_inc(l2_done, 2)
            turn(0, 0)
            turn(1, 0)
            up(0, 0)
            with pe.Fori(0, NITEM // 4 - 1) as m:
                for s in range(4):
                    turn((s + 2) % 4, m + (s + 2) // 4)
                    up((s + 1) % 4, m + (s + 1) // 4)
                    down(s, m)
            last = NITEM // 4 - 1
            for s in range(4):
                if s < 2:
                    turn(s + 2, last)
                if s < 3:
                    up(s + 1, last)
                down(s, last)

            pe.wait_ge(yo_ready, NITEM + 2)
            for q in range(NG):
                s = q % 2
                pe.wait_ge(zx_loaded[s], 2 * DMA * (q // 2 + 1))
                if q >= 2:
                    pe.wait_ge(normed, q - 1)
                for b in range(GB):
                    t.matmul(p_sum[s][:, b, :], ident[0:BT, 0:BT], XX3[s][0:BT, b, 1, :], start=True, stop=False)
                    t.matmul(p_sum[s][:, b, :], ident[0:BT, 0:BT], Z[s][0:BT, b, 0, :], start=False, stop=False)
                    ins = t.matmul(p_sum[s][:, b, :], ident[0:BT, 0:BT], Z[s][0:BT, b, 1, :], start=False, stop=True)
                ins.then_inc(summed, 1)

        @block.vector
        def _(dve):
            v = nc.vector

            v.memset(srow, 0).then_inc(edge_pads, 1)
            v.memset(drow, int(FAR)).then_inc(edge_pads, 1)
            v.memset(drow2, 0).then_inc(edge_pads, 1)
            link, n0 = counted_link(dve, dve_step, 0)
            for c in range(NG):
                dve.wait_ge(x_loaded[c], DMA)
                bs = range(c * GB, (c + 1) * GB)
                for b in bs:
                    ins = v.bn_stats(stats0[:, b, :], X[:, b, :])
                link(ins)
                for b in bs:
                    ins = v.bn_aggr(mv0[:, b, :], stats0[:, b, :])
            link(ins)
            rsqrt(v, link, mv0[:, :, 1], tmp0, rstd0)
            for c in range(NG):
                for b in range(c * GB, (c + 1) * GB):
                    ins = v.tensor_scalar(H[:, b, :], X[:, b, :], mv0[:, b, 0:1], rstd0[:, b:b + 1], ALU.subtract, ALU.mult)
                ins.then_inc(h_made, 1)
            dve.wait_ge(edges_loaded, 6 * DMA)
            v.tensor_copy(srowf, srow)
            v.tensor_copy(drowf, drow)
            link(v.tensor_copy(drowf2, drow2))
            link(v.tensor_reduce(bmin, drowf, AX.X, ALU.min))
            link(v.tensor_reduce(bmax, drowf2, AX.X, ALU.max))
            v.tensor_scalar(drowf, drowf, bmin, None, ALU.subtract).then_inc(rows_ready, 1)
            link(v.tensor_scalar(bmax, bmax, bmin, None, ALU.subtract))
            link(v.tensor_scalar(bad, bmax, float(P) - 0.5, None, ALU.is_gt))
            dve.sem_inc(rows_ready, 1)
            v.memset(relT[:, ET:ETP], FAR)
            dve.wait_ge(const_loaded, 9 * DMA)
            link(v.tensor_scalar(ws[:, 0, :, :], wsf, WSS, None, ALU.mult))
            v.scalar_tensor_tensor(ws[:, 1, :, :], wsf, WSS, ws[:, 0, :, :], ALU.mult, ALU.subtract).then_inc(edge_out, 1)
            dve.wait_ge(edge_T, 1)
            v.tensor_copy(srcT[:, 0:ET].rearrange("p (r j) -> p j r", j=TPR), PS[:, 0:TPR, 0:ER]).then_inc(edge_out, 1)
            v.tensor_copy(relT[:, 0:ET].rearrange("p (r j) -> p j r", j=TPR), PS[:, 0:TPR, P:P + ER]).then_inc(edge_out, 1)
            v.tensor_copy(base_row[0:1, :], PS[0:1, 0, 2 * P:2 * P + ER]).then_inc(edge_out, 1)
            link(v.tensor_reduce(badf, PS[0:1, 1, 2 * P:2 * P + ER], AX.X, ALU.max))
            v.tensor_copy(irregular[:, :], badf).then_inc(flag_ready, 1)
            v.tensor_copy(b1T[:, :], PS[:, 2, 2 * P:2 * P + NEXP * FC]).then_inc(edge_out, 1)
            v.memset(AGG[:, :, :], 0.0).then_inc(edge_out, 2)
            dve.wait_ge(edge_out, 7)
            dve.wait_ge(flag_ready, 1)

            def onehots(r, h, signal):
                v.tensor_tensor(oh[:, h, :, :], iota16[:, :].unsqueeze(1).to_broadcast([P, QT, P]),
                                relT[:, bass.ds(TPR * r + QT * h, QT)].unsqueeze(2).to_broadcast([P, QT, P]),
                                ALU.is_equal).then_inc(signal, 1)

            dve.wait_ge(consts_made, 14)
            flag = dve.value_load(irregular[0:1, 0:1], min_val=0, max_val=1)
            with dve.If(flag == 1):
                dve.sem_inc(fb_done, 1)
                dve.sem_inc(fb_moved, 1)
                with dve.Fori(0, NWIN) as w:
                    with dve.Fori(0, ER) as r:
                        dve.wait_ge(fb_moved, 2 * w + 1)
                        base = dve.value_load(base_row[0:1, bass.ds(r, 1)], min_val=0, max_val=N)
                        dve.wait_ge(fb_done, ER * w + r + 1)
                        carry(dve)
                        onehots(r, 0, fb_oh)
                        onehots(r, 1, fb_oh)
                        dve.wait_ge(fb_sums, ER * w + r + 1)
                        win = AGG[:, :, bass.ds(base, P)]
                        v.tensor_tensor(win, win, p_agg[0], ALU.add).then_inc(fb_done, 1)
                    dve.wait_ge(fb_done, ER * w + ER + 1)
                    v.tensor_scalar(relT[:, 0:ET], relT[:, 0:ET], -float(P), None, ALU.add).then_inc(fb_moved, 1)
                    v.tensor_scalar(base_row[0:1, :], base_row[0:1, :], float(P), float(N), ALU.add, ALU.min).then_inc(fb_moved, 1)
                dve.wait_ge(fb_moved, 2 * NWIN + 1)
                v.memset(relT[:, 0:ET], FAR).then_inc(fb_moved, 1)
                dve.wait_ge(fb_moved, 2 * NWIN + 2)

            def quad_onehots(r, h, ahead):
                if ahead is not None:
                    dve.wait_ge(quads_done, ahead + 1 + QR)
                onehots(r, h, oh_ready)

            def add(i, g):
                r = 2 * i + g
                base = dve.value_load(base_row[0:1, bass.ds(r, 1)], min_val=0, max_val=N)
                dve.wait_ge(quads_done, 2 * r + 2 + QR)
                dve.wait_ge(adds_done, r + 2)
                win = AGG[:, :, bass.ds(base, P)]
                v.tensor_tensor(win, win, p_agg[g], ALU.add).then_inc(adds_done, 1)

            dve.sem_inc(adds_done, 2)
            dve.sem_inc(rows_free, 1)
            quad_onehots(0, 0, None)
            quad_onehots(0, 1, None)
            for lo, hi, own, experts in SPANS:
                with dve.Fori(lo, hi) as i:
                    quad_onehots(2 * i + 1, 0, QR * i)
                    quad_onehots(2 * i + 1, 1, QR * i + 1)
                    add(i, 0)
                    if experts:
                        dve.wait_ge(w_hi, 2 * i + 1)
                        w = W1[:, bass.ds(i, 1), :, :, :].rearrange("p e a k f -> p (e a) (k f)")
                        v.scalar_tensor_tensor(w[:, 1, :], wstg, WS1, w[:, 0, :], ALU.mult, ALU.subtract).then_inc(w_lo, 1)
                    quad_onehots(2 * i + 2, 0, QR * i + 2)
                    if own:
                        dve.wait_ge(self_done, i + 1)
                        v.scalar_tensor_tensor(hx_x[0:BT, :], p_s, 1.0 / WSS, hx_x[0:BT, :], ALU.mult, ALU.add).then_inc(sout_ready, 1)
                    quad_onehots(2 * i + 2, 1, QR * i + 3)
                    add(i, 1)
                    if experts:
                        dve.wait_ge(w_hi, 2 * i + 2)
                        w = W2[:, bass.ds(i, 1), :, :, :].rearrange("p e a c d -> p (e a) (c d)")
                        v.scalar_tensor_tensor(w[:, 1, :], wstg, WS2, w[:, 0, :], ALU.mult, ALU.subtract).then_inc(w_lo, 1)

            dve.wait_ge(adds_done, ER + 2)
            dve.wait_ge(quads_done, 2 * ER + QR)
            base_steps = n0[0]
            PER = 28
            with dve.Fori(0, NG) as q:
                link, n1 = counted_link(dve, dve_step, base_steps + PER * q)
                bs = range(GB)
                deg = AGG[:, KC, bass.ds(q * GT, GT)]
                link(v.tensor_scalar_max(deg, deg, 1.0), alone=True)
                link(v.reciprocal(deg, deg))
                v.tensor_tensor(hn, AGG[:, 0:KC, bass.ds(q * GT, GT)],
                                AGG[:, KC:KC + 1, bass.ds(q * GT, GT)].to_broadcast([P, KC, GT]), ALU.mult).then_inc(agg_norm, 1)
                dve.wait_ge(neigh_done, q + 1)
                dve.wait_ge(s_back, DMA * (q + 1))
                x1 = XX[0:BT, :, 0, :]
                xt = XX[0:BT, :, 1, :]
                link(v.tensor_tensor(x1, p_n[:, 0:GB, :], x1, ALU.add))
                for b in bs:
                    ins = v.bn_stats(stats[0:BT, b, :], x1[:, b, :])
                link(ins, alone=True)
                for b in bs:
                    ins = v.bn_aggr(mv[0:BT, b, :], stats[0:BT, b, :])
                link(ins)
                rsqrt(v, link, mv[0:BT, :, 1], tmp, rstd[0:BT, :])
                for b in bs:
                    ins = v.tensor_scalar(xt[:, b, :], x1[:, b, :], mv[0:BT, b, 0:1], rstd[0:BT, b:b + 1], ALU.subtract, ALU.mult)
                ins.then_inc(xt_made, 1)
                dve.wait_ge(xt_made, q + 1)
                v.tensor_tensor(x1, x1, beta_b[:, :].unsqueeze(1).to_broadcast([BT, GB, D]), ALU.add)
                dve.wait_ge(hi_made, q + 1)
                v.tensor_tensor(pay_h[0:BT, :, 0, D:2 * D], xt, pay_h[0:BT, :, 0, 0:D], ALU.subtract).then_inc(lo_made, 1)
                dve.wait_ge(logits, q + 1)
                carry(dve)
                for b in bs:
                    ins = v.max(m8[0:BT, b, :], p_lg[:, b, :])
                link(ins, alone=True)
                for b in bs:
                    v.max_index(i8[0:BT, b, :], m8[0:BT, b, :], p_lg[:, b, :])
                v.tensor_tensor(dl[0:BT, :], m8[0:BT, :, 1], m8[0:BT, :, 0], ALU.subtract).then_inc(delta, 1)
                dve.wait_ge(delta, q + 1)
                link(v.tensor_copy(idxf[0:BT, :, :], i8[0:BT, :, 0:2]))
                io = iota[0:BT, 0:NEXP].unsqueeze(1)
                for k in range(2):
                    ins = v.tensor_tensor(oh2[0:BT, :, k, :], io.to_broadcast([BT, GB, NEXP]),
                                          idxf[0:BT, :, k].unsqueeze(2).to_broadcast([BT, GB, NEXP]), ALU.is_equal)
                link(ins)
                v.tensor_tensor(ohs[0:BT, :, :], oh2[0:BT, :, 0, :], oh2[0:BT, :, 1, :], ALU.add).then_inc(ohs_made, 1)
                dve.wait_ge(expd, q + 1)
                link(v.tensor_scalar_add(dl[0:BT, :], e1[0:BT, :], 1.0))
                link(v.reciprocal(wt[0:BT, :, 0], dl[0:BT, :]))
                link(v.tensor_tensor(wt[0:BT, :, 1], e1[0:BT, :], wt[0:BT, :, 0], ALU.mult))
                dve.wait_ge(pos_made, q + 1)
                v.tensor_tensor(posb[0:BT, :, :], p_pos, ebase[:, :].unsqueeze(1).to_broadcast([BT, GB, NEXP]), ALU.add)
                for k in range(2):
                    ins = v.tensor_tensor(gates4[:, :, k, :], oh2[0:BT, :, k, :],
                                          wt[0:BT, :, k].unsqueeze(2).to_broadcast([BT, GB, NEXP]), ALU.mult)
                link(ins)
                v.tensor_tensor(gates[0:BT, :, :], gates4[:, :, 0, :], gates4[:, :, 1, :], ALU.add).then_inc(gates_made, 1)
                for k in range(2):
                    ins = v.tensor_tensor(prod[0:BT, :, k, :], oh2[0:BT, :, k, :], posb[0:BT, :, :], ALU.mult)
                link(ins)
                link(v.tensor_reduce(slotf[0:BT, :, :], prod[0:BT, :, :, :], AX.X, ALU.add))
                dve.wait_ge(rows_free, q + 1)
                v.tensor_copy(sloti[0:BT, :, :], slotf[0:BT, :, :])
                v.tensor_copy(pay_i[0:BT, :, :, D], tok2[:, :, :])
                v.tensor_scalar(pay[0:BT, :, :, D + 1], wt[0:BT, :, :], 1.0 / WS2, None, ALU.mult).then_inc(meta_made, 1)
                dve.wait_ge(meta_made, q + 1)
                v.tensor_scalar_add(tok2[:, :, :], tok2[:, :, :], float(2 * GT))
                link(v.tensor_reduce(gsum[0:BT, :], ohs[0:BT, :, :].rearrange("p b e -> p e b"), AX.X, ALU.add))
                link(v.tensor_tensor(acc[:, :], acc[:, :], gsum[0:BT, :], ALU.add))
                dve.wait_ge(b2_made, q + 1)
                dve.wait_ge(hi_made, q + 1)
                v.tensor_tensor(xt, p_n[:, 0:GB, :], xt, ALU.add).then_inc(xx_ready, 1)
                per = n1[0]
            assert per == PER, per

            base2 = base_steps + PER * NG
            link, n2 = counted_link(dve, dve_step, base2)
            link(v.tensor_scalar(thr, iota[:, 0:NTHR], float(P), None, ALU.mult))
            v.memset(padt, 0.0)
            dve.wait_ge(counted, 1)
            link(v.tensor_copy(cnt, p_cnt))
            v.memset(padt.bitcast(i32)[:, D:D + 1], SKIP)
            link(v.tensor_tensor(cmp1, cnt.unsqueeze(2).to_broadcast([P, NEXP, NTHR]),
                                 thr.unsqueeze(1).to_broadcast([P, NEXP, NTHR]), ALU.is_gt))
            link(v.tensor_reduce(ntile, cmp1, AX.X, ALU.add))
            link(v.tensor_tensor_scan(pincl, ones[:, 0:NEXP], ntile, 0.0, ALU.mult, ALU.add))
            link(v.tensor_scalar(cmp2, pincl, iotap[:, :], None, ALU.is_le))
            v.tensor_reduce(scr[:, 2:3], cmp2, AX.X, ALU.add)
            link(v.tensor_tensor(cmp2, cmp2, pincl, ALU.mult))
            link(v.tensor_reduce(scr[:, 3:4], cmp2, AX.X, ALU.max))
            link(v.tensor_tensor(scr[:, 4:5], iotap[:, :], scr[:, 3:4], ALU.subtract))
            link(v.tensor_scalar(scr[:, 5:6], scr[:, 2:3], float(REG), -float(DUMMY), ALU.mult, ALU.add))
            link(v.scalar_tensor_tensor(scr[:, 6:7], scr[:, 4:5], float(P), scr[:, 5:6], ALU.mult, ALU.add))
            link(v.tensor_scalar(scr[:, 7:8], scr[:, 2:3], float(NEXP) - 0.5, None, ALU.is_lt))
            link(v.tensor_tensor(scr[:, 8:9], scr[:, 6:7], scr[:, 7:8], ALU.mult))
            link(v.tensor_scalar_add(scr[:, 1:2], scr[:, 8:9], float(DUMMY)))
            v.tensor_scalar_min(scr[:, 0:1], scr[:, 2:3], float(NEXP - 1)).then_inc(item_cols, 1)
            v.tensor_tensor(padrow[:, :], cnt[0:1, :], ebase[0:1, :], ALU.add)
            dve.wait_ge(item_T, 1)
            v.tensor_copy(items[:, :, :], p_item[:, :, 0:NITEM]).then_inc(items_ready, 1)
            dve.wait_ge(items_ready, 1)

            def load_w1(s, m):
                n = 4 * m + s
                e = dve.value_load(items[0:1, 0, bass.ds(n, 1)], min_val=0, max_val=NEXP - 1)
                dve.wait_ge(l1_done, n + 1)
                dve.wait_ge(relu_done, n + 1)
                v.tensor_copy(b1e[:, s % 2, :], b1T[:, bass.ds(e * FC, FC)])
                v.tensor_copy(w1e[:, s % 2, :, :, :].rearrange("p a k f -> p (a k f)"),
                              W1[:, bass.ds(e, 1), :, :, :].rearrange("p e a k f -> p (e a k f)")).then_inc(w1_copied, 1)
                return e

            def load_w2(s, m, e):
                n = 4 * m + s
                dve.wait_ge(l2_done, n + 1)
                v.tensor_copy(w2e[:, s % 2, :, :, :].rearrange("p a c d -> p (a c d)"),
                              W2[:, bass.ds(e, 1), :, :, :].rearrange("p e a c d -> p (e a c d)")).then_inc(w2_copied, 1)

            def take(s, m):
                dve.wait_ge(xs_in[s], DMA * (m + 1))
                if not (isinstance(m, int) and m == 0):
                    dve.wait_ge(yo_out[s], DMA * m)
                v.tensor_copy(meta[:, s, :], xsr[:, s, D:D + 2]).then_inc(meta_taken, 1)

            def split(s, m):
                n = 4 * m + s
                dve.wait_ge(relu_done, n + 3)
                dve.wait_ge(l2_done, n + 1)
                v.tensor_copy(hh[:, s % 2, :], hr[:, s % 2, :]).then_inc(hi_split, 1)
                dve.wait_ge(hi_split, n + 1)
                v.tensor_tensor(hl[:, s % 2, :], hr[:, s % 2, :], hh[:, s % 2, :], ALU.subtract).then_inc(h_split, 1)

            dve.wait_ge(xx_stored, (NG + 1) * DMA)
            dve.wait_ge(scattered, NB * 2 * DMA)
            dve.sem_inc(meta_taken, 4)
            dve.sem_inc(h_split, 2)
            e = load_w1(0, 0)
            load_w2(0, 0, e)
            take(0, 0)

            def dve_items(m):
                for s in range(4):
                    nxt = ((s + 1) % 4, m + (s + 1) // 4)
                    e = load_w1(*nxt)
                    take(*nxt)
                    split(s, m)
                    load_w2(*nxt, e)

            dve_items(0)
            with dve.Fori(1, NITEM // 4 - 1) as m:
                dve_items(m)
            last = NITEM // 4 - 1
            for s in range(4):
                if s < 3:
                    e = load_w1(s + 1, last)
                    take(s + 1, last)
                split(s, last)
                if s < 3:
                    load_w2(s + 1, last, e)

            link, _ = counted_link(dve, dve_step, base2 + n2[0])
            for q in range(NG + 1):
                if q < NG:
                    s = q % 2
                    dve.wait_ge(summed, q + 1)
                    for b in range(GB):
                        ins = v.bn_stats(stats3[0:BT, b, :], p_sum[s][:, b, :])
                    link(ins)
                    for b in range(GB):
                        ins = v.bn_aggr(mv3[s][:, b, :], stats3[0:BT, b, :])
                    link(ins)
                    rsqrt(v, link, mv3[s][:, :, 1], tmp3, rstd3[s])
                    v.scalar_tensor_tensor(nmr3[s], mv3[s][:, :, 0], -1.0, rstd3[s], ALU.mult, ALU.mult).then_inc(stats_made, 1)
                if q >= 1:
                    s = 1 - q % 2
                    y = Y[s][0:BT, :, :]
                    dve.wait_ge(normed, q)
                    link(v.tensor_tensor(y, y, gamma_b[:, :].unsqueeze(1).to_broadcast([BT, GB, D]), ALU.mult))
                    v.tensor_tensor(y, y, XX3[s][0:BT, :, 0, :], ALU.add).then_inc(out_ready, 1)


_INS = ["x", "src", "dst", "L0_gnn_W_self", "L0_gnn_W_neigh", "L0_gnn_b", "L0_ffn_gate_w", "L0_ffn_gate_b",
        "L0_ffn_w1", "L0_ffn_b1", "L0_ffn_w2", "L0_ffn_b2", "L0_ffn_gamma", "L0_ffn_beta"]


def kernel(**inputs):
    import numpy as np
    import concourse.bacc as bacc
    from concourse import mybir as mb
    from concourse.bass_utils import run_bass_kernel_spmd

    nc = bacc.Bacc("TRN2", target_bir_lowering=False, num_devices=1)
    arrays, args = {}, []
    for name in _INS:
        a = np.ascontiguousarray(inputs[name])
        arrays[f"in_{name}"] = a
        args.append(nc.dram_tensor(f"in_{name}", a.shape, mb.dt.from_np(a.dtype), kind="ExternalInput").ap())
    args.append(nc.dram_tensor("out_0", (N, D), mb.dt.float32, kind="ExternalOutput").ap())
    build(nc, *args)
    r = run_bass_kernel_spmd(nc, [arrays], core_ids=[0])
    return r.results[0]["out_0"]
```

```python
import concourse.bass as bass
from concourse import mybir
from contextlib import ExitStack

N = 3125
D = 256
E = 53125
NEXP = 16
F = 512
EPS = 1e-5

P = 128
KC = D // P
FC = F // P
BT = 125
NB = N // BT
GB = 5
NG = NB // GB
GT = GB * BT

ET = -(-E // P)
TPR = 8
ER = ET // TPR
ETP = ET + 8
QT = 4
QR = 4
RING = QT * QR
NIT = ET // RING
LAG = 2
AGGW = N + P + 9
FAR = 1.0e6
NWIN = -(-N // P)

WSS = 16.0
WS1 = 16.0
WS2 = 64.0
REG = 26 * P
DUMMY = NEXP * REG
ROW = D + 2
NITEM = NEXP + (2 * N - NEXP) // P
SKIP = 1 << 20
ARENA = 7680
NTHR = -(-N // P)


def build(nc, x, src, dst, w_self, w_neigh, gnn_b, gate_w, gate_b, w1, b1, w2, b2, gamma, beta, out):
    f32, f16, i32, u32 = mybir.dt.float32, mybir.dt.float16, mybir.dt.int32, mybir.dt.uint32
    ALU = mybir.AluOpType
    ACT = mybir.ActivationFunctionType
    AX = mybir.AxisListType

    ctx = ExitStack()
    with ctx:
        def sb(name, shape, dt=f32):
            return ctx.enter_context(nc.sbuf_tensor(name, shape, dt))

        def sem(name):
            return ctx.enter_context(nc.semaphore(name))

        def dram(name, shape, dt=f32):
            return nc.dram_tensor(name, shape, dt, kind="Internal").ap()

        h_tab = dram("h_tab", [N, 2 * D], f16)
        xh_tab = dram("xh_tab", [N, 2 * D], f16)
        xx_tab = dram("xx_tab", [N, 2 * D])
        xs = dram("xs", [DUMMY + P, ROW])
        z_tab = dram("z_tab", [2 * N, D])

        W1 = sb("W1", [P, NEXP, 2, KC, F], f16)
        W2 = sb("W2", [P, NEXP, 2, FC, D], f16)
        AGG = sb("AGG", [P, KC + 1, AGGW])
        ident = sb("ident", [P, P])
        ident16 = sb("ident16", [P, P], f16)
        iota = sb("iota", [P, P])
        iotap = sb("iotap", [P, 1])
        iota16 = sb("iota16", [P, P], f16)
        ones16 = sb("ones16", [P, P], f16)
        bias_one = sb("bias_one", [1, BT])
        lower = sb("lower", [BT, BT])
        lower16 = sb("lower16", [BT, BT], f16)
        ws = sb("ws", [P, 2, KC, D], f16)
        wn = sb("wn", [P, KC, D])
        gw = sb("gw", [P, KC, NEXP])
        brow = sb("brow", [1, D])
        gb_b = sb("gb_b", [BT, NEXP])
        beta_b = sb("beta_b", [BT, D])
        b1T = sb("b1T", [P, NEXP * FC])
        need = sb("need", [1, ER + 1])
        lg = sb("lg", [BT, NEXP])
        m8 = sb("m8", [BT, 8])
        i8 = sb("i8", [BT, 8], u32)
        val = sb("val", [BT, NB, 2])
        idxf = sb("idxf", [BT, NB, 2])
        items = sb("items", [1, 2, NITEM], i32)
        irregular = sb("irregular", [1, 1], i32)
        padrow = sb("padrow", [1, NEXP], i32)
        arena = sb("arena", [P, ARENA])

        at = [0]

        def part(words):
            a = at[0]
            at[0] += words
            assert at[0] <= ARENA, at[0]
            return arena[:, a:a + words]

        pro = W2[:, :, :, :, :].rearrange("p e s c f -> p (e s c f)").bitcast(f32)
        X = pro[0:BT, 0:NB * D].rearrange("p (b d) -> p b d", d=D)
        H = pro[0:BT, NB * D:2 * NB * D].rearrange("p (b d) -> p b d", d=D)
        pr1 = W1[:, :, :, :, :].rearrange("p e s c f -> p (e s c f)").bitcast(f32)
        H16 = pr1[0:BT, 0:NB * D].bitcast(f16).rearrange("p (b a d) -> p b a d", a=2, d=D)
        o = NB * D
        L = TPR * P
        srow = pr1[0:ER, o:o + L].bitcast(i32)
        drow = pr1[0:ER, o + L:o + 2 * L].bitcast(i32)
        drow2 = pr1[0:ER, o + 2 * L:o + 3 * L].bitcast(i32)
        srowf = pr1[0:ER, o + 3 * L:o + 4 * L]
        drowf = pr1[0:ER, o + 4 * L:o + 5 * L]
        drowf2 = pr1[0:ER, o + 5 * L:o + 6 * L]
        o += 6 * L
        wsf = pr1[:, o:o + KC * D].rearrange("p (k d) -> p k d", d=D)
        b1rows = pr1[0:NEXP * FC, o + KC * D:o + KC * D + P]
        o += KC * D + P
        stats0 = pr1[0:BT, o:o + NB * 6].rearrange("p (b s) -> p b s", s=6)
        mv0 = pr1[0:BT, o + 200:o + 200 + NB * 2].rearrange("p (b s) -> p b s", s=2)
        rstd0 = pr1[0:BT, o + 260:o + 260 + NB]
        tmp0 = [pr1[0:BT, a:a + NB] for a in (o + 290, o + 320)]
        bmin = pr1[0:ER, o + 350:o + 351]
        bmax = pr1[0:ER, o + 351:o + 352]
        bad = pr1[0:ER, o + 352:o + 353]
        badf = pr1[0:1, o + 353:o + 354]
        lateness = pr1[0:1, o + 354:o + 355]
        late_row = pr1[0:1, o + 360:o + 360 + ER]
        wnf = pr1[:, o + 420:o + 420 + KC * D].rearrange("p (k d) -> p k d", d=D)
        assert o + 420 + KC * D <= NEXP * 2 * KC * F // 2

        msg = part(RING * D).bitcast(f16).rearrange("p (q u a d) -> p q u a d", u=QT, a=2, d=D)
        oh = part(2 * QT * P // 2).bitcast(f16).rearrange("p (h u c) -> p h u c", u=QT, c=P)
        wstg1 = W1[:, NEXP - 1, :, :, :].rearrange("p s c f -> p (s c f)").bitcast(f32)
        wstg2 = W2[:, NEXP - 1, :, :, :].rearrange("p s c f -> p (s c f)").bitcast(f32)
        srcT = part(ET)
        relT = part(ETP)
        base_row = part(ER).bitcast(i32)
        stage = part(RING).bitcast(i32).rearrange("p (h u) -> p h u", u=QT)
        hx_h = part(D).bitcast(f16).rearrange("p (a d) -> p a d", d=D)
        hx_x = part(D)
        hT = part(2 * KC * BT // 2).bitcast(f16).rearrange("p (a k t) -> p a k t", a=2, k=KC)
        deg = part(BT)
        meanT = part(KC * BT).rearrange("p (k t) -> p k t", t=BT)
        xx = part(2 * D).rearrange("p (a d) -> p a d", d=D)
        xh = part(D).bitcast(f16).rearrange("p (a d) -> p a d", d=D)
        xtT = part(KC * BT).rearrange("p (k t) -> p k t", t=BT)
        stats = part(6)[0:BT, :]
        mv = part(2)[0:BT, :]
        rstd, *tmp = [stats[:, c:c + 1] for c in range(3)]
        at[0] = 0
        pay_w = part(NB * ROW)
        pay = pay_w.rearrange("p (b w) -> p b w", w=ROW)
        pay_i = pay_w.bitcast(i32).rearrange("p (b w) -> p b w", w=ROW)
        wstg3 = part(KC * F)
        agg_f = AGG[:, :, :].rearrange("p k c -> p (k c)")
        gT = agg_f[0:NEXP, 0:N].rearrange("p (b t) -> p b t", t=BT)
        AFTER_GT = N + 1
        ag = [AFTER_GT]

        def spare(words):
            a = ag[0]
            ag[0] += words
            assert ag[0] <= (KC + 1) * AGGW, ag[0]
            return agg_f[:, a:a + words]

        wt = spare(NB * 2)[0:BT, :].rearrange("p (b k) -> p b k", k=2)
        dl = spare(NB)[0:BT, :]
        e1 = spare(NB)[0:BT, :]
        oh2 = spare(NB * 2 * NEXP)[0:BT, :].rearrange("p (b k e) -> p b k e", k=2, e=NEXP)
        prod = spare(NB * 2 * NEXP)[0:BT, :].rearrange("p (b k e) -> p b k e", k=2, e=NEXP)
        gates = spare(NB * NEXP)[0:BT, :].rearrange("p (b e) -> p b e", e=NEXP)
        ohs, incl, excl, keep = [spare(NEXP * NB // 2)[0:BT, :].bitcast(f16) for _ in range(4)]
        posb = spare(NEXP * NB)[0:BT, :]
        tokf = spare(NB * 2)[0:BT, :].rearrange("p (b k) -> p b k", k=2)
        slotf = spare(NB * 2)[0:BT, :].rearrange("p (b k) -> p b k", k=2)
        sloti = spare(NB * 2)[0:BT, :].bitcast(i32).rearrange("p (b k) -> p b k", k=2)
        padt = spare(ROW)
        ebase = spare(NEXP)[0:BT, :]
        thr = spare(NTHR)
        cmp1 = spare(NEXP * NTHR).rearrange("p (e k) -> p e k", k=NTHR)
        cnt, ntile, pincl, cmp2, scr = [spare(NEXP) for _ in range(5)]
        at[0] = 0
        xsr = part(4 * ROW).rearrange("p (s w) -> p s w", w=ROW)
        xT = part(2 * 2 * KC * P // 2).bitcast(f16).rearrange("p (s a k t) -> p s a k t", s=2, a=2, k=KC)
        meta = part(4 * 2).rearrange("p (s w) -> p s w", w=2)
        b1e = part(2 * FC).rearrange("p (s c) -> p s c", c=FC)
        hr = part(2 * F).rearrange("p (s t) -> p s t", t=F)
        hh = part(2 * F // 2).bitcast(f16).rearrange("p (s t) -> p s t", t=F)
        hl = part(2 * F // 2).bitcast(f16).rearrange("p (s t) -> p s t", t=F)
        yo = part(4 * D).rearrange("p (s d) -> p s d", d=D)
        WPLACE = 2 * KC * F + 4 * FC * D
        agg_w = agg_f[:, AFTER_GT:AFTER_GT + WPLACE].bitcast(f16)
        w1e = agg_w[:, 0:4 * KC * F].rearrange("p (s a k f) -> p s a k f", s=2, a=2, k=KC)
        w2e = agg_w[:, 4 * KC * F:2 * WPLACE].rearrange("p (s a c d) -> p s a c d", s=4, a=2, c=FC)
        at[0] = 0
        part(4 * ROW + 4 * P + 2 * 4 + 2 * FC + 2 * F + 2 * F + 4 * D)
        XX3 = [part(GB * 2 * D)]
        a = AFTER_GT + WPLACE
        w1_f = W1[:, :, :, :, :].rearrange("p e s c f -> p (e s c f)").bitcast(f32)
        w2_f = W2[:, :, :, :, :].rearrange("p e s c f -> p (e s c f)").bitcast(f32)
        late = [f[:, s * GB * 2 * D:(s + 1) * GB * 2 * D] for f in (w1_f, w2_f) for s in range(6)]
        EARLY = len(XX3)
        XX3 += late[0:NG - EARLY]
        XX3 = [z.rearrange("p (b a d) -> p b a d", a=2, d=D) for z in XX3]
        late = late[NG - EARLY:]
        Z = [z.rearrange("p (b k d) -> p b k d", k=2, d=D) for z in late[0:NG]]
        late = late[NG:]
        Y = [late[c // 2][:, c % 2 * GB * D:(c % 2 + 1) * GB * D].rearrange("p (b d) -> p b d", d=D) for c in range(NG)]
        b2s = agg_f[0:NEXP, a:a + D]
        gamma_b = agg_f[0:BT, a + D:a + 2 * D]
        assert a + 2 * D <= (KC + 1) * AGGW
        at[0] = 0
        stats3 = part(GB * 6).rearrange("p (b s) -> p b s", s=6)
        mv3 = [part(GB * 2)[0:BT, :].rearrange("p (b s) -> p b s", s=2) for _ in range(2)]
        rstd3 = [part(GB)[0:BT, :] for _ in range(2)]
        nmr3 = [part(GB)[0:BT, :] for _ in range(2)]
        tmp3 = [part(GB)[0:BT, :] for _ in range(2)]

        PS = ctx.enter_context(nc.psum_tensor("PS", [P, 8, 512], f32))
        p_agg = [PS[:, b * (KC + 1):(b + 1) * (KC + 1), 0:P] for b in range(2)]
        p_hT = PS[:, 6, 0:KC * P].bitcast(f16).rearrange("p (a k t) -> p a k t", a=2, k=KC)
        p_xT = PS[:, 6, KC * P:2 * KC * P].rearrange("p (k t) -> p k t", t=P)
        p_x1 = PS[0:BT, 7, 0:D]
        p_lg = PS[0:BT, 7, D:D + NEXP]
        p_pos = PS[0:BT, 0, 0:NEXP * NB]
        p_gT = PS[0:NEXP, 1:8, :].rearrange("p n (h t) -> p (n h) t", t=P)
        p_cnt = PS[:, 0, NB * NEXP:(NB + 1) * NEXP]
        p_item = PS[0:1, 0, 0:2 * P].rearrange("p (a t) -> p a t", t=P)
        p_x16 = [PS[:, s, 0:256].bitcast(f16).rearrange("p (a k t) -> p a k t", a=2, k=KC) for s in range(2)]
        p_h = [PS[:, 2 + s, :] for s in range(2)]
        p_y = [PS[:, 4 + s, 0:D] for s in range(2)]
        p_sum = [PS[0:BT, 3 * s:3 * s + 3, :].rearrange("p n (h d) -> p (n h) d", d=D) for s in range(2)]

        const_loaded = sem("const_loaded")
        consts_made = sem("consts_made")
        edges_loaded = sem("edges_loaded")
        edge_pads = sem("edge_pads")
        x_loaded = [sem(f"x_loaded{c}") for c in range(NG)]
        h_made = sem("h_made")
        h_hi = sem("h_hi")
        h_lo = sem("h_lo")
        h_lo_dve = sem("h_lo_dve")
        flag_ready = sem("flag_ready")
        fb_staged = sem("fb_staged")
        fb_gathered = [sem(f"fb_gathered{u}") for u in range(TPR)]
        fb_oh = sem("fb_oh")
        fb_sums = sem("fb_sums")
        fb_done = sem("fb_done")
        fb_moved = sem("fb_moved")
        h_stored = sem("h_stored")
        dve_step = sem("dve_step")
        waits_passed = sem("waits_passed")
        rows_ready = sem("rows_ready")
        edge_T = sem("edge_T")
        edge_out = sem("edge_out")
        stage_ready = sem("stage_ready")
        gathered = [sem(f"gathered{u}") for u in range(QR)]
        oh_ready = sem("oh_ready")
        quads_done = sem("quads_done")
        adds_done = sem("adds_done")
        w1_loaded = sem("w1_loaded")
        w1_hi = sem("w1_hi")
        w1_lo = sem("w1_lo")
        w2_loaded = sem("w2_loaded")
        w2_hi = sem("w2_hi")
        w2_lo = sem("w2_lo")
        hxh_loaded = sem("hxh_loaded")
        hxx_loaded = sem("hxx_loaded")
        hT_made = sem("hT_made")
        hT_copied = sem("hT_copied")
        deg_step = sem("deg_step")
        mean_made = sem("mean_made")
        x1_summed = sem("x1_summed")
        x1_made = sem("x1_made")
        ln_step = sem("ln_step")
        xt_made = sem("xt_made")
        x1_ready = sem("x1_ready")
        xt_hi = sem("xt_hi")
        xt_lo = sem("xt_lo")
        xx_stored = sem("xx_stored")
        xh_stored = sem("xh_stored")
        xtT_made = sem("xtT_made")
        xtT_copied = sem("xtT_copied")
        logits = sem("logits")
        logits_out = sem("logits_out")
        top_step = sem("top_step")
        top_out = sem("top_out")
        tok_made = sem("tok_made")
        pay_loaded = sem("pay_loaded")
        meta_made = sem("meta_made")
        gates_made = sem("gates_made")
        gT_made = sem("gT_made")
        gT_copied = sem("gT_copied")
        scattered = [sem(f"scattered{h}") for h in range(2)]
        tail_loaded = sem("tail_loaded")
        delta = sem("delta")
        expd = sem("expd")
        ohs_made = sem("ohs_made")
        pos_made = sem("pos_made")
        counted = sem("counted")
        item_cols = sem("item_cols")
        item_T = sem("item_T")
        items_ready = sem("items_ready")
        padded = sem("padded")
        xs_in = [sem(f"xs_in{s}") for s in range(4)]
        x16_made = sem("x16_made")
        x16_copied = sem("x16_copied")
        meta_taken = sem("meta_taken")
        w1_copied = sem("w1_copied")
        w2_copied = sem("w2_copied")
        l1_done = sem("l1_done")
        relu_done = sem("relu_done")
        hi_split = sem("hi_split")
        h_split = sem("h_split")
        l2_done = sem("l2_done")
        yo_ready = sem("yo_ready")
        yo_out = [sem(f"yo_out{s}") for s in range(4)]
        zx_loaded = [sem(f"zx_loaded{q}") for q in range(NG)]
        z_added = sem("z_added")
        summed = sem("summed")
        stats_made = sem("stats_made")
        normed = sem("normed")
        out_ready = sem("out_ready")
        out_stored = sem("out_stored")

        out_b = out.rearrange("(c b p) d -> c p b d", p=BT, b=GB)
        POOL_LOW = 3
        HT = TPR // 2

        x_b = x.rearrange("(c b p) d -> c p b d", p=BT, b=GB)
        h_b = h_tab.rearrange("(c b p) d -> c p b d", p=BT, b=GB)
        DMA = 16

        def carry(engine):
            engine.sem_inc(waits_passed, 1)

        def counted_link(engine, signal, base):
            n = [0]

            def link(ins, alone=False):
                n[0] += 1
                ins.then_inc(signal, 1)
                engine.wait_ge(signal, base + n[0])
                if alone:
                    carry(engine)
            return link, n

        def rsqrt(v, link, var, tmp, y):
            link(v.tensor_scalar(tmp[0], var, EPS, None, ALU.add))
            link(v.tensor_scalar(tmp[1].bitcast(i32), tmp[0].bitcast(i32), 1, None, ALU.logical_shift_right))
            link(v.tensor_scalar(y.bitcast(i32), tmp[1].bitcast(i32), -1.0, float(0x5F3759DF), ALU.mult, ALU.add))
            for _ in range(3):
                link(v.scalar_tensor_tensor(tmp[1], y, -0.5, y, ALU.mult, ALU.mult))
                link(v.tensor_tensor(tmp[1], tmp[1], tmp[0], ALU.mult))
                link(v.scalar_tensor_tensor(y, tmp[1], 1.5, y, ALU.add, ALU.mult))

        def run_item(job, n, ahead, m):
            k = n + ahead
            if m is not None:
                job(k % 4, m + k // 4)
            elif 0 <= k < NITEM:
                job(k % 4, k // 4)

        block = ctx.enter_context(nc.Block())

        SPANS = [(0, LAG, "both", None), (LAG, LAG + 1, "both", "first"), (LAG + 1, NEXP - 1, "both", "block"),
                 (NEXP - 1, NEXP, "last w1", "block"), (NEXP, NIT - 1, None, "block"), (NIT - 1, NIT, None, "last")]
        LATE = [(0, 1, None, False, False), (1, LAG + 1, "both", False, False), (LAG + 1, LAG + 2, "both", True, False),
                (LAG + 2, NEXP, "both", True, True), (NEXP, NEXP + 1, "last w1", True, True), (NEXP + 1, NIT, None, True, True)]
        HALF_NB = NB // 2
        PARTS = [range(0, HALF_NB), range(HALF_NB, NB)]

        @block.sync
        def _(sp):
            full = ER - 1
            rest = E - full * L
            sp.wait_ge(edge_pads, 3)
            for t, a in ((srow, src), (drow, dst), (drow2, dst)):
                sp.dma_start(t[0:full, :], a[0:full * L].rearrange("(r c) -> r c", c=L)).then_inc(edges_loaded, DMA)
                sp.dma_start(t[full:ER, 0:rest], a[full * L:E].rearrange("(r c) -> r c", r=1)).then_inc(edges_loaded, DMA)
            for c in range(NG):
                sp.dma_start(X[:, c * GB:(c + 1) * GB, :], x_b[c]).then_inc(x_loaded[c], DMA)
            for t, a in ((wsf, w_self.rearrange("(k p) d -> p k d", p=P)),
                         (wnf, w_neigh.rearrange("(k p) d -> p k d", p=P)),
                         (gw[:, :, :], gate_w.rearrange("(k p) e -> p k e", p=P)),
                         (brow[:, :], gnn_b.rearrange("(a d) -> a d", a=1)),
                         (gb_b[:, :], gate_b.rearrange("(a d) -> a d", a=1).to_broadcast([BT, NEXP])),
                         (beta_b[:, :], beta.rearrange("(a d) -> a d", a=1).to_broadcast([BT, D])),
                         (b1rows, b1.rearrange("e (c f) -> (e c) f", f=P))):
                sp.dma_start(t, a).then_inc(const_loaded, DMA)
            for c in range(NG):
                if c < POOL_LOW:
                    sp.wait_ge(h_lo, c + 1)
                else:
                    sp.wait_ge(h_lo_dve, c - POOL_LOW + 1)
                sp.dma_start(h_b[c], H16[:, c * GB:(c + 1) * GB, :, :].rearrange("p b a d -> p b (a d)")).then_inc(h_stored, DMA)
            sp.wait_ge(h_stored, NG * DMA)
            sp.wait_ge(edge_out, 6)
            sp.sem_inc(w1_lo, 1)
            sp.sem_inc(w2_lo, 1)
            sp.sem_inc(hT_made, 1)
            sp.sem_inc(x1_made, 1)
            sp.sem_inc(xx_stored, DMA)
            sp.sem_inc(xh_stored, DMA)

            def block_load(j):
                sp.wait_ge(hT_made, j + 1)
                sp.dma_start(hx_h[0:BT, :, :], h_tab[bass.ds(j * BT, BT), :].rearrange("p (a d) -> p a d", a=2)).then_inc(hxh_loaded, DMA)
                sp.wait_ge(x1_made, j + 1)
                sp.dma_start(hx_x[0:BT, :], x[bass.ds(j * BT, BT), :]).then_inc(hxx_loaded, DMA)

            def block_store(j):
                sp.wait_ge(x1_ready, j + 1)
                sp.dma_start(xx_tab[bass.ds(j * BT, BT), :].rearrange("p (a d) -> p a d", a=2), xx[0:BT, :, :]).then_inc(xx_stored, DMA)
                sp.wait_ge(xt_lo, j + 1)
                carry(sp)
                sp.dma_start(xh_tab[bass.ds(j * BT, BT), :].rearrange("p (a d) -> p a d", a=2), xh[0:BT, :, :]).then_inc(xh_stored, DMA)

            for lo, hi, weights, own in SPANS:
                with sp.Fori(lo, hi) as i:
                    if weights == "both":
                        sp.wait_ge(w1_lo, i + 1)
                        sp.dma_start(wstg1.rearrange("p (k f) -> p k f", f=F),
                                     w1[bass.ds(i, 1), :, :].rearrange("e (k p) f -> p (e k) f", p=P)).then_inc(w1_loaded, DMA)
                        sp.wait_ge(w2_lo, i + 1)
                        sp.dma_start(wstg2.rearrange("p (c d) -> p c d", d=D),
                                     w2[bass.ds(i, 1), :, :].rearrange("e (c p) d -> p (e c) d", p=P)).then_inc(w2_loaded, DMA)
                    if weights == "last w1":
                        sp.wait_ge(w2_lo, NEXP)
                        sp.dma_start(wstg2.rearrange("p (k f) -> p k f", f=F),
                                     w1[NEXP - 1, :, :].rearrange("(k p) f -> p k f", p=P)).then_inc(w1_loaded, DMA)
                    if own:
                        block_load(i - LAG)
                    if own in ("block", "last"):
                        block_store(i - LAG - 1)
            block_load(NB - 1)
            block_store(NB - 2)
            sp.wait_ge(adds_done, ER + 2)
            for c in range(NG):
                if c == NG - 1:
                    block_store(NB - 1)
                    sp.wait_ge(logits_out, NB)
                    sp.wait_ge(xx_stored, (NB + 1) * DMA)
                sp.wait_ge(xh_stored, (GB * (c + 1) + 1) * DMA)
                sp.dma_start(pay_w.bitcast(f16).rearrange("p (b w) -> p b w", w=2 * ROW)[0:BT, c * GB:(c + 1) * GB, 0:2 * D],
                             xh_tab[c * GT:(c + 1) * GT, :].rearrange("(b p) d -> p b d", p=BT)).then_inc(pay_loaded, DMA)
            sp.dma_start(wstg3.rearrange("p (c d) -> p c d", d=D),
                         w2[NEXP - 1, :, :].rearrange("(c p) d -> p c d", p=P)).then_inc(w2_loaded, DMA)

            sp.wait_ge(items_ready, 1)
            with sp.Fori(0, NEXP) as e:
                row = sp.value_load(padrow[0:1, bass.ds(e, 1)], min_val=0, max_val=NEXP * REG - P)
                sp.dma_start(xs[bass.ds(row, P), :], padt).then_inc(padded, DMA)
            sp.dma_start(xs[DUMMY:DUMMY + P, :], padt).then_inc(padded, DMA)
            sp.wait_ge(padded, (NEXP + 1) * DMA)
            for h in range(2):
                sp.wait_ge(scattered[h], 2 * len(PARTS[h]) * DMA)

            def xx_load(q):
                sp.dma_start(XX3[q][0:BT, :, :, :],
                             xx_tab[q * GT:(q + 1) * GT, :].rearrange("(b p) (a d) -> p b a d", p=BT, a=2)).then_inc(zx_loaded[q], DMA)

            with sp.Fori(0, NITEM // 4) as m:
                for s in range(4):
                    row = sp.value_load(items[0:1, 1, bass.ds(4 * m + s, 1)], min_val=0, max_val=DUMMY)
                    sp.wait_ge(x16_copied, 4 * m + s + 1)
                    sp.wait_ge(meta_taken, 4 * m + s + 1)
                    sp.dma_start(xsr[:, s, :], xs[bass.ds(row, P), :]).then_inc(xs_in[s], DMA)

            for q in range(EARLY):
                xx_load(q)
            sp.dma_start(b2s, b2).then_inc(tail_loaded, DMA)
            sp.dma_start(gamma_b, gamma.rearrange("(a d) -> a d", a=1).to_broadcast([BT, D])).then_inc(tail_loaded, DMA)
            for s in range(4):
                sp.wait_ge(yo_out[s], NITEM // 4 * DMA)
            for q in range(NG):
                if q >= EARLY:
                    xx_load(q)
                sp.dma_start(Z[q][0:BT, :, :, :],
                             z_tab[2 * q * GT:2 * (q + 1) * GT, :].rearrange("(b p k) d -> p b k d", p=BT, k=2)).then_inc(zx_loaded[q], DMA)
            for q in range(NG):
                sp.wait_ge(out_ready, q + 1)
                sp.dma_start(out_b[q], Y[q][0:BT, :, :]).then_inc(out_stored, DMA)
            sp.wait_ge(out_stored, NG * DMA)

        @block.gpsimd
        def _(pool):
            g = nc.gpsimd
            g.iota(iota[:, :], [[1, P]], base=0, channel_multiplier=0, allow_small_or_imprecise_dtypes=True).then_inc(consts_made, 1)
            g.iota(iotap[:, :], [[0, 1]], base=0, channel_multiplier=1, allow_small_or_imprecise_dtypes=True).then_inc(consts_made, 1)
            g.iota(need[0:1, 1:ER + 1], [[BT, NIT], [0, 2]], base=-BT * (LAG - 1), channel_multiplier=0,
                   allow_small_or_imprecise_dtypes=True).then_inc(consts_made, 1)
            g.memset(ident[:, :], 0.0).then_inc(consts_made, 1)
            g.memset(lower[:, :], 0.0).then_inc(consts_made, 1)
            g.memset(bias_one[:, :], WSS).then_inc(consts_made, 1)
            g.memset(ones16[:, :], 1.0).then_inc(consts_made, 1)
            pool.wait_ge(consts_made, 3)
            g.memset(need[0:1, 0:1], 0.0).then_inc(consts_made, 1)
            pool.wait_ge(consts_made, 8)
            g.affine_select(out=ident[:, :], in_=ident[:, :], compare_op=ALU.not_equal, fill=1.0,
                            base=0, pattern=[[-1, P]], channel_multiplier=1).then_inc(consts_made, 1)
            g.affine_select(out=lower[:, :], in_=lower[:, :], compare_op=ALU.is_ge, fill=1.0,
                            base=0, pattern=[[-1, BT]], channel_multiplier=1).then_inc(consts_made, 1)
            g.tensor_copy(iota16[:, :], iota[:, :]).then_inc(consts_made, 1)
            pool.wait_ge(consts_made, 11)
            g.tensor_copy(ident16[:, :], ident[:, :]).then_inc(consts_made, 1)
            g.tensor_copy(lower16[:, :], lower[:, :]).then_inc(consts_made, 1)
            pool.wait_ge(edges_loaded, 6 * DMA)
            g.tensor_copy(srowf, srow).then_inc(rows_ready, 1)
            g.memset(AGG[:, :, :], 0.0).then_inc(consts_made, 1)
            for c in range(POOL_LOW):
                bs = slice(c * GB, (c + 1) * GB)
                pool.wait_ge(h_hi, c + 1)
                g.tensor_tensor(H16[:, bs, 1, :], H[:, bs, :], H16[:, bs, 0, :], ALU.subtract).then_inc(h_lo, 1)

            pool.wait_ge(h_stored, NG * DMA)
            pool.wait_ge(flag_ready, 1)
            flag = pool.value_load(irregular[0:1, 0:1], min_val=0, max_val=1)
            with pool.If(flag == 1):
                with pool.Fori(0, NWIN) as w:
                    with pool.Fori(0, ER) as r:
                        pool.wait_ge(fb_staged, ER * w + r + 1)
                        carry(pool)
                        for j in range(TPR):
                            g.indirect_dma_start(msg[:, j // QT, j % QT, :, :].rearrange("p a d -> p (a d)"), None, h_tab[:, :],
                                                 bass.IndirectOffsetOnAxis(ap=stage[:, j // QT, j % QT:j % QT + 1], axis=0)
                                                 ).then_inc(fb_gathered[j], DMA)
            with pool.Fori(0, NIT) as i:
                for s in range(QR):
                    pool.wait_ge(stage_ready, QR * i + s + 1)
                    carry(pool)
                    for u in range(QT):
                        g.indirect_dma_start(msg[:, s, u, :, :].rearrange("p a d -> p (a d)"), None, h_tab[:, :],
                                             bass.IndirectOffsetOnAxis(ap=stage[:, s, u:u + 1], axis=0)
                                             ).then_inc(gathered[s], DMA)

            pool.wait_ge(mean_made, NB)
            g.iota(ebase, [[REG, NEXP]], base=0, channel_multiplier=0, allow_small_or_imprecise_dtypes=True).then_inc(tok_made, 1)
            g.iota(tokf, [[2 * BT, NB], [1, 2]], base=0, channel_multiplier=2, allow_small_or_imprecise_dtypes=True).then_inc(tok_made, 1)

            for k in range(2):
                for h in range(2):
                    pool.wait_ge(meta_made, 2 * k + h + 1)
                    if k == 0:
                        pool.wait_ge(pay_loaded, NG * DMA)
                    carry(pool)
                    for b in PARTS[h]:
                        g.indirect_dma_start(xs[:, :], bass.IndirectOffsetOnAxis(ap=sloti[:, b, k:k + 1], axis=0),
                                             pay[0:BT, b, :], None).then_inc(scattered[h], DMA)

            def take(s, m):
                pool.wait_ge(xs_in[s], DMA * (m + 1))
                if not (isinstance(m, int) and m == 0):
                    pool.wait_ge(yo_out[s], DMA * m)
                carry(pool)
                g.tensor_copy(meta[:, s, :], xsr[:, s, D:D + 2]).then_inc(meta_taken, 1)

            def send(s, m):
                pool.wait_ge(yo_ready, 4 * m + s + 3)
                carry(pool)
                g.indirect_dma_start(z_tab[:, :], bass.IndirectOffsetOnAxis(ap=meta[:, s, 0:1].bitcast(i32), axis=0),
                                     yo[:, s, :], None, bounds_check=2 * N - 1, oob_is_err=False).then_inc(yo_out[s], DMA)

            def pool_step(n, m=None):
                for job, ahead in ((send, 0), (take, 2)):
                    run_item(job, n, ahead, m)

            pool.sem_inc(meta_taken, 4)
            for n in range(-2, 4):
                pool_step(n)
            with pool.Fori(1, NITEM // 4 - 1) as m:
                for s in range(4):
                    pool_step(s, m)
            for n in range(NITEM - 4, NITEM):
                pool_step(n)

            for q in range(NG):
                pool.wait_ge(zx_loaded[q], 2 * DMA)
                g.tensor_tensor(Z[q][0:BT, :, 0, :], Z[q][0:BT, :, 0, :], Z[q][0:BT, :, 1, :], ALU.add).then_inc(z_added, 1)

        @block.scalar
        def _(act):
            a = nc.scalar
            act.wait_ge(edge_T, 1)
            a.activation(srcT[:, 0:ET].rearrange("p (r j) -> p j r", j=TPR), PS[:, 0:TPR, 0:ER], ACT.Copy).then_inc(edge_out, 1)
            a.activation(relT[:, 0:ET].rearrange("p (r j) -> p j r", j=TPR), PS[:, 0:TPR, P:P + ER], ACT.Copy).then_inc(edge_out, 1)
            a.activation(base_row[0:1, :], PS[0:1, 0, 2 * P:2 * P + ER], ACT.Copy).then_inc(edge_out, 1)
            a.activation(b1T[:, :], PS[:, 2, 2 * P:2 * P + NEXP * FC], ACT.Copy).then_inc(edge_out, 1)
            for c in range(NG):
                bs = slice(c * GB, (c + 1) * GB)
                act.wait_ge(h_made, c + 1)
                a.activation(H16[:, bs, 0, :], H[:, bs, :], ACT.Copy).then_inc(h_hi, 1)
            act.wait_ge(edge_out, 6)
            act.wait_ge(h_stored, NG * DMA)
            act.wait_ge(flag_ready, 1)
            flag = act.value_load(irregular[0:1, 0:1], min_val=0, max_val=1)
            with act.If(flag == 1):
                with act.Fori(0, NWIN) as w:
                    with act.Fori(0, ER) as r:
                        act.wait_ge(fb_done, ER * w + r + 1)
                        a.activation(stage[:, 0:2, :], srcT[:, bass.ds(TPR * r, TPR)].rearrange("p (h u) -> p h u", u=QT),
                                     ACT.Copy).then_inc(fb_staged, 1)
                act.wait_ge(fb_done, ER * NWIN + 1)

            def stage_quad(i, s):
                act.wait_ge(quads_done, QR * i + s + 1)
                a.activation(stage[:, s, :], srcT[:, bass.ds(RING * i + QT * s, QT)], ACT.Copy).then_inc(stage_ready, 1)

            def hT_out(j):
                act.wait_ge(hT_made, j + 2)
                a.activation(hT, p_hT[:, :, :, 0:BT], ACT.Copy).then_inc(hT_copied, 1)

            def xt_high(j):
                act.wait_ge(xt_made, j + 1)
                act.wait_ge(xh_stored, DMA * (j + 1))
                a.activation(xh[0:BT, 0, :], xx[0:BT, 1, :], ACT.Copy).then_inc(xt_hi, 1)

            def xtT_out(j):
                act.wait_ge(xtT_made, j + 1)
                a.activation(xtT, p_xT[:, :, 0:BT], ACT.Copy).then_inc(xtT_copied, 1)

            for lo, hi, weights, first, second in LATE:
                with act.Fori(lo, hi) as i:
                    stage_quad(i, 0)
                    if second:
                        xt_high(i - LAG - 2)
                    stage_quad(i, 1)
                    if first:
                        hT_out(i - LAG - 1)
                    if second:
                        xtT_out(i - LAG - 2)
                    if weights == "both":
                        act.wait_ge(w1_loaded, DMA * i)
                        a.activation(W1[:, bass.ds(i - 1, 1), 0, :, :].rearrange("p e k f -> p (e k f)"), wstg1, ACT.Copy, scale=WS1).then_inc(w1_hi, 1)
                    if weights == "last w1":
                        act.wait_ge(w1_loaded, DMA * NEXP)
                        act.wait_ge(w1_lo, NEXP)
                        a.activation(W1[:, NEXP - 1, 0, :, :].rearrange("p k f -> p (k f)"), wstg2, ACT.Copy, scale=WS1).then_inc(w1_hi, 1)
                    stage_quad(i, 2)
                    stage_quad(i, 3)
                    if weights == "both":
                        act.wait_ge(w2_loaded, DMA * i)
                        a.activation(W2[:, bass.ds(i - 1, 1), 0, :, :].rearrange("p e c d -> p (e c d)"), wstg2, ACT.Copy, scale=WS2).then_inc(w2_hi, 1)
            xt_high(NB - 3)
            hT_out(NB - 2)
            xtT_out(NB - 3)
            xt_high(NB - 2)
            hT_out(NB - 1)
            xtT_out(NB - 2)
            xt_high(NB - 1)
            xtT_out(NB - 1)

            act.wait_ge(delta, 1)
            a.activation(e1, dl, ACT.Exp).then_inc(expd, 1)
            act.wait_ge(w2_loaded, DMA * NEXP)
            act.wait_ge(w1_lo, NEXP + 1)
            a.activation(W2[:, NEXP - 1, 0, :, :].rearrange("p c d -> p (c d)"), wstg3, ACT.Copy, scale=WS2).then_inc(w2_hi, 1)
            act.wait_ge(gT_made, 1)
            a.activation(gT, p_gT[:, 0:NB, 0:BT], ACT.Copy).then_inc(gT_copied, 1)

            def x_out(s, m):
                n = 4 * m + s
                act.wait_ge(x16_made, n + 1)
                act.wait_ge(l1_done, n + 1)
                a.activation(xT[:, s % 2, :, :, :], p_x16[s % 2], ACT.Copy).then_inc(x16_copied, 1)

            def relu(s, m):
                n = 4 * m + s
                act.wait_ge(l1_done, n + 3)
                act.wait_ge(w1_copied, n + 1)
                act.wait_ge(h_split, n + 1)
                for c in range(FC):
                    ins = a.activation(hr[:, s % 2, c * P:(c + 1) * P], p_h[s % 2][:, c * P:(c + 1) * P], ACT.Relu,
                                       bias=b1e[:, s % 2, c:c + 1], scale=1.0 / WS1)
                ins.then_inc(relu_done, 1)

            def high(s, m):
                n = 4 * m + s
                act.wait_ge(relu_done, n + 3)
                act.wait_ge(l2_done, n + 1)
                a.activation(hh[:, s % 2, :], hr[:, s % 2, :], ACT.Copy).then_inc(hi_split, 1)

            def weigh(s, m):
                n = 4 * m + s
                act.wait_ge(l2_done, n + 3)
                act.wait_ge(meta_taken, n + 5)
                if not (isinstance(m, int) and m == 0):
                    act.wait_ge(yo_out[s], DMA * m)
                a.activation(yo[:, s, :], p_y[s % 2], ACT.Copy, scale=meta[:, s, 1:2]).then_inc(yo_ready, 1)

            act.wait_ge(items_ready, 1)
            act.sem_inc(relu_done, 2)
            act.sem_inc(yo_ready, 2)
            act.sem_inc(x16_copied, 4)

            def act_step(n, m=None):
                for job, ahead in ((x_out, 3), (relu, 2), (high, 2), (weigh, 0)):
                    run_item(job, n, ahead, m)

            for n in range(-3, 4):
                act_step(n)
            with act.Fori(1, NITEM // 4 - 1) as m:
                for s in range(4):
                    act_step(s, m)
            for n in range(NITEM - 4, NITEM):
                act_step(n)

            for q in range(NG):
                act.wait_ge(stats_made, q + 1)
                for b in range(GB):
                    ins = a.activation(Y[q][0:BT, b, :], p_sum[q % 2][:, b, :], ACT.Identity,
                                       bias=nmr3[q % 2][:, b:b + 1], scale=rstd3[q % 2][:, b:b + 1])
                ins.then_inc(normed, 1)

        @block.tensor
        def _(pe):
            t = nc.tensor
            pe.wait_ge(consts_made, 14)
            pe.wait_ge(rows_ready, 3)
            for j in range(TPR):
                t.transpose(PS[:, j, 0:ER], srowf[:, j * P:(j + 1) * P], ident[0:ER, 0:ER])
                t.transpose(PS[:, j, P:P + ER], drowf[:, j * P:(j + 1) * P], ident[0:ER, 0:ER])
            t.transpose(PS[0:1, 0, 2 * P:2 * P + ER], bmin, ident[0:ER, 0:ER])
            t.transpose(PS[0:1, 1, 2 * P:2 * P + ER], bad, ident[0:ER, 0:ER])
            pe.wait_ge(const_loaded, 7 * DMA)
            ins = t.transpose(PS[:, 2, 2 * P:2 * P + NEXP * FC], b1rows, ident[0:NEXP * FC, 0:NEXP * FC])
            ins.then_inc(edge_T, 1)
            pe.wait_ge(edge_out, 6)
            pe.sem_inc(quads_done, QR)

            def tile_sums(bank, s, u, h, first, last):
                p = p_agg[bank]
                for k in range(KC):
                    for a in range(2):
                        t.matmul(p[:, k, :], msg[:, s, u, a, k * P:(k + 1) * P], oh[:, h, u, :],
                                 start=(first and a == 0), stop=(last and a == 1))
                return t.matmul(p[:, KC, :], ones16[:, :], oh[:, h, u, :], start=first, stop=last)

            pe.wait_ge(flag_ready, 1)
            flag = pe.value_load(irregular[0:1, 0:1], min_val=0, max_val=1)
            with pe.If(flag == 1):
                with pe.Fori(0, NWIN) as w:
                    with pe.Fori(0, ER) as r:
                        pe.wait_ge(fb_oh, 2 * (ER * w + r + 1))
                        pe.wait_ge(fb_done, ER * w + r + 1)
                        for j in range(TPR):
                            pe.wait_ge(fb_gathered[j], DMA * (ER * w + r + 1))
                            ins = tile_sums(0, j // QT, j % QT, j // QT, j == 0, j == TPR - 1)
                        ins.then_inc(fb_sums, 1)

            def turn_h(j):
                pe.wait_ge(hxh_loaded, DMA * (j + 1))
                for a in range(2):
                    for k in range(KC):
                        ins = t.transpose(p_hT[:, a, k, 0:BT], hx_h[0:BT, a, k * P:(k + 1) * P], ident16[0:BT, 0:BT])
                ins.then_inc(hT_made, 1)

            def x1_sum(j):
                pe.wait_ge(hT_copied, j + 1)
                pe.wait_ge(x1_made, j + 1)
                t.matmul(p_x1, bias_one[:, :], brow[:, :], start=True, stop=False)
                for ha, wa in ((0, 0), (1, 0), (0, 1)):
                    for k in range(KC):
                        t.matmul(p_x1, hT[:, ha, k, :], ws[:, wa, k, :], start=False, stop=False)
                pe.wait_ge(mean_made, j + 1)
                for k in range(KC):
                    ins = t.matmul(p_x1, meanT[:, k, :], wn[:, k, :], start=False, stop=(k == KC - 1))
                ins.then_inc(x1_summed, 1)

            def turn_xt(j):
                pe.wait_ge(xt_made, j + 1)
                for k in range(KC):
                    ins = t.transpose(p_xT[:, k, 0:BT], xx[0:BT, 1, k * P:(k + 1) * P], ident[0:BT, 0:BT])
                ins.then_inc(xtT_made, 1)

            def gate(j):
                pe.wait_ge(xtT_copied, j + 1)
                for k in range(KC):
                    ins = t.matmul(p_lg, xtT[:, k, :], gw[:, k, :], start=(k == 0), stop=(k == KC - 1))
                ins.then_inc(logits, 1)

            for lo, hi, weights, own in SPANS:
                with pe.Fori(lo, hi) as i:
                    for s in range(QR):
                        if s % 2 == 0:
                            pe.wait_ge(adds_done, 2 * i + s // 2 + 1)
                        pe.wait_ge(oh_ready, QR * i + s + 1)
                        pe.wait_ge(gathered[s], QT * DMA * (i + 1))
                        for u in range(QT):
                            ins = tile_sums(s // 2, s, u, s % 2, s % 2 == 0 and u == 0, s % 2 == 1 and u == QT - 1)
                        ins.then_inc(quads_done, 1)
                        if own and s == 1:
                            if own in ("block", "last"):
                                turn_xt(i - LAG - 1)
                            turn_h(i - LAG)
                        if own and s == 2:
                            x1_sum(i - LAG)
                            if own in ("block", "last"):
                                gate(i - LAG - 1)
            turn_xt(NB - 2)
            turn_h(NB - 1)
            x1_sum(NB - 1)
            gate(NB - 2)
            turn_xt(NB - 1)
            gate(NB - 1)

            pe.wait_ge(ohs_made, 1)
            t.matmul(p_cnt, ones16[0:BT, :], incl.rearrange("p (e b) -> p e b", b=NB)[:, :, NB - 1], start=True, stop=True).then_inc(counted, 1)
            t.matmul(p_pos, lower16[:, :], ohs, start=True, stop=False)
            t.matmul(p_pos, ones16[0:BT, 0:BT], excl, start=False, stop=True).then_inc(pos_made, 1)
            pe.wait_ge(gates_made, 1)
            for b in range(NB):
                ins = t.transpose(p_gT[:, b, 0:BT], gates[:, b, :], ident[0:BT, 0:BT])
            ins.then_inc(gT_made, 1)
            pe.wait_ge(item_cols, 1)
            for c in range(2):
                ins = t.transpose(p_item[:, c, 0:NITEM], scr[0:NITEM, c:c + 1], ident[0:NITEM, 0:NITEM])
            ins.then_inc(item_T, 1)

            def turn(s, m):
                n = 4 * m + s
                pe.wait_ge(xs_in[s], DMA * (m + 1))
                pe.wait_ge(x16_copied, n + 3)
                v = xsr[:, s, 0:D].bitcast(f16).rearrange("p (a k h) -> p a k h", a=2, k=KC)
                for h in range(2):
                    for k in range(KC):
                        ins = t.transpose(p_x16[s % 2][:, h, k, :], v[:, h, k, :], ident16[:, :])
                ins.then_inc(x16_made, 1)

            def up(s, m):
                n = 4 * m + s
                pe.wait_ge(w1_copied, n + 1)
                pe.wait_ge(x16_copied, n + 5)
                pe.wait_ge(relu_done, n + 1)
                for c in range(FC):
                    terms = [(wa, xa, k) for wa, xa in ((0, 0), (0, 1), (1, 0)) for k in range(KC)]
                    for y, (wa, xa, k) in enumerate(terms):
                        ins = t.matmul(p_h[s % 2][:, c * P:(c + 1) * P], w1e[:, s % 2, wa, k, c * P:(c + 1) * P],
                                       xT[:, s % 2, xa, k, :], start=(y == 0), stop=(y == len(terms) - 1))
                ins.then_inc(l1_done, 1)

            def down(s, m):
                n = 4 * m + s
                pe.wait_ge(w2_copied, n + 1)
                pe.wait_ge(h_split, n + 3)
                pe.wait_ge(yo_ready, n + 1)
                terms = [(h, wa, c) for h, wa in ((hh, 0), (hh, 1), (hl, 0)) for c in range(FC)]
                for y, (h, wa, c) in enumerate(terms):
                    ins = t.matmul(p_y[s % 2], h[:, s % 2, c * P:(c + 1) * P], w2e[:, s, wa, c, :],
                                   start=(y == 0), stop=(y == len(terms) - 1))
                ins.then_inc(l2_done, 1)

            pe.wait_ge(items_ready, 1)
            pe.wait_ge(gT_copied, 1)
            pe.sem_inc(l1_done, 2)
            pe.sem_inc(l2_done, 2)

            def pe_step(n, m=None):
                for job, ahead in ((turn, 3), (up, 2), (down, 0)):
                    run_item(job, n, ahead, m)

            for n in range(-3, 4):
                pe_step(n)
            with pe.Fori(1, NITEM // 4 - 1) as m:
                for s in range(4):
                    pe_step(s, m)
            for n in range(NITEM - 4, NITEM):
                pe_step(n)

            pe.wait_ge(tail_loaded, 2 * DMA)
            pe.wait_ge(yo_ready, NITEM + 2)
            for q in range(NG):
                s = q % 2
                pe.wait_ge(zx_loaded[q], 2 * DMA)
                pe.wait_ge(z_added, q + 1)
                if q >= 2:
                    pe.wait_ge(normed, q - 1)
                for b in range(GB):
                    t.matmul(p_sum[s][:, b, :], ident[0:BT, 0:BT], XX3[q][0:BT, b, 1, :], start=True, stop=False)
                    t.matmul(p_sum[s][:, b, :], ident[0:BT, 0:BT], Z[q][0:BT, b, 0, :], start=False, stop=False)
                    ins = t.matmul(p_sum[s][:, b, :], gT[:, GB * q + b, :], b2s, start=False, stop=True)
                ins.then_inc(summed, 1)

        @block.vector
        def _(dve):
            v = nc.vector

            v.memset(srow, 0).then_inc(edge_pads, 1)
            v.memset(drow, int(FAR)).then_inc(edge_pads, 1)
            v.memset(drow2, 0).then_inc(edge_pads, 1)
            link, n0 = counted_link(dve, dve_step, 0)
            dve.wait_ge(edges_loaded, 6 * DMA)
            v.tensor_copy(drowf, drow)
            link(v.tensor_copy(drowf2, drow2))
            link(v.tensor_reduce(bmin, drowf, AX.X, ALU.min))
            link(v.tensor_reduce(bmax, drowf2, AX.X, ALU.max))
            v.tensor_scalar(drowf, drowf, bmin, None, ALU.subtract).then_inc(rows_ready, 1)
            link(v.tensor_scalar(bmax, bmax, bmin, None, ALU.subtract))
            v.tensor_scalar(bad, bmax, float(P) - 0.5, None, ALU.is_gt).then_inc(rows_ready, 1)
            v.memset(relT[:, ET:ETP], FAR)
            for c in range(NG):
                dve.wait_ge(x_loaded[c], DMA)
                bs = range(c * GB, (c + 1) * GB)
                for b in bs:
                    ins = v.bn_stats(stats0[:, b, :], X[:, b, :])
                link(ins)
                for b in bs:
                    ins = v.bn_aggr(mv0[:, b, :], stats0[:, b, :])
            link(ins)
            rsqrt(v, link, mv0[:, :, 1], tmp0, rstd0)
            for c in range(NG):
                for b in range(c * GB, (c + 1) * GB):
                    ins = v.tensor_scalar(H[:, b, :], X[:, b, :], mv0[:, b, 0:1], rstd0[:, b:b + 1], ALU.subtract, ALU.mult)
                ins.then_inc(h_made, 1)
            for c in range(POOL_LOW, NG):
                bs = slice(c * GB, (c + 1) * GB)
                dve.wait_ge(h_made, c + 1)
                dve.wait_ge(h_hi, c + 1)
                v.tensor_tensor(H16[:, bs, 1, :], H[:, bs, :], H16[:, bs, 0, :], ALU.subtract).then_inc(h_lo_dve, 1)
            dve.wait_ge(const_loaded, 7 * DMA)
            v.tensor_scalar(wn[:, :, :], wnf, WSS, None, ALU.mult).then_inc(edge_out, 1)
            link(v.tensor_scalar(ws[:, 0, :, :], wsf, WSS, None, ALU.mult))
            v.scalar_tensor_tensor(ws[:, 1, :, :], wsf, WSS, ws[:, 0, :, :], ALU.mult, ALU.subtract).then_inc(edge_out, 1)
            dve.wait_ge(edge_out, 6)
            dve.wait_ge(consts_made, 14)
            v.tensor_reduce(badf, PS[0:1, 1, 2 * P:2 * P + ER], AX.X, ALU.max)
            link(v.tensor_tensor(late_row, need[:, 0:ER], PS[0:1, 0, 2 * P:2 * P + ER], ALU.subtract))
            link(v.tensor_reduce(lateness, late_row, AX.X, ALU.max))
            link(v.tensor_scalar(lateness, lateness, 0.5, None, ALU.is_gt))
            link(v.tensor_tensor(badf, badf, lateness, ALU.max))
            v.tensor_copy(irregular[:, :], badf).then_inc(flag_ready, 1)
            dve.wait_ge(flag_ready, 1)

            def onehots(r, h, signal):
                v.tensor_tensor(oh[:, h, :, :], iota16[:, :].unsqueeze(1).to_broadcast([P, QT, P]),
                                relT[:, bass.ds(TPR * r + QT * h, QT)].unsqueeze(2).to_broadcast([P, QT, P]),
                                ALU.is_equal).then_inc(signal, 1)

            flag = dve.value_load(irregular[0:1, 0:1], min_val=0, max_val=1)
            with dve.If(flag == 1):
                dve.sem_inc(fb_done, 1)
                dve.sem_inc(fb_moved, 1)
                with dve.Fori(0, NWIN) as w:
                    with dve.Fori(0, ER) as r:
                        dve.wait_ge(fb_moved, 2 * w + 1)
                        base = dve.value_load(base_row[0:1, bass.ds(r, 1)], min_val=0, max_val=N)
                        dve.wait_ge(fb_done, ER * w + r + 1)
                        carry(dve)
                        onehots(r, 0, fb_oh)
                        onehots(r, 1, fb_oh)
                        dve.wait_ge(fb_sums, ER * w + r + 1)
                        win = AGG[:, :, bass.ds(base, P)]
                        v.tensor_tensor(win, win, p_agg[0], ALU.add).then_inc(fb_done, 1)
                    dve.wait_ge(fb_done, ER * w + ER + 1)
                    v.tensor_scalar(relT[:, 0:ET], relT[:, 0:ET], -float(P), None, ALU.add).then_inc(fb_moved, 1)
                    v.tensor_scalar(base_row[0:1, :], base_row[0:1, :], float(P), float(N), ALU.add, ALU.min).then_inc(fb_moved, 1)
                dve.wait_ge(fb_moved, 2 * NWIN + 1)
                v.memset(relT[:, 0:ET], FAR).then_inc(fb_moved, 1)
                dve.wait_ge(fb_moved, 2 * NWIN + 2)

            def quad_onehots(r, h, ahead):
                if ahead is not None:
                    dve.wait_ge(quads_done, ahead + 1 + QR)
                onehots(r, h, oh_ready)

            def add(i, g):
                r = 2 * i + g
                base = dve.value_load(base_row[0:1, bass.ds(r, 1)], min_val=0, max_val=N)
                dve.wait_ge(quads_done, 2 * r + 2 + QR)
                dve.wait_ge(adds_done, r + 2)
                win = AGG[:, :, bass.ds(base, P)]
                v.tensor_tensor(win, win, p_agg[g], ALU.add).then_inc(adds_done, 1)

            dve.sem_inc(adds_done, 2)
            quad_onehots(0, 0, None)
            quad_onehots(0, 1, None)
            def mean(j):
                link, _ = counted_link(dve, deg_step, 2 * j)
                link(v.tensor_scalar_max(deg, AGG[:, KC, bass.ds(j * BT, BT)], 1.0), alone=True)
                link(v.reciprocal(deg, deg))
                v.tensor_tensor(meanT, AGG[:, 0:KC, bass.ds(j * BT, BT)], deg.unsqueeze(1).to_broadcast([P, KC, BT]),
                                ALU.mult).then_inc(mean_made, 1)

            LN_STEPS = 15

            def x1_norm(j):
                link, n = counted_link(dve, ln_step, LN_STEPS * j)
                x1, xt = xx[0:BT, 0, :], xx[0:BT, 1, :]
                dve.wait_ge(x1_summed, j + 1)
                dve.wait_ge(hxx_loaded, DMA * (j + 1))
                dve.wait_ge(xx_stored, DMA * (j + 1))
                v.scalar_tensor_tensor(x1, p_x1, 1.0 / WSS, hx_x[0:BT, :], ALU.mult, ALU.add).then_inc(x1_made, 1)
                dve.wait_ge(x1_made, j + 2)
                carry(dve)
                link(v.bn_stats(stats, x1), alone=True)
                link(v.bn_aggr(mv, stats))
                rsqrt(v, link, mv[:, 1:2], tmp, rstd)
                v.tensor_scalar(xt, x1, mv[:, 0:1], rstd, ALU.subtract, ALU.mult).then_inc(xt_made, 1)
                dve.wait_ge(xt_made, j + 1)
                v.tensor_tensor(x1, x1, beta_b[:, :], ALU.add).then_inc(x1_ready, 1)
                dve.sem_inc(ln_step, LN_STEPS - n[0])

            def xt_low(j):
                dve.wait_ge(xt_hi, j + 1)
                v.tensor_tensor(xh[0:BT, 1, :], xx[0:BT, 1, :], xh[0:BT, 0, :], ALU.subtract).then_inc(xt_lo, 1)

            def gate_out(j):
                dve.wait_ge(logits, j + 1)
                v.tensor_tensor(lg[:, :], p_lg, gb_b[:, :], ALU.add).then_inc(logits_out, 1)
                dve.wait_ge(logits_out, j + 1)
                dve.wait_ge(top_out, 2 * j + 2)
                carry(dve)
                v.max(m8[:, :], lg[:, :]).then_inc(top_step, 1)
                dve.wait_ge(top_step, 2 * j + 1)
                carry(dve)
                v.max_index(i8[:, :], m8[:, :], lg[:, :]).then_inc(top_step, 1)
                v.tensor_copy(val[:, bass.ds(j, 1), :].rearrange("p b k -> p (b k)"), m8[:, 0:2]).then_inc(top_out, 1)
                dve.wait_ge(top_step, 2 * j + 2)
                v.tensor_copy(idxf[:, bass.ds(j, 1), :].rearrange("p b k -> p (b k)"), i8[:, 0:2]).then_inc(top_out, 1)

            dve.sem_inc(top_out, 2)
            for lo, hi, weights, own in SPANS:
                with dve.Fori(lo, hi) as i:
                    quad_onehots(2 * i + 1, 0, QR * i)
                    quad_onehots(2 * i + 1, 1, QR * i + 1)
                    add(i, 0)
                    if own:
                        dve.wait_ge(adds_done, 2 * i + 3)
                        mean(i - LAG)
                    if own in ("block", "last"):
                        xt_low(i - LAG - 1)
                    if own != "last":
                        quad_onehots(2 * i + 2, 0, QR * i + 2)
                    if weights == "both":
                        dve.wait_ge(w1_hi, i + 1)
                        w = W1[:, bass.ds(i, 1), :, :, :].rearrange("p e a k f -> p (e a) (k f)")
                        v.scalar_tensor_tensor(w[:, 1, :], wstg1, WS1, w[:, 0, :], ALU.mult, ALU.subtract).then_inc(w1_lo, 1)
                    if weights == "last w1":
                        dve.wait_ge(w1_hi, NEXP)
                        w = W1[:, NEXP - 1, :, :, :].rearrange("p a k f -> p a (k f)")
                        v.scalar_tensor_tensor(w[:, 1, :], wstg2, WS1, w[:, 0, :], ALU.mult, ALU.subtract).then_inc(w1_lo, 1)
                    if own in ("block", "last"):
                        gate_out(i - LAG - 1)
                    if own == "last":
                        x1_norm(i - LAG)
                    else:
                        quad_onehots(2 * i + 2, 1, QR * i + 3)
                    add(i, 1)
                    if weights == "both":
                        dve.wait_ge(w2_hi, i + 1)
                        w = W2[:, bass.ds(i, 1), :, :, :].rearrange("p e a c d -> p (e a) (c d)")
                        v.scalar_tensor_tensor(w[:, 1, :], wstg2, WS2, w[:, 0, :], ALU.mult, ALU.subtract).then_inc(w2_lo, 1)
                    if own and own != "last":
                        x1_norm(i - LAG)
            dve.wait_ge(adds_done, ER + 2)
            mean(NB - 1)
            xt_low(NB - 2)
            gate_out(NB - 2)
            dve.wait_ge(mean_made, NB)
            link, n1 = counted_link(dve, dve_step, n0[0])
            by_expert = lambda ap: ap.rearrange("p (e b) -> p e b", b=NB)
            v.memset(padt, 0.0)
            v.tensor_scalar(thr, iota[:, 0:NTHR], float(P), None, ALU.mult)
            link(v.memset(keep, 1.0))
            v.memset(by_expert(keep)[:, :, 0], 0.0)
            link(v.memset(padt.bitcast(i32)[:, D:D + 1], SKIP))
            x1_norm(NB - 1)
            xt_low(NB - 1)
            gate_out(NB - 1)
            dve.wait_ge(top_out, 2 * NB + 2)
            v.tensor_tensor(dl, val[:, :, 1], val[:, :, 0], ALU.subtract).then_inc(delta, 1)
            link(v.tensor_tensor(oh2, iota[0:BT, 0:NEXP].unsqueeze(1).unsqueeze(1).to_broadcast([BT, NB, 2, NEXP]),
                                 idxf[:, :, :].unsqueeze(3).to_broadcast([BT, NB, 2, NEXP]), ALU.is_equal))
            link(v.tensor_tensor(by_expert(ohs), oh2[:, :, 0, :].rearrange("p b e -> p e b"),
                                 oh2[:, :, 1, :].rearrange("p b e -> p e b"), ALU.add))
            link(v.tensor_tensor_scan(incl, keep, ohs, 0.0, ALU.mult, ALU.add))
            v.tensor_tensor(excl, incl, ohs, ALU.subtract).then_inc(ohs_made, 1)
            dve.wait_ge(expd, 1)
            link(v.tensor_scalar_add(dl, e1, 1.0))
            link(v.reciprocal(wt[:, :, 0], dl))
            link(v.tensor_tensor(wt[:, :, 1], e1, wt[:, :, 0], ALU.mult))
            dve.wait_ge(tok_made, 2)
            dve.wait_ge(pos_made, 1)
            link(v.tensor_tensor(by_expert(posb), by_expert(p_pos), ebase[:, :].unsqueeze(2).to_broadcast([BT, NEXP, NB]), ALU.add))
            at_of = by_expert(posb).rearrange("p e b -> p b e")

            def slots(k):
                link(v.tensor_tensor(prod[:, :, k, :], oh2[:, :, k, :], at_of, ALU.mult))
                link(v.tensor_reduce(slotf[:, :, k], prod[:, :, k, :], AX.X, ALU.add))
                link(v.tensor_copy(sloti[:, :, k], slotf[:, :, k]))

            slots(0)
            dve.wait_ge(quads_done, 2 * ER + QR)
            dve.wait_ge(xx_stored, (NB + 1) * DMA)
            dve.wait_ge(xh_stored, (NB + 1) * DMA)
            for k in range(2):
                for h in range(2):
                    if k == 1:
                        dve.wait_ge(scattered[h], len(PARTS[h]) * DMA)
                    bh = slice(PARTS[h][0], PARTS[h][-1] + 1)
                    v.tensor_copy(pay_i[0:BT, bh, D], tokf[:, bh, k])
                    v.tensor_scalar(pay[0:BT, bh, D + 1], wt[:, bh, k], 1.0 / WS2, None, ALU.mult).then_inc(meta_made, 1)
                if k == 0:
                    slots(1)
                    link(v.tensor_tensor(prod, oh2, wt.unsqueeze(3).to_broadcast([BT, NB, 2, NEXP]), ALU.mult))
                    v.tensor_tensor(gates, prod[:, :, 0, :], prod[:, :, 1, :], ALU.add).then_inc(gates_made, 1)
                    dve.wait_ge(counted, 1)
                    link(v.tensor_copy(cnt, p_cnt))
                    link(v.tensor_tensor(cmp1, cnt.unsqueeze(2).to_broadcast([P, NEXP, NTHR]),
                                         thr.unsqueeze(1).to_broadcast([P, NEXP, NTHR]), ALU.is_gt))
                    link(v.tensor_reduce(ntile, cmp1, AX.X, ALU.add))
                    link(v.tensor_tensor_scan(pincl, ones16[:, 0:NEXP], ntile, 0.0, ALU.mult, ALU.add))
                    link(v.tensor_scalar(cmp2, pincl, iotap[:, :], None, ALU.is_le))
                    v.tensor_reduce(scr[:, 2:3], cmp2, AX.X, ALU.add)
                    link(v.tensor_tensor(cmp2, cmp2, pincl, ALU.mult))
                    link(v.tensor_reduce(scr[:, 3:4], cmp2, AX.X, ALU.max))
                    link(v.tensor_tensor(scr[:, 4:5], iotap[:, :], scr[:, 3:4], ALU.subtract))
                    link(v.tensor_scalar(scr[:, 5:6], scr[:, 2:3], float(REG), -float(DUMMY), ALU.mult, ALU.add))
                    link(v.scalar_tensor_tensor(scr[:, 6:7], scr[:, 4:5], float(P), scr[:, 5:6], ALU.mult, ALU.add))
                    link(v.tensor_scalar(scr[:, 7:8], scr[:, 2:3], float(NEXP) - 0.5, None, ALU.is_lt))
                    link(v.tensor_tensor(scr[:, 8:9], scr[:, 6:7], scr[:, 7:8], ALU.mult))
                    link(v.tensor_scalar_add(scr[:, 1:2], scr[:, 8:9], float(DUMMY)))
                    v.tensor_scalar_min(scr[:, 0:1], scr[:, 2:3], float(NEXP - 1)).then_inc(item_cols, 1)
                    v.tensor_tensor(padrow[:, :], cnt[0:1, :], ebase[0:1, :], ALU.add)
                    dve.wait_ge(item_T, 1)
                    v.tensor_copy(items[:, :, :], p_item[:, :, 0:NITEM]).then_inc(items_ready, 1)
                    dve.wait_ge(items_ready, 1)
                    dve.wait_ge(w2_hi, NEXP)
                    w = W2[:, NEXP - 1, :, :, :].rearrange("p a c d -> p a (c d)")
                    v.scalar_tensor_tensor(w[:, 1, :], wstg3, WS2, w[:, 0, :], ALU.mult, ALU.subtract).then_inc(w2_lo, 1)
            base2 = n0[0] + n1[0]

            def load_w(s, m):
                n = 4 * m + s
                e = dve.value_load(items[0:1, 0, bass.ds(n, 1)], min_val=0, max_val=NEXP - 1)
                dve.wait_ge(l1_done, n + 1)
                dve.wait_ge(relu_done, n + 1)
                v.tensor_copy(b1e[:, s % 2, :], b1T[:, bass.ds(e * FC, FC)])
                v.tensor_copy(w1e[:, s % 2, :, :, :].rearrange("p a k f -> p (a k f)"),
                              W1[:, bass.ds(e, 1), :, :, :].rearrange("p e a k f -> p (e a k f)")).then_inc(w1_copied, 1)
                if not (isinstance(m, int) and m == 0):
                    dve.wait_ge(l2_done, 4 * (m - 1) + s + 3)
                v.tensor_copy(w2e[:, s, :, :, :].rearrange("p a c d -> p (a c d)"),
                              W2[:, bass.ds(e, 1), :, :, :].rearrange("p e a c d -> p (e a c d)")).then_inc(w2_copied, 1)

            def split(s, m):
                n = 4 * m + s
                dve.wait_ge(hi_split, n + 1)
                v.tensor_tensor(hl[:, s % 2, :], hr[:, s % 2, :], hh[:, s % 2, :], ALU.subtract).then_inc(h_split, 1)

            for h in range(2):
                dve.wait_ge(scattered[h], 2 * len(PARTS[h]) * DMA)
            dve.wait_ge(gT_made, 1)
            dve.wait_ge(padded, (NEXP + 1) * DMA)
            dve.wait_ge(w2_lo, NEXP + 1)
            dve.sem_inc(h_split, 2)

            def dve_step_of(n, m=None):
                for job, ahead in ((load_w, 3), (split, 2)):
                    run_item(job, n, ahead, m)

            for n in range(-3, 4):
                dve_step_of(n)
            with dve.Fori(1, NITEM // 4 - 1) as m:
                for s in range(4):
                    dve_step_of(s, m)
            for n in range(NITEM - 4, NITEM):
                dve_step_of(n)

            dve.wait_ge(tail_loaded, 2 * DMA)
            link, _ = counted_link(dve, dve_step, base2)
            for q in range(NG + 1):
                if q < NG:
                    s = q % 2
                    dve.wait_ge(summed, q + 1)
                    for b in range(GB):
                        ins = v.bn_stats(stats3[0:BT, b, :], p_sum[s][:, b, :])
                    link(ins)
                    for b in range(GB):
                        ins = v.bn_aggr(mv3[s][:, b, :], stats3[0:BT, b, :])
                    link(ins)
                    rsqrt(v, link, mv3[s][:, :, 1], tmp3, rstd3[s])
                    v.scalar_tensor_tensor(nmr3[s], mv3[s][:, :, 0], -1.0, rstd3[s], ALU.mult, ALU.mult).then_inc(stats_made, 1)
                if q >= 1:
                    y = Y[q - 1][0:BT, :, :]
                    dve.wait_ge(normed, q)
                    link(v.tensor_tensor(y, y, gamma_b[:, :].unsqueeze(1).to_broadcast([BT, GB, D]), ALU.mult))
                    v.tensor_tensor(y, y, XX3[q - 1][0:BT, :, 0, :], ALU.add).then_inc(out_ready, 1)


_INS = ["x", "src", "dst", "L0_gnn_W_self", "L0_gnn_W_neigh", "L0_gnn_b", "L0_ffn_gate_w", "L0_ffn_gate_b",
        "L0_ffn_w1", "L0_ffn_b1", "L0_ffn_w2", "L0_ffn_b2", "L0_ffn_gamma", "L0_ffn_beta"]


def kernel(**inputs):
    import numpy as np
    import concourse.bacc as bacc
    from concourse import mybir as mb
    from concourse.bass_utils import run_bass_kernel_spmd

    nc = bacc.Bacc("TRN2", target_bir_lowering=False, num_devices=1)
    arrays, args = {}, []
    for name in _INS:
        a = np.ascontiguousarray(inputs[name])
        arrays[f"in_{name}"] = a
        args.append(nc.dram_tensor(f"in_{name}", a.shape, mb.dt.from_np(a.dtype), kind="ExternalInput").ap())
    args.append(nc.dram_tensor("out_0", (N, D), mb.dt.float32, kind="ExternalOutput").ap())
    build(nc, *args)
    r = run_bass_kernel_spmd(nc, [arrays], core_ids=[0])
    return r.results[0]["out_0"]
```

```python
import concourse.bass as bass
from concourse import mybir
from contextlib import ExitStack

N = 3125
D = 256
E = 53125
NEXP = 16
F = 512
EPS = 1e-5

P = 128
KC = D // P
FC = F // P
BT = 125
NB = N // BT
GB = 5
NG = NB // GB
GT = GB * BT

ET = -(-E // P)
TPR = 8
ER = ET // TPR
ETP = ET + 8
QT = 4
QR = 4
RING = QT * QR
NIT = ET // RING
LAG = 2
AGGW = N + P + 9
FAR = 1.0e6
NWIN = -(-N // P)

WSS = 16.0
WS1 = 16.0
WS2 = 64.0
NITEM = NEXP + (2 * N - NEXP) // P
SKIP = 1 << 20
ARENA = 7680
NTHR = -(-N // P)


def build(nc, x, src, dst, w_self, w_neigh, gnn_b, gate_w, gate_b, w1, b1, w2, b2, gamma, beta, out):
    f32, f16, i32, u32 = mybir.dt.float32, mybir.dt.float16, mybir.dt.int32, mybir.dt.uint32
    ALU = mybir.AluOpType
    ACT = mybir.ActivationFunctionType
    AX = mybir.AxisListType

    ctx = ExitStack()
    with ctx:
        def sb(name, shape, dt=f32):
            return ctx.enter_context(nc.sbuf_tensor(name, shape, dt))

        def sem(name):
            return ctx.enter_context(nc.semaphore(name))

        def dram(name, shape, dt=f32):
            return nc.dram_tensor(name, shape, dt, kind="Internal").ap()

        h_tab = dram("h_tab", [N, 2 * D], f16)
        xh_tab = dram("xh_tab", [N, 2 * D], f16)
        xx_tab = dram("xx_tab", [N, 2 * D])
        z_tab = dram("z_tab", [2 * N, D])

        W1 = sb("W1", [P, NEXP, 2, KC, F], f16)
        W2 = sb("W2", [P, NEXP, 2, FC, D], f16)
        AGG = sb("AGG", [P, KC + 1, AGGW])
        ident = sb("ident", [P, P])
        ident16 = sb("ident16", [P, P], f16)
        iota = sb("iota", [P, P])
        iotap = sb("iotap", [P, 1])
        iota16 = sb("iota16", [P, P], f16)
        ones16 = sb("ones16", [P, P], f16)
        bias_one = sb("bias_one", [1, BT])
        lower = sb("lower", [BT, BT])
        lower16 = sb("lower16", [BT, BT], f16)
        ws = sb("ws", [P, 2, KC, D], f16)
        wn = sb("wn", [P, KC, D])
        gw = sb("gw", [P, KC, NEXP])
        brow = sb("brow", [1, D])
        gb_b = sb("gb_b", [BT, NEXP])
        beta_b = sb("beta_b", [BT, D])
        b1T = sb("b1T", [P, NEXP * FC])
        need = sb("need", [1, ER + 1])
        lg = sb("lg", [BT, NEXP])
        m8 = sb("m8", [BT, 8])
        i8 = sb("i8", [BT, 8], u32)
        val = sb("val", [BT, NB, 2])
        idxf = sb("idxf", [BT, NB, 2])
        items = sb("items", [1, NITEM + 4], i32)
        tok_of = sb("tok_of", [P, NITEM + 4], i32)
        meta_of = sb("meta_of", [P, NITEM + 4, 2])
        irregular = sb("irregular", [1, 1], i32)
        arena = sb("arena", [P, ARENA])

        at = [0]

        def part(words):
            a = at[0]
            at[0] += words
            assert at[0] <= ARENA, at[0]
            return arena[:, a:a + words]

        pro = W2[:, :, :, :, :].rearrange("p e s c f -> p (e s c f)").bitcast(f32)
        X = pro[0:BT, 0:NB * D].rearrange("p (b d) -> p b d", d=D)
        H = pro[0:BT, NB * D:2 * NB * D].rearrange("p (b d) -> p b d", d=D)
        pr1 = W1[:, :, :, :, :].rearrange("p e s c f -> p (e s c f)").bitcast(f32)
        H16 = pr1[0:BT, 0:NB * D].bitcast(f16).rearrange("p (b a d) -> p b a d", a=2, d=D)
        o = NB * D
        L = TPR * P
        srow = pr1[0:ER, o:o + L].bitcast(i32)
        drow = pr1[0:ER, o + L:o + 2 * L].bitcast(i32)
        drow2 = pr1[0:ER, o + 2 * L:o + 3 * L].bitcast(i32)
        srowf = pr1[0:ER, o + 3 * L:o + 4 * L]
        drowf = pr1[0:ER, o + 4 * L:o + 5 * L]
        drowf2 = pr1[0:ER, o + 5 * L:o + 6 * L]
        o += 6 * L
        wsf = pr1[:, o:o + KC * D].rearrange("p (k d) -> p k d", d=D)
        b1rows = pr1[0:NEXP * FC, o + KC * D:o + KC * D + P]
        o += KC * D + P
        stats0 = pr1[0:BT, o:o + NB * 6].rearrange("p (b s) -> p b s", s=6)
        mv0 = pr1[0:BT, o + 200:o + 200 + NB * 2].rearrange("p (b s) -> p b s", s=2)
        rstd0 = pr1[0:BT, o + 260:o + 260 + NB]
        tmp0 = [pr1[0:BT, a:a + NB] for a in (o + 290, o + 320)]
        bmin = pr1[0:ER, o + 350:o + 351]
        bmax = pr1[0:ER, o + 351:o + 352]
        bad = pr1[0:ER, o + 352:o + 353]
        badf = pr1[0:1, o + 353:o + 354]
        lateness = pr1[0:1, o + 354:o + 355]
        late_row = pr1[0:1, o + 360:o + 360 + ER]
        wnf = pr1[:, o + 420:o + 420 + KC * D].rearrange("p (k d) -> p k d", d=D)
        assert o + 420 + KC * D <= NEXP * 2 * KC * F // 2

        msg = part(RING * D).bitcast(f16).rearrange("p (q u a d) -> p q u a d", u=QT, a=2, d=D)
        oh = part(2 * QT * P // 2).bitcast(f16).rearrange("p (h u c) -> p h u c", u=QT, c=P)
        wstg1 = W1[:, NEXP - 1, :, :, :].rearrange("p s c f -> p (s c f)").bitcast(f32)
        wstg2 = W2[:, NEXP - 1, :, :, :].rearrange("p s c f -> p (s c f)").bitcast(f32)
        srcT = part(ET)
        relT = part(ETP)
        base_row = part(ER).bitcast(i32)
        stage = part(RING).bitcast(i32).rearrange("p (h u) -> p h u", u=QT)
        hx_h = part(D).bitcast(f16).rearrange("p (a d) -> p a d", d=D)
        hx_x = part(D)
        hT = part(2 * KC * BT // 2).bitcast(f16).rearrange("p (a k t) -> p a k t", a=2, k=KC)
        deg = part(BT)
        meanT = part(KC * BT).rearrange("p (k t) -> p k t", t=BT)
        xx = part(2 * D).rearrange("p (a d) -> p a d", d=D)
        xh = part(D).bitcast(f16).rearrange("p (a d) -> p a d", d=D)
        xtT = part(KC * BT).rearrange("p (k t) -> p k t", t=BT)
        stats = part(6)[0:BT, :]
        mv = part(2)[0:BT, :]
        rstd, *tmp = [stats[:, c:c + 1] for c in range(3)]
        at[0] = 0
        BK = NB * 2
        CH = BK // NG
        oh_row = part(BK * P)[0:BT, :].rearrange("p (j c) -> p j c", c=P)
        wstg3 = part(KC * F)
        agg_f = AGG[:, :, :].rearrange("p k c -> p (k c)")
        gT = agg_f[0:NEXP, 0:N].rearrange("p (b t) -> p b t", t=BT)
        AFTER_GT = N + 1
        ag = [AFTER_GT]

        def spare(words):
            a = ag[0]
            ag[0] += words
            assert ag[0] <= (KC + 1) * AGGW, ag[0]
            return agg_f[:, a:a + words]

        wt = spare(NB * 2)[0:BT, :].rearrange("p (b k) -> p b k", k=2)
        dl = spare(NB)[0:BT, :]
        e1 = spare(NB)[0:BT, :]
        oh2 = spare(NB * 2 * NEXP)[0:BT, :].rearrange("p (b k e) -> p b k e", k=2, e=NEXP)
        prod = spare(NB * 2 * NEXP)[0:BT, :].rearrange("p (b k e) -> p b k e", k=2, e=NEXP)
        gates = spare(NB * NEXP)[0:BT, :].rearrange("p (b e) -> p b e", e=NEXP)
        running = spare(2 * NEXP * NB)
        ohs, incl, excl, keep = [running[0:BT, c * NEXP * NB // 2:(c + 1) * NEXP * NB // 2].bitcast(f16) for c in range(4)]
        posb_w = spare(NEXP * NB)
        posb = posb_w[0:BT, :]
        tokf = spare(NB * 2)[0:BT, :].rearrange("p (b k) -> p b k", k=2)
        slotf = spare(BK)[0:BT, :]
        rowf, itemf, wts = [spare(BK)[0:BT, :] for _ in range(3)]
        sloti = spare(BK)[0:BT, :].bitcast(i32)
        pv = [spare(CH * 2 * NITEM)[0:BT, :].rearrange("p (j a i) -> p j a i", a=2, i=NITEM) for _ in range(2)]
        eq = [z[:, 0:CH * NITEM].rearrange("p (j i) -> p j i", i=NITEM)
              for z in (prod.rearrange("p b k e -> p (b k e)"), running[0:BT, :])]
        skip = posb_w[:, 0:NITEM]
        thr = spare(NTHR)
        cmp1 = posb_w[:, 0:NEXP * NTHR].rearrange("p (e k) -> p e k", k=NTHR)
        cnt, ntile, pincl, cmp2, scr = [spare(NEXP) for _ in range(5)]
        at[0] = 0
        xsr = part(4 * D).rearrange("p (s w) -> p s w", w=D)
        idx = part(4).bitcast(i32)
        xT = part(2 * 2 * KC * P // 2).bitcast(f16).rearrange("p (s a k t) -> p s a k t", s=2, a=2, k=KC)
        meta = part(4 * 2).rearrange("p (s w) -> p s w", w=2)
        b1e = part(2 * FC).rearrange("p (s c) -> p s c", c=FC)
        hr = part(2 * F).rearrange("p (s t) -> p s t", t=F)
        hh = part(2 * F // 2).bitcast(f16).rearrange("p (s t) -> p s t", t=F)
        hl = part(2 * F // 2).bitcast(f16).rearrange("p (s t) -> p s t", t=F)
        yo = part(4 * D).rearrange("p (s d) -> p s d", d=D)
        WPLACE = 2 * KC * F + 4 * FC * D
        agg_w = agg_f[:, AFTER_GT:AFTER_GT + WPLACE].bitcast(f16)
        w1e = agg_w[:, 0:4 * KC * F].rearrange("p (s a k f) -> p s a k f", s=2, a=2, k=KC)
        w2e = agg_w[:, 4 * KC * F:2 * WPLACE].rearrange("p (s a c d) -> p s a c d", s=4, a=2, c=FC)
        at[0] = 0
        part(4 * D + 4 + 4 * P + 2 * 4 + 2 * FC + 2 * F + 2 * F + 4 * D)
        XX3 = [part(GB * 2 * D)]
        a = AFTER_GT + WPLACE
        w1_f = W1[:, :, :, :, :].rearrange("p e s c f -> p (e s c f)").bitcast(f32)
        w2_f = W2[:, :, :, :, :].rearrange("p e s c f -> p (e s c f)").bitcast(f32)
        late = [f[:, s * GB * 2 * D:(s + 1) * GB * 2 * D] for f in (w1_f, w2_f) for s in range(6)]
        XX3 += late[0:NG - 1]
        XX3 = [z.rearrange("p (b a d) -> p b a d", a=2, d=D) for z in XX3]
        late = late[NG - 1:]
        Z = [z.rearrange("p (b k d) -> p b k d", k=2, d=D) for z in late[0:NG]]
        late = late[NG:]
        Y = [late[c // 2][:, c % 2 * GB * D:(c % 2 + 1) * GB * D].rearrange("p (b d) -> p b d", d=D) for c in range(NG)]
        b2s = agg_f[0:NEXP, a:a + D]
        gamma_b = agg_f[0:BT, a + D:a + 2 * D]
        assert a + 2 * D <= (KC + 1) * AGGW
        at[0] = 0
        stats3 = part(GB * 6).rearrange("p (b s) -> p b s", s=6)
        mv3 = [part(GB * 2)[0:BT, :].rearrange("p (b s) -> p b s", s=2) for _ in range(2)]
        rstd3 = [part(GB)[0:BT, :] for _ in range(2)]
        nmr3 = [part(GB)[0:BT, :] for _ in range(2)]
        tmp3 = [part(GB)[0:BT, :] for _ in range(2)]

        PS = ctx.enter_context(nc.psum_tensor("PS", [P, 8, 512], f32))
        p_agg = [PS[:, b * (KC + 1):(b + 1) * (KC + 1), 0:P] for b in range(2)]
        p_hT = PS[:, 6, 0:KC * P].bitcast(f16).rearrange("p (a k t) -> p a k t", a=2, k=KC)
        p_xT = PS[:, 6, KC * P:2 * KC * P].rearrange("p (k t) -> p k t", t=P)
        p_x1 = PS[0:BT, 7, 0:D]
        p_lg = PS[0:BT, 7, D:D + NEXP]
        p_pos = PS[0:BT, 0, 0:NEXP * NB]
        p_gT = PS[0:NEXP, 1:8, :].rearrange("p n (h t) -> p (n h) t", t=P)
        p_cnt = PS[:, 1, 0:NEXP]
        p_item = PS[0:1, 7, 2 * P:2 * P + NITEM]
        p_meta = PS[:, 0, 0:2 * NITEM].rearrange("p (a i) -> p a i", a=2)
        p_x16 = [PS[:, s, 0:256].bitcast(f16).rearrange("p (a k t) -> p a k t", a=2, k=KC) for s in range(2)]
        p_h = [PS[:, 2 + s, :] for s in range(2)]
        p_y = [PS[:, 4 + s, 0:D] for s in range(2)]
        p_sum = [PS[0:BT, 3 * s:3 * s + 3, :].rearrange("p n (h d) -> p (n h) d", d=D) for s in range(2)]

        const_loaded = sem("const_loaded")
        consts_made = sem("consts_made")
        edges_loaded = sem("edges_loaded")
        edge_pads = sem("edge_pads")
        x_loaded = [sem(f"x_loaded{c}") for c in range(NG)]
        h_made = sem("h_made")
        h_hi = sem("h_hi")
        h_lo = sem("h_lo")
        h_lo_dve = sem("h_lo_dve")
        flag_ready = sem("flag_ready")
        fb_staged = sem("fb_staged")
        fb_gathered = [sem(f"fb_gathered{u}") for u in range(TPR)]
        fb_oh = sem("fb_oh")
        fb_sums = sem("fb_sums")
        fb_done = sem("fb_done")
        fb_moved = sem("fb_moved")
        h_stored = sem("h_stored")
        dve_step = sem("dve_step")
        waits_passed = sem("waits_passed")
        rows_ready = sem("rows_ready")
        edge_T = sem("edge_T")
        edge_out = sem("edge_out")
        stage_ready = sem("stage_ready")
        gathered = [sem(f"gathered{u}") for u in range(QR)]
        oh_ready = sem("oh_ready")
        quads_done = sem("quads_done")
        adds_done = sem("adds_done")
        w1_loaded = sem("w1_loaded")
        w1_hi = sem("w1_hi")
        w1_lo = sem("w1_lo")
        w2_loaded = sem("w2_loaded")
        w2_hi = sem("w2_hi")
        w2_lo = sem("w2_lo")
        hxh_loaded = sem("hxh_loaded")
        hxx_loaded = sem("hxx_loaded")
        hT_made = sem("hT_made")
        hT_copied = sem("hT_copied")
        deg_step = sem("deg_step")
        mean_made = sem("mean_made")
        x1_summed = sem("x1_summed")
        x1_made = sem("x1_made")
        ln_step = sem("ln_step")
        xt_made = sem("xt_made")
        x1_ready = sem("x1_ready")
        xt_hi = sem("xt_hi")
        xt_lo = sem("xt_lo")
        xx_stored = sem("xx_stored")
        xh_stored = sem("xh_stored")
        xtT_made = sem("xtT_made")
        xtT_copied = sem("xtT_copied")
        logits = sem("logits")
        logits_out = sem("logits_out")
        top_step = sem("top_step")
        top_out = sem("top_out")
        tok_made = sem("tok_made")
        slots_made = sem("slots_made")
        oh_row_made = sem("oh_row_made")
        pv_made = sem("pv_made")
        eq_made = sem("eq_made")
        gate_step = sem("gate_step")
        chunk_done = sem("chunk_done")
        tok_of_made = sem("tok_of_made")
        meta_of_made = sem("meta_of_made")
        idx_made = sem("idx_made")
        gates_made = sem("gates_made")
        gT_made = sem("gT_made")
        gT_copied = sem("gT_copied")
        tail_loaded = sem("tail_loaded")
        delta = sem("delta")
        expd = sem("expd")
        ohs_made = sem("ohs_made")
        pos_made = sem("pos_made")
        counted = sem("counted")
        item_cols = sem("item_cols")
        item_T = sem("item_T")
        items_ready = sem("items_ready")
        xs_in = [sem(f"xs_in{s}") for s in range(4)]
        x16_made = sem("x16_made")
        x16_copied = sem("x16_copied")
        meta_taken = sem("meta_taken")
        w1_copied = sem("w1_copied")
        w2_copied = sem("w2_copied")
        l1_done = sem("l1_done")
        relu_done = sem("relu_done")
        hi_split = sem("hi_split")
        h_split = sem("h_split")
        l2_done = sem("l2_done")
        yo_ready = sem("yo_ready")
        yo_out = [sem(f"yo_out{s}") for s in range(4)]
        zx_loaded = [sem(f"zx_loaded{q}") for q in range(NG)]
        z_added = sem("z_added")
        summed = sem("summed")
        scaled = sem("scaled")
        stats_made = sem("stats_made")
        normed = sem("normed")
        out_ready = sem("out_ready")
        out_last = sem("out_last")
        out_stored = sem("out_stored")

        out_b = out.rearrange("(c b p) d -> c p b d", p=BT, b=GB)
        POOL_LOW = 3
        BANKED = [slice(b, min(b + 2, GB)) for b in range(0, GB, 2)]

        x_b = x.rearrange("(c b p) d -> c p b d", p=BT, b=GB)
        h_b = h_tab.rearrange("(c b p) d -> c p b d", p=BT, b=GB)
        DMA = 16

        def carry(engine):
            engine.sem_inc(waits_passed, 1)

        def counted_link(engine, signal, base):
            n = [0]

            def link(ins, alone=False):
                n[0] += 1
                ins.then_inc(signal, 1)
                engine.wait_ge(signal, base + n[0])
                if alone:
                    carry(engine)
            return link, n

        def rsqrt(v, link, var, tmp, y):
            link(v.tensor_scalar(tmp[0], var, EPS, None, ALU.add))
            link(v.tensor_scalar(tmp[1].bitcast(i32), tmp[0].bitcast(i32), 1, None, ALU.logical_shift_right))
            link(v.tensor_scalar(y.bitcast(i32), tmp[1].bitcast(i32), -1.0, float(0x5F3759DF), ALU.mult, ALU.add))
            for _ in range(3):
                link(v.scalar_tensor_tensor(tmp[1], y, -0.5, y, ALU.mult, ALU.mult))
                link(v.tensor_tensor(tmp[1], tmp[1], tmp[0], ALU.mult))
                link(v.scalar_tensor_tensor(y, tmp[1], 1.5, y, ALU.add, ALU.mult))

        def run_item(job, n, ahead, m):
            k = n + ahead
            if m is not None:
                job(k % 4, m + k // 4)
            elif 0 <= k < NITEM:
                job(k % 4, k // 4)

        block = ctx.enter_context(nc.Block())

        SPANS = [(0, LAG, "both", None), (LAG, LAG + 1, "both", "first"), (LAG + 1, NEXP - 1, "both", "block"),
                 (NEXP - 1, NEXP, "last w1", "block"), (NEXP, NIT - 1, None, "block"), (NIT - 1, NIT, None, "last")]
        LATE = [(0, 1, None, False, False), (1, LAG + 1, "both", False, False), (LAG + 1, LAG + 2, "both", True, False),
                (LAG + 2, NEXP, "both", True, True), (NEXP, NEXP + 1, "last w1", True, True), (NEXP + 1, NIT, None, True, True)]

        @block.sync
        def _(sp):
            full = ER - 1
            rest = E - full * L
            sp.wait_ge(edge_pads, 3)
            for t, a in ((srow, src), (drow, dst), (drow2, dst)):
                sp.dma_start(t[0:full, :], a[0:full * L].rearrange("(r c) -> r c", c=L)).then_inc(edges_loaded, DMA)
                sp.dma_start(t[full:ER, 0:rest], a[full * L:E].rearrange("(r c) -> r c", r=1)).then_inc(edges_loaded, DMA)
            for c in range(NG):
                sp.dma_start(X[:, c * GB:(c + 1) * GB, :], x_b[c]).then_inc(x_loaded[c], DMA)
            for t, a in ((wsf, w_self.rearrange("(k p) d -> p k d", p=P)),
                         (wnf, w_neigh.rearrange("(k p) d -> p k d", p=P)),
                         (gw[:, :, :], gate_w.rearrange("(k p) e -> p k e", p=P)),
                         (brow[:, :], gnn_b.rearrange("(a d) -> a d", a=1)),
                         (gb_b[:, :], gate_b.rearrange("(a d) -> a d", a=1).to_broadcast([BT, NEXP])),
                         (beta_b[:, :], beta.rearrange("(a d) -> a d", a=1).to_broadcast([BT, D])),
                         (b1rows, b1.rearrange("e (c f) -> (e c) f", f=P))):
                sp.dma_start(t, a).then_inc(const_loaded, DMA)
            for c in range(NG):
                if c < POOL_LOW:
                    sp.wait_ge(h_lo, c + 1)
                else:
                    sp.wait_ge(h_lo_dve, c - POOL_LOW + 1)
                sp.dma_start(h_b[c], H16[:, c * GB:(c + 1) * GB, :, :].rearrange("p b a d -> p b (a d)")).then_inc(h_stored, DMA)
            sp.wait_ge(h_stored, NG * DMA)
            sp.wait_ge(edge_out, 6)
            sp.sem_inc(w1_lo, 1)
            sp.sem_inc(w2_lo, 1)
            sp.sem_inc(hT_made, 1)
            sp.sem_inc(x1_made, 1)
            sp.sem_inc(xx_stored, DMA)
            sp.sem_inc(xh_stored, DMA)

            def block_load(j):
                sp.wait_ge(hT_made, j + 1)
                sp.dma_start(hx_h[0:BT, :, :], h_tab[bass.ds(j * BT, BT), :].rearrange("p (a d) -> p a d", a=2)).then_inc(hxh_loaded, DMA)
                sp.wait_ge(x1_made, j + 1)
                sp.dma_start(hx_x[0:BT, :], x[bass.ds(j * BT, BT), :]).then_inc(hxx_loaded, DMA)

            def block_store(j):
                sp.wait_ge(x1_ready, j + 1)
                sp.dma_start(xx_tab[bass.ds(j * BT, BT), :].rearrange("p (a d) -> p a d", a=2), xx[0:BT, :, :]).then_inc(xx_stored, DMA)
                sp.wait_ge(xt_lo, j + 1)
                carry(sp)
                sp.dma_start(xh_tab[bass.ds(j * BT, BT), :].rearrange("p (a d) -> p a d", a=2), xh[0:BT, :, :]).then_inc(xh_stored, DMA)

            for lo, hi, weights, own in SPANS:
                with sp.Fori(lo, hi) as i:
                    if weights == "both":
                        sp.wait_ge(w1_lo, i + 1)
                        sp.dma_start(wstg1.rearrange("p (k f) -> p k f", f=F),
                                     w1[bass.ds(i, 1), :, :].rearrange("e (k p) f -> p (e k) f", p=P)).then_inc(w1_loaded, DMA)
                        sp.wait_ge(w2_lo, i + 1)
                        sp.dma_start(wstg2.rearrange("p (c d) -> p c d", d=D),
                                     w2[bass.ds(i, 1), :, :].rearrange("e (c p) d -> p (e c) d", p=P)).then_inc(w2_loaded, DMA)
                    if weights == "last w1":
                        sp.wait_ge(w2_lo, NEXP)
                        sp.dma_start(wstg2.rearrange("p (k f) -> p k f", f=F),
                                     w1[NEXP - 1, :, :].rearrange("(k p) f -> p k f", p=P)).then_inc(w1_loaded, DMA)
                    if own:
                        block_load(i - LAG)
                    if own in ("block", "last"):
                        block_store(i - LAG - 1)
            block_load(NB - 1)
            block_store(NB - 2)
            block_store(NB - 1)
            sp.wait_ge(logits_out, NB)
            sp.wait_ge(xx_stored, (NB + 1) * DMA)
            sp.wait_ge(xh_stored, (NB + 1) * DMA)
            sp.dma_start(wstg3.rearrange("p (c d) -> p c d", d=D),
                         w2[NEXP - 1, :, :].rearrange("(c p) d -> p c d", p=P)).then_inc(w2_loaded, DMA)

            def xx_load(q):
                sp.dma_start(XX3[q][0:BT, :, :, :],
                             xx_tab[q * GT:(q + 1) * GT, :].rearrange("(b p) (a d) -> p b a d", p=BT, a=2)).then_inc(zx_loaded[q], DMA)

            sp.wait_ge(w2_lo, NEXP + 1)
            sp.wait_ge(x16_made, 4)
            xx_load(0)
            sp.dma_start(b2s, b2).then_inc(tail_loaded, DMA)
            sp.dma_start(gamma_b, gamma.rearrange("(a d) -> a d", a=1).to_broadcast([BT, D])).then_inc(tail_loaded, DMA)
            sp.wait_ge(w2_copied, NITEM)
            xx_load(1)
            for s in range(4):
                sp.wait_ge(yo_out[s], NITEM // 4 * DMA)
            for q in range(NG):
                if q >= 2:
                    xx_load(q)
                sp.dma_start(Z[q][0:BT, :, :, :],
                             z_tab[2 * q * GT:2 * (q + 1) * GT, :].rearrange("(b p k) d -> p b k d", p=BT, k=2)).then_inc(zx_loaded[q], DMA)
            for q in range(NG):
                if q < NG - 1:
                    sp.wait_ge(out_ready, q + 1)
                else:
                    sp.wait_ge(out_last, 1)
                sp.dma_start(out_b[q], Y[q][0:BT, :, :]).then_inc(out_stored, DMA)
            sp.wait_ge(out_stored, NG * DMA)

        @block.gpsimd
        def _(pool):
            g = nc.gpsimd
            g.iota(iota[:, :], [[1, P]], base=0, channel_multiplier=0, allow_small_or_imprecise_dtypes=True).then_inc(consts_made, 1)
            g.iota(iotap[:, :], [[0, 1]], base=0, channel_multiplier=1, allow_small_or_imprecise_dtypes=True).then_inc(consts_made, 1)
            g.iota(need[0:1, 1:ER + 1], [[BT, NIT], [0, 2]], base=-BT * (LAG - 1), channel_multiplier=0,
                   allow_small_or_imprecise_dtypes=True).then_inc(consts_made, 1)
            g.memset(ident[:, :], 0.0).then_inc(consts_made, 1)
            g.memset(lower[:, :], 0.0).then_inc(consts_made, 1)
            g.memset(bias_one[:, :], WSS).then_inc(consts_made, 1)
            g.memset(ones16[:, :], 1.0).then_inc(consts_made, 1)
            pool.wait_ge(consts_made, 3)
            g.memset(need[0:1, 0:1], 0.0).then_inc(consts_made, 1)
            pool.wait_ge(consts_made, 8)
            g.affine_select(out=ident[:, :], in_=ident[:, :], compare_op=ALU.not_equal, fill=1.0,
                            base=0, pattern=[[-1, P]], channel_multiplier=1).then_inc(consts_made, 1)
            g.affine_select(out=lower[:, :], in_=lower[:, :], compare_op=ALU.is_ge, fill=1.0,
                            base=0, pattern=[[-1, BT]], channel_multiplier=1).then_inc(consts_made, 1)
            g.tensor_copy(iota16[:, :], iota[:, :]).then_inc(consts_made, 1)
            pool.wait_ge(consts_made, 11)
            g.tensor_copy(ident16[:, :], ident[:, :]).then_inc(consts_made, 1)
            g.tensor_copy(lower16[:, :], lower[:, :]).then_inc(consts_made, 1)
            pool.wait_ge(edges_loaded, 6 * DMA)
            g.tensor_copy(srowf, srow).then_inc(rows_ready, 1)
            g.memset(AGG[:, :, :], 0.0).then_inc(consts_made, 1)
            for c in range(POOL_LOW):
                bs = slice(c * GB, (c + 1) * GB)
                pool.wait_ge(h_hi, c + 1)
                g.tensor_tensor(H16[:, bs, 1, :], H[:, bs, :], H16[:, bs, 0, :], ALU.subtract).then_inc(h_lo, 1)

            pool.wait_ge(h_stored, NG * DMA)
            pool.wait_ge(flag_ready, 1)
            flag = pool.value_load(irregular[0:1, 0:1], min_val=0, max_val=1)
            with pool.If(flag == 1):
                with pool.Fori(0, NWIN) as w:
                    with pool.Fori(0, ER) as r:
                        pool.wait_ge(fb_staged, ER * w + r + 1)
                        carry(pool)
                        for j in range(TPR):
                            g.indirect_dma_start(msg[:, j // QT, j % QT, :, :].rearrange("p a d -> p (a d)"), None, h_tab[:, :],
                                                 bass.IndirectOffsetOnAxis(ap=stage[:, j // QT, j % QT:j % QT + 1], axis=0)
                                                 ).then_inc(fb_gathered[j], DMA)
            with pool.Fori(0, NIT) as i:
                for s in range(QR):
                    pool.wait_ge(stage_ready, QR * i + s + 1)
                    carry(pool)
                    for u in range(QT):
                        g.indirect_dma_start(msg[:, s, u, :, :].rearrange("p a d -> p (a d)"), None, h_tab[:, :],
                                             bass.IndirectOffsetOnAxis(ap=stage[:, s, u:u + 1], axis=0)
                                             ).then_inc(gathered[s], DMA)

            pool.wait_ge(mean_made, NB)
            g.iota(tokf, [[2 * BT, NB], [1, 2]], base=1, channel_multiplier=2, allow_small_or_imprecise_dtypes=True).then_inc(tok_made, 1)
            pool.wait_ge(tok_made, 1)
            tok1 = tokf.rearrange("p b k -> p (b k)")
            for c in range(NG):
                js = slice(c * CH, (c + 1) * CH)
                pool.wait_ge(eq_made, c + 1)
                if c >= 2:
                    pool.wait_ge(chunk_done, c - 1)
                g.tensor_tensor(pv[c % 2][:, :, 0, :], eq[c % 2], tok1[:, js].unsqueeze(2).to_broadcast([BT, CH, NITEM]), ALU.mult).then_inc(pv_made, 1)
                g.tensor_tensor(pv[c % 2][:, :, 1, :], eq[c % 2], wts[:, js].unsqueeze(2).to_broadcast([BT, CH, NITEM]), ALU.mult).then_inc(pv_made, 1)
                if c == 0:
                    g.tensor_tensor(oh2, oh2, wt.unsqueeze(3).to_broadcast([BT, NB, 2, NEXP]), ALU.mult).then_inc(gate_step, 1)
                    pool.wait_ge(gate_step, 1)
                    g.tensor_tensor(gates, oh2[:, :, 0, :], oh2[:, :, 1, :], ALU.add).then_inc(gates_made, 1)

            def fetch(s, m):
                n = 4 * m + s
                pool.wait_ge(x16_copied, n + 1)
                carry(pool)
                g.tensor_copy(idx[:, s:s + 1], tok_of[:, bass.ds(n, 1)]).then_inc(idx_made, 1)
                pool.wait_ge(idx_made, n + 1)
                carry(pool)
                g.indirect_dma_start(xsr[:, s, :].bitcast(f16), None, xh_tab[:, :],
                                     bass.IndirectOffsetOnAxis(ap=idx[:, s:s + 1], axis=0)).then_inc(xs_in[s], DMA)

            def take(s, m):
                if not (isinstance(m, int) and m == 0):
                    pool.wait_ge(yo_out[s], DMA * m)
                carry(pool)
                g.tensor_copy(meta[:, s, :], meta_of[:, bass.ds(4 * m + s, 1), :].rearrange("p n w -> p (n w)")).then_inc(meta_taken, 1)

            def send(s, m):
                pool.wait_ge(yo_ready, 4 * m + s + 3)
                carry(pool)
                g.indirect_dma_start(z_tab[:, :], bass.IndirectOffsetOnAxis(ap=meta[:, s, 0:1].bitcast(i32), axis=0),
                                     yo[:, s, :], None, bounds_check=2 * N - 1, oob_is_err=False).then_inc(yo_out[s], DMA)

            def pool_step(n, m=None):
                for job, ahead in ((fetch, 6), (send, 0), (take, 2)):
                    run_item(job, n, ahead, m)

            pool.wait_ge(tok_of_made, 1)
            for n in range(-6, 4):
                if n == -2:
                    pool.wait_ge(meta_of_made, 2)
                pool_step(n)
            with pool.Fori(1, NITEM // 4 - 2) as m:
                for s in range(4):
                    pool_step(s, m)
            for n in range(NITEM - 8, NITEM):
                pool_step(n)

            def add_x1(q):
                pool.wait_ge(scaled, q + 1)
                g.tensor_tensor(Y[q][0:BT, :, :], Y[q][0:BT, :, :], XX3[q][0:BT, :, 0, :], ALU.add).then_inc(out_ready, 1)

            def add_z(q):
                pool.wait_ge(zx_loaded[q], 2 * DMA)
                for bs in BANKED:
                    g.tensor_tensor(Z[q][0:BT, bs, 0, :], Z[q][0:BT, bs, 0, :], Z[q][0:BT, bs, 1, :], ALU.add).then_inc(z_added, 1)

            for q in range(NG - 1):
                add_z(q)
            add_x1(0)
            add_z(NG - 1)
            for q in range(1, NG - 1):
                add_x1(q)

        @block.scalar
        def _(act):
            a = nc.scalar
            act.wait_ge(edge_T, 1)
            a.activation(srcT[:, 0:ET].rearrange("p (r j) -> p j r", j=TPR), PS[:, 0:TPR, 0:ER], ACT.Copy).then_inc(edge_out, 1)
            a.activation(relT[:, 0:ET].rearrange("p (r j) -> p j r", j=TPR), PS[:, 0:TPR, P:P + ER], ACT.Copy).then_inc(edge_out, 1)
            a.activation(base_row[0:1, :], PS[0:1, 0, 2 * P:2 * P + ER], ACT.Copy).then_inc(edge_out, 1)
            a.activation(b1T[:, :], PS[:, 2, 2 * P:2 * P + NEXP * FC], ACT.Copy).then_inc(edge_out, 1)
            for c in range(NG):
                bs = slice(c * GB, (c + 1) * GB)
                act.wait_ge(h_made, c + 1)
                a.activation(H16[:, bs, 0, :], H[:, bs, :], ACT.Copy).then_inc(h_hi, 1)
            act.wait_ge(edge_out, 6)
            act.wait_ge(h_stored, NG * DMA)
            act.wait_ge(flag_ready, 1)
            flag = act.value_load(irregular[0:1, 0:1], min_val=0, max_val=1)
            with act.If(flag == 1):
                with act.Fori(0, NWIN) as w:
                    with act.Fori(0, ER) as r:
                        act.wait_ge(fb_done, ER * w + r + 1)
                        a.activation(stage[:, 0:2, :], srcT[:, bass.ds(TPR * r, TPR)].rearrange("p (h u) -> p h u", u=QT),
                                     ACT.Copy).then_inc(fb_staged, 1)
                act.wait_ge(fb_done, ER * NWIN + 1)

            def stage_quad(i, s):
                act.wait_ge(quads_done, QR * i + s + 1)
                a.activation(stage[:, s, :], srcT[:, bass.ds(RING * i + QT * s, QT)], ACT.Copy).then_inc(stage_ready, 1)

            def hT_out(j):
                act.wait_ge(hT_made, j + 2)
                a.activation(hT, p_hT[:, :, :, 0:BT], ACT.Copy).then_inc(hT_copied, 1)

            def xt_high(j):
                act.wait_ge(xt_made, j + 1)
                act.wait_ge(xh_stored, DMA * (j + 1))
                a.activation(xh[0:BT, 0, :], xx[0:BT, 1, :], ACT.Copy).then_inc(xt_hi, 1)

            def xtT_out(j):
                act.wait_ge(xtT_made, j + 1)
                a.activation(xtT, p_xT[:, :, 0:BT], ACT.Copy).then_inc(xtT_copied, 1)

            for lo, hi, weights, first, second in LATE:
                with act.Fori(lo, hi) as i:
                    stage_quad(i, 0)
                    if second:
                        xt_high(i - LAG - 2)
                    stage_quad(i, 1)
                    if first:
                        hT_out(i - LAG - 1)
                    if second:
                        xtT_out(i - LAG - 2)
                    if weights == "both":
                        act.wait_ge(w1_loaded, DMA * i)
                        a.activation(W1[:, bass.ds(i - 1, 1), 0, :, :].rearrange("p e k f -> p (e k f)"), wstg1, ACT.Copy, scale=WS1).then_inc(w1_hi, 1)
                    if weights == "last w1":
                        act.wait_ge(w1_loaded, DMA * NEXP)
                        act.wait_ge(w1_lo, NEXP)
                        a.activation(W1[:, NEXP - 1, 0, :, :].rearrange("p k f -> p (k f)"), wstg2, ACT.Copy, scale=WS1).then_inc(w1_hi, 1)
                    stage_quad(i, 2)
                    stage_quad(i, 3)
                    if weights == "both":
                        act.wait_ge(w2_loaded, DMA * i)
                        a.activation(W2[:, bass.ds(i - 1, 1), 0, :, :].rearrange("p e c d -> p (e c d)"), wstg2, ACT.Copy, scale=WS2).then_inc(w2_hi, 1)
            xt_high(NB - 3)
            hT_out(NB - 2)
            xtT_out(NB - 3)
            xt_high(NB - 2)
            hT_out(NB - 1)
            xtT_out(NB - 2)
            xt_high(NB - 1)
            xtT_out(NB - 1)

            act.wait_ge(delta, 1)
            a.activation(e1, dl, ACT.Exp).then_inc(expd, 1)
            act.wait_ge(w2_loaded, DMA * NEXP)
            act.wait_ge(w1_lo, NEXP + 1)
            a.activation(W2[:, NEXP - 1, 0, :, :].rearrange("p c d -> p (c d)"), wstg3, ACT.Copy, scale=WS2).then_inc(w2_hi, 1)
            act.wait_ge(gT_made, 1)
            a.activation(gT, p_gT[:, 0:NB, 0:BT], ACT.Copy).then_inc(gT_copied, 1)

            def x_out(s, m):
                n = 4 * m + s
                act.wait_ge(x16_made, n + 1)
                act.wait_ge(l1_done, n + 1)
                a.activation(xT[:, s % 2, :, :, :], p_x16[s % 2], ACT.Copy).then_inc(x16_copied, 1)

            def relu(s, m):
                n = 4 * m + s
                act.wait_ge(l1_done, n + 3)
                act.wait_ge(w1_copied, n + 1)
                act.wait_ge(h_split, n + 1)
                for c in range(FC):
                    ins = a.activation(hr[:, s % 2, c * P:(c + 1) * P], p_h[s % 2][:, c * P:(c + 1) * P], ACT.Relu,
                                       bias=b1e[:, s % 2, c:c + 1], scale=1.0 / WS1)
                ins.then_inc(relu_done, 1)

            def high(s, m):
                n = 4 * m + s
                act.wait_ge(relu_done, n + 3)
                act.wait_ge(l2_done, n + 1)
                a.activation(hh[:, s % 2, :], hr[:, s % 2, :], ACT.Copy).then_inc(hi_split, 1)

            def weigh(s, m):
                n = 4 * m + s
                act.wait_ge(l2_done, n + 3)
                act.wait_ge(meta_taken, n + 1)
                if not (isinstance(m, int) and m == 0):
                    act.wait_ge(yo_out[s], DMA * m)
                a.activation(yo[:, s, :], p_y[s % 2], ACT.Copy, scale=meta[:, s, 1:2]).then_inc(yo_ready, 1)

            act.wait_ge(items_ready, 1)
            act.sem_inc(relu_done, 2)
            act.sem_inc(yo_ready, 2)
            act.sem_inc(x16_copied, 4)

            def act_step(n, m=None):
                for job, ahead in ((x_out, 3), (relu, 2), (high, 2), (weigh, 0)):
                    run_item(job, n, ahead, m)

            for n in range(-3, 4):
                act_step(n)
            with act.Fori(1, NITEM // 4 - 1) as m:
                for s in range(4):
                    act_step(s, m)
            for n in range(NITEM - 4, NITEM):
                act_step(n)

            for q in range(NG):
                act.wait_ge(stats_made, q + 1)
                for b in range(GB):
                    ins = a.activation(Y[q][0:BT, b, :], p_sum[q % 2][:, b, :], ACT.Identity,
                                       bias=nmr3[q % 2][:, b:b + 1], scale=rstd3[q % 2][:, b:b + 1])
                ins.then_inc(normed, 1)

        @block.tensor
        def _(pe):
            t = nc.tensor
            pe.wait_ge(consts_made, 14)
            pe.wait_ge(rows_ready, 3)
            for j in range(TPR):
                t.transpose(PS[:, j, 0:ER], srowf[:, j * P:(j + 1) * P], ident[0:ER, 0:ER])
                t.transpose(PS[:, j, P:P + ER], drowf[:, j * P:(j + 1) * P], ident[0:ER, 0:ER])
            t.transpose(PS[0:1, 0, 2 * P:2 * P + ER], bmin, ident[0:ER, 0:ER])
            t.transpose(PS[0:1, 1, 2 * P:2 * P + ER], bad, ident[0:ER, 0:ER])
            pe.wait_ge(const_loaded, 7 * DMA)
            ins = t.transpose(PS[:, 2, 2 * P:2 * P + NEXP * FC], b1rows, ident[0:NEXP * FC, 0:NEXP * FC])
            ins.then_inc(edge_T, 1)
            pe.wait_ge(edge_out, 6)
            pe.sem_inc(quads_done, QR)

            def tile_sums(bank, s, u, h, first, last):
                p = p_agg[bank]
                for k in range(KC):
                    for a in range(2):
                        t.matmul(p[:, k, :], msg[:, s, u, a, k * P:(k + 1) * P], oh[:, h, u, :],
                                 start=(first and a == 0), stop=(last and a == 1))
                return t.matmul(p[:, KC, :], ones16[:, :], oh[:, h, u, :], start=first, stop=last)

            pe.wait_ge(flag_ready, 1)
            flag = pe.value_load(irregular[0:1, 0:1], min_val=0, max_val=1)
            with pe.If(flag == 1):
                with pe.Fori(0, NWIN) as w:
                    with pe.Fori(0, ER) as r:
                        pe.wait_ge(fb_oh, 2 * (ER * w + r + 1))
                        pe.wait_ge(fb_done, ER * w + r + 1)
                        for j in range(TPR):
                            pe.wait_ge(fb_gathered[j], DMA * (ER * w + r + 1))
                            ins = tile_sums(0, j // QT, j % QT, j // QT, j == 0, j == TPR - 1)
                        ins.then_inc(fb_sums, 1)

            def turn_h(j):
                pe.wait_ge(hxh_loaded, DMA * (j + 1))
                for a in range(2):
                    for k in range(KC):
                        ins = t.transpose(p_hT[:, a, k, 0:BT], hx_h[0:BT, a, k * P:(k + 1) * P], ident16[0:BT, 0:BT])
                ins.then_inc(hT_made, 1)

            def x1_sum(j):
                pe.wait_ge(hT_copied, j + 1)
                pe.wait_ge(x1_made, j + 1)
                t.matmul(p_x1, bias_one[:, :], brow[:, :], start=True, stop=False)
                for ha, wa in ((0, 0), (1, 0), (0, 1)):
                    for k in range(KC):
                        t.matmul(p_x1, hT[:, ha, k, :], ws[:, wa, k, :], start=False, stop=False)
                pe.wait_ge(mean_made, j + 1)
                for k in range(KC):
                    ins = t.matmul(p_x1, meanT[:, k, :], wn[:, k, :], start=False, stop=(k == KC - 1))
                ins.then_inc(x1_summed, 1)

            def turn_xt(j):
                pe.wait_ge(xt_made, j + 1)
                for k in range(KC):
                    ins = t.transpose(p_xT[:, k, 0:BT], xx[0:BT, 1, k * P:(k + 1) * P], ident[0:BT, 0:BT])
                ins.then_inc(xtT_made, 1)

            def gate(j):
                pe.wait_ge(xtT_copied, j + 1)
                for k in range(KC):
                    ins = t.matmul(p_lg, xtT[:, k, :], gw[:, k, :], start=(k == 0), stop=(k == KC - 1))
                ins.then_inc(logits, 1)

            for lo, hi, weights, own in SPANS:
                with pe.Fori(lo, hi) as i:
                    for s in range(QR):
                        if s % 2 == 0:
                            pe.wait_ge(adds_done, 2 * i + s // 2 + 1)
                        pe.wait_ge(oh_ready, QR * i + s + 1)
                        pe.wait_ge(gathered[s], QT * DMA * (i + 1))
                        for u in range(QT):
                            ins = tile_sums(s // 2, s, u, s % 2, s % 2 == 0 and u == 0, s % 2 == 1 and u == QT - 1)
                        ins.then_inc(quads_done, 1)
                        if own and s == 1:
                            if own in ("block", "last"):
                                turn_xt(i - LAG - 1)
                            turn_h(i - LAG)
                        if own and s == 2:
                            x1_sum(i - LAG)
                            if own in ("block", "last"):
                                gate(i - LAG - 1)
            turn_xt(NB - 2)
            turn_h(NB - 1)
            x1_sum(NB - 1)
            gate(NB - 2)
            turn_xt(NB - 1)
            gate(NB - 1)

            pe.wait_ge(ohs_made, 1)
            t.matmul(p_cnt, ones16[0:BT, :], incl.rearrange("p (e b) -> p e b", b=NB)[:, :, NB - 1], start=True, stop=True).then_inc(counted, 1)
            t.matmul(p_pos, lower16[:, :], ohs, start=True, stop=False)
            t.matmul(p_pos, ones16[0:BT, 0:BT], excl, start=False, stop=True).then_inc(pos_made, 1)
            pe.wait_ge(item_cols, 1)
            t.transpose(p_item, scr[0:NITEM, 0:1], ident[0:NITEM, 0:NITEM]).then_inc(item_T, 1)
            for c in range(NG):
                pe.wait_ge(oh_row_made, c + 1)
                pe.wait_ge(pv_made, 2 * (c + 1))
                for j in range(CH):
                    ins = t.matmul(p_meta, oh_row[:, c * CH + j, :], pv[c % 2][:, j, :, :],
                                   start=(c == 0 and j == 0), stop=(c == NG - 1 and j == CH - 1))
                ins.then_inc(chunk_done, 1)
                if c == 0:
                    pe.wait_ge(gates_made, 1)
                    pe.wait_ge(items_ready, 1)
                    for b in range(NB):
                        ins = t.transpose(p_gT[:, b, 0:BT], gates[:, b, :], ident[0:BT, 0:BT])
                    ins.then_inc(gT_made, 1)
            def turn(s, m):
                n = 4 * m + s
                pe.wait_ge(xs_in[s], DMA * (m + 1))
                pe.wait_ge(x16_copied, n + 3)
                v = xsr[:, s, :].bitcast(f16).rearrange("p (a k h) -> p a k h", a=2, k=KC)
                for h in range(2):
                    for k in range(KC):
                        ins = t.transpose(p_x16[s % 2][:, h, k, :], v[:, h, k, :], ident16[:, :])
                ins.then_inc(x16_made, 1)

            def up(s, m):
                n = 4 * m + s
                pe.wait_ge(w1_copied, n + 1)
                pe.wait_ge(x16_copied, n + 5)
                pe.wait_ge(relu_done, n + 1)
                for c in range(FC):
                    terms = [(wa, xa, k) for wa, xa in ((0, 0), (0, 1), (1, 0)) for k in range(KC)]
                    for y, (wa, xa, k) in enumerate(terms):
                        ins = t.matmul(p_h[s % 2][:, c * P:(c + 1) * P], w1e[:, s % 2, wa, k, c * P:(c + 1) * P],
                                       xT[:, s % 2, xa, k, :], start=(y == 0), stop=(y == len(terms) - 1))
                ins.then_inc(l1_done, 1)

            def down(s, m):
                n = 4 * m + s
                pe.wait_ge(w2_copied, n + 1)
                pe.wait_ge(h_split, n + 3)
                pe.wait_ge(yo_ready, n + 1)
                terms = [(h, wa, c) for h, wa in ((hh, 0), (hh, 1), (hl, 0)) for c in range(FC)]
                for y, (h, wa, c) in enumerate(terms):
                    ins = t.matmul(p_y[s % 2], h[:, s % 2, c * P:(c + 1) * P], w2e[:, s, wa, c, :],
                                   start=(y == 0), stop=(y == len(terms) - 1))
                ins.then_inc(l2_done, 1)

            pe.wait_ge(items_ready, 1)
            pe.wait_ge(gT_copied, 1)
            pe.wait_ge(meta_of_made, 2)
            pe.sem_inc(l1_done, 2)
            pe.sem_inc(l2_done, 2)

            def pe_step(n, m=None):
                for job, ahead in ((turn, 3), (up, 2), (down, 0)):
                    run_item(job, n, ahead, m)

            for n in range(-3, 4):
                pe_step(n)
            with pe.Fori(1, NITEM // 4 - 1) as m:
                for s in range(4):
                    pe_step(s, m)
            for n in range(NITEM - 4, NITEM):
                pe_step(n)

            pe.wait_ge(tail_loaded, 2 * DMA)
            pe.wait_ge(yo_ready, NITEM + 2)
            for q in range(NG):
                s = q % 2
                pe.wait_ge(zx_loaded[q], 2 * DMA)
                if q >= 2:
                    pe.wait_ge(normed, q - 1)
                for b in range(GB):
                    pe.wait_ge(z_added, len(BANKED) * q + b // 2 + 1)
                    t.matmul(p_sum[s][:, b, :], ident[0:BT, 0:BT], XX3[q][0:BT, b, 1, :], start=True, stop=False)
                    t.matmul(p_sum[s][:, b, :], ident[0:BT, 0:BT], Z[q][0:BT, b, 0, :], start=False, stop=False)
                    ins = t.matmul(p_sum[s][:, b, :], gT[:, GB * q + b, :], b2s, start=False, stop=True)
                    if b % 2 == 1 or b == GB - 1:
                        ins.then_inc(summed, 1)

        @block.vector
        def _(dve):
            v = nc.vector

            v.memset(srow, 0).then_inc(edge_pads, 1)
            v.memset(drow, int(FAR)).then_inc(edge_pads, 1)
            v.memset(drow2, 0).then_inc(edge_pads, 1)
            link, n0 = counted_link(dve, dve_step, 0)
            dve.wait_ge(edges_loaded, 6 * DMA)
            v.tensor_copy(drowf, drow)
            link(v.tensor_copy(drowf2, drow2))
            link(v.tensor_reduce(bmin, drowf, AX.X, ALU.min))
            link(v.tensor_reduce(bmax, drowf2, AX.X, ALU.max))
            v.tensor_scalar(drowf, drowf, bmin, None, ALU.subtract).then_inc(rows_ready, 1)
            link(v.tensor_scalar(bmax, bmax, bmin, None, ALU.subtract))
            v.tensor_scalar(bad, bmax, float(P) - 0.5, None, ALU.is_gt).then_inc(rows_ready, 1)
            v.memset(relT[:, ET:ETP], FAR)
            for c in range(NG):
                dve.wait_ge(x_loaded[c], DMA)
                bs = range(c * GB, (c + 1) * GB)
                for b in bs:
                    ins = v.bn_stats(stats0[:, b, :], X[:, b, :])
                link(ins)
                for b in bs:
                    ins = v.bn_aggr(mv0[:, b, :], stats0[:, b, :])
            link(ins)
            rsqrt(v, link, mv0[:, :, 1], tmp0, rstd0)
            for c in range(NG):
                for b in range(c * GB, (c + 1) * GB):
                    ins = v.tensor_scalar(H[:, b, :], X[:, b, :], mv0[:, b, 0:1], rstd0[:, b:b + 1], ALU.subtract, ALU.mult)
                ins.then_inc(h_made, 1)
            for c in range(POOL_LOW, NG):
                bs = slice(c * GB, (c + 1) * GB)
                dve.wait_ge(h_made, c + 1)
                dve.wait_ge(h_hi, c + 1)
                v.tensor_tensor(H16[:, bs, 1, :], H[:, bs, :], H16[:, bs, 0, :], ALU.subtract).then_inc(h_lo_dve, 1)
            dve.wait_ge(const_loaded, 7 * DMA)
            v.tensor_scalar(wn[:, :, :], wnf, WSS, None, ALU.mult).then_inc(edge_out, 1)
            link(v.tensor_scalar(ws[:, 0, :, :], wsf, WSS, None, ALU.mult))
            v.scalar_tensor_tensor(ws[:, 1, :, :], wsf, WSS, ws[:, 0, :, :], ALU.mult, ALU.subtract).then_inc(edge_out, 1)
            dve.wait_ge(edge_out, 6)
            dve.wait_ge(consts_made, 14)
            v.tensor_reduce(badf, PS[0:1, 1, 2 * P:2 * P + ER], AX.X, ALU.max)
            link(v.tensor_tensor(late_row, need[:, 0:ER], PS[0:1, 0, 2 * P:2 * P + ER], ALU.subtract))
            link(v.tensor_reduce(lateness, late_row, AX.X, ALU.max))
            link(v.tensor_scalar(lateness, lateness, 0.5, None, ALU.is_gt))
            link(v.tensor_tensor(badf, badf, lateness, ALU.max))
            v.tensor_copy(irregular[:, :], badf).then_inc(flag_ready, 1)
            dve.wait_ge(flag_ready, 1)

            def onehots(r, h, signal):
                v.tensor_tensor(oh[:, h, :, :], iota16[:, :].unsqueeze(1).to_broadcast([P, QT, P]),
                                relT[:, bass.ds(TPR * r + QT * h, QT)].unsqueeze(2).to_broadcast([P, QT, P]),
                                ALU.is_equal).then_inc(signal, 1)

            flag = dve.value_load(irregular[0:1, 0:1], min_val=0, max_val=1)
            with dve.If(flag == 1):
                dve.sem_inc(fb_done, 1)
                dve.sem_inc(fb_moved, 1)
                with dve.Fori(0, NWIN) as w:
                    with dve.Fori(0, ER) as r:
                        dve.wait_ge(fb_moved, 2 * w + 1)
                        base = dve.value_load(base_row[0:1, bass.ds(r, 1)], min_val=0, max_val=N)
                        dve.wait_ge(fb_done, ER * w + r + 1)
                        carry(dve)
                        onehots(r, 0, fb_oh)
                        onehots(r, 1, fb_oh)
                        dve.wait_ge(fb_sums, ER * w + r + 1)
                        win = AGG[:, :, bass.ds(base, P)]
                        v.tensor_tensor(win, win, p_agg[0], ALU.add).then_inc(fb_done, 1)
                    dve.wait_ge(fb_done, ER * w + ER + 1)
                    v.tensor_scalar(relT[:, 0:ET], relT[:, 0:ET], -float(P), None, ALU.add).then_inc(fb_moved, 1)
                    v.tensor_scalar(base_row[0:1, :], base_row[0:1, :], float(P), float(N), ALU.add, ALU.min).then_inc(fb_moved, 1)
                dve.wait_ge(fb_moved, 2 * NWIN + 1)
                v.memset(relT[:, 0:ET], FAR).then_inc(fb_moved, 1)
                dve.wait_ge(fb_moved, 2 * NWIN + 2)

            def quad_onehots(r, h, ahead):
                if ahead is not None:
                    dve.wait_ge(quads_done, ahead + 1 + QR)
                onehots(r, h, oh_ready)

            def add(i, g):
                r = 2 * i + g
                base = dve.value_load(base_row[0:1, bass.ds(r, 1)], min_val=0, max_val=N)
                dve.wait_ge(quads_done, 2 * r + 2 + QR)
                dve.wait_ge(adds_done, r + 2)
                win = AGG[:, :, bass.ds(base, P)]
                v.tensor_tensor(win, win, p_agg[g], ALU.add).then_inc(adds_done, 1)

            dve.sem_inc(adds_done, 2)
            quad_onehots(0, 0, None)
            quad_onehots(0, 1, None)
            def mean(j):
                link, _ = counted_link(dve, deg_step, 2 * j)
                link(v.tensor_scalar_max(deg, AGG[:, KC, bass.ds(j * BT, BT)], 1.0), alone=True)
                link(v.reciprocal(deg, deg))
                v.tensor_tensor(meanT, AGG[:, 0:KC, bass.ds(j * BT, BT)], deg.unsqueeze(1).to_broadcast([P, KC, BT]),
                                ALU.mult).then_inc(mean_made, 1)

            LN_STEPS = 15

            def x1_norm(j):
                link, n = counted_link(dve, ln_step, LN_STEPS * j)
                x1, xt = xx[0:BT, 0, :], xx[0:BT, 1, :]
                dve.wait_ge(x1_summed, j + 1)
                dve.wait_ge(hxx_loaded, DMA * (j + 1))
                dve.wait_ge(xx_stored, DMA * (j + 1))
                v.scalar_tensor_tensor(x1, p_x1, 1.0 / WSS, hx_x[0:BT, :], ALU.mult, ALU.add).then_inc(x1_made, 1)
                dve.wait_ge(x1_made, j + 2)
                carry(dve)
                link(v.bn_stats(stats, x1), alone=True)
                link(v.bn_aggr(mv, stats))
                rsqrt(v, link, mv[:, 1:2], tmp, rstd)
                v.tensor_scalar(xt, x1, mv[:, 0:1], rstd, ALU.subtract, ALU.mult).then_inc(xt_made, 1)
                dve.wait_ge(xt_made, j + 1)
                v.tensor_tensor(x1, x1, beta_b[:, :], ALU.add).then_inc(x1_ready, 1)
                dve.sem_inc(ln_step, LN_STEPS - n[0])

            def xt_low(j):
                dve.wait_ge(xt_hi, j + 1)
                v.tensor_tensor(xh[0:BT, 1, :], xx[0:BT, 1, :], xh[0:BT, 0, :], ALU.subtract).then_inc(xt_lo, 1)

            def gate_out(j):
                dve.wait_ge(logits, j + 1)
                v.tensor_tensor(lg[:, :], p_lg, gb_b[:, :], ALU.add).then_inc(logits_out, 1)
                dve.wait_ge(logits_out, j + 1)
                dve.wait_ge(top_out, 2 * j + 2)
                carry(dve)
                v.max(m8[:, :], lg[:, :]).then_inc(top_step, 1)
                dve.wait_ge(top_step, 2 * j + 1)
                carry(dve)
                v.max_index(i8[:, :], m8[:, :], lg[:, :]).then_inc(top_step, 1)
                v.tensor_copy(val[:, bass.ds(j, 1), :].rearrange("p b k -> p (b k)"), m8[:, 0:2]).then_inc(top_out, 1)
                dve.wait_ge(top_step, 2 * j + 2)
                v.tensor_copy(idxf[:, bass.ds(j, 1), :].rearrange("p b k -> p (b k)"), i8[:, 0:2]).then_inc(top_out, 1)

            dve.sem_inc(top_out, 2)
            for lo, hi, weights, own in SPANS:
                with dve.Fori(lo, hi) as i:
                    quad_onehots(2 * i + 1, 0, QR * i)
                    quad_onehots(2 * i + 1, 1, QR * i + 1)
                    add(i, 0)
                    if own:
                        dve.wait_ge(adds_done, 2 * i + 3)
                        mean(i - LAG)
                    if own in ("block", "last"):
                        xt_low(i - LAG - 1)
                    if own != "last":
                        quad_onehots(2 * i + 2, 0, QR * i + 2)
                    if weights == "both":
                        dve.wait_ge(w1_hi, i + 1)
                        w = W1[:, bass.ds(i, 1), :, :, :].rearrange("p e a k f -> p (e a) (k f)")
                        v.scalar_tensor_tensor(w[:, 1, :], wstg1, WS1, w[:, 0, :], ALU.mult, ALU.subtract).then_inc(w1_lo, 1)
                    if weights == "last w1":
                        dve.wait_ge(w1_hi, NEXP)
                        w = W1[:, NEXP - 1, :, :, :].rearrange("p a k f -> p a (k f)")
                        v.scalar_tensor_tensor(w[:, 1, :], wstg2, WS1, w[:, 0, :], ALU.mult, ALU.subtract).then_inc(w1_lo, 1)
                    if own in ("block", "last"):
                        gate_out(i - LAG - 1)
                    if own == "last":
                        x1_norm(i - LAG)
                    else:
                        quad_onehots(2 * i + 2, 1, QR * i + 3)
                    add(i, 1)
                    if weights == "both":
                        dve.wait_ge(w2_hi, i + 1)
                        w = W2[:, bass.ds(i, 1), :, :, :].rearrange("p e a c d -> p (e a) (c d)")
                        v.scalar_tensor_tensor(w[:, 1, :], wstg2, WS2, w[:, 0, :], ALU.mult, ALU.subtract).then_inc(w2_lo, 1)
                    if own and own != "last":
                        x1_norm(i - LAG)
            dve.wait_ge(adds_done, ER + 2)
            mean(NB - 1)
            xt_low(NB - 2)
            dve.wait_ge(mean_made, NB)
            link, n1 = counted_link(dve, dve_step, n0[0])
            by_expert = lambda ap: ap.rearrange("p (e b) -> p e b", b=NB)
            v.tensor_scalar(thr, iota[:, 0:NTHR], float(P), None, ALU.mult)
            link(v.memset(keep, 1.0))
            link(v.memset(by_expert(keep)[:, :, 0], 0.0))
            gate_out(NB - 2)
            x1_norm(NB - 1)
            xt_low(NB - 1)
            gate_out(NB - 1)
            dve.wait_ge(top_out, 2 * NB + 2)
            v.tensor_tensor(dl, val[:, :, 1], val[:, :, 0], ALU.subtract).then_inc(delta, 1)
            link(v.tensor_tensor(oh2, iota[0:BT, 0:NEXP].unsqueeze(1).unsqueeze(1).to_broadcast([BT, NB, 2, NEXP]),
                                 idxf[:, :, :].unsqueeze(3).to_broadcast([BT, NB, 2, NEXP]), ALU.is_equal))
            link(v.tensor_tensor(by_expert(ohs), oh2[:, :, 0, :].rearrange("p b e -> p e b"),
                                 oh2[:, :, 1, :].rearrange("p b e -> p e b"), ALU.add))
            link(v.tensor_tensor_scan(incl, keep, ohs, 0.0, ALU.mult, ALU.add))
            v.tensor_tensor(excl, incl, ohs, ALU.subtract).then_inc(ohs_made, 1)
            dve.wait_ge(expd, 1)
            link(v.tensor_scalar_add(dl, e1, 1.0))
            link(v.reciprocal(wt[:, :, 0], dl))
            link(v.tensor_tensor(wt[:, :, 1], e1, wt[:, :, 0], ALU.mult))
            link(v.tensor_scalar(wts, wt.rearrange("p b k -> p (b k)"), 1.0 / WS2, None, ALU.mult))
            dve.wait_ge(counted, 1)
            link(v.tensor_copy(cnt, p_cnt))
            link(v.tensor_tensor(cmp1, cnt.unsqueeze(2).to_broadcast([P, NEXP, NTHR]),
                                 thr.unsqueeze(1).to_broadcast([P, NEXP, NTHR]), ALU.is_gt))
            link(v.tensor_reduce(ntile, cmp1, AX.X, ALU.add))
            link(v.tensor_tensor_scan(pincl, ones16[:, 0:NEXP], ntile, 0.0, ALU.mult, ALU.add))
            link(v.tensor_tensor(cmp2, pincl, ntile, ALU.subtract))
            link(v.tensor_scalar(cmp2, cmp2, float(P), None, ALU.mult))
            dve.wait_ge(pos_made, 1)
            link(v.tensor_tensor(by_expert(posb), by_expert(p_pos), cmp2[0:BT, :].unsqueeze(2).to_broadcast([BT, NEXP, NB]), ALU.add))
            link(v.tensor_tensor(prod, oh2, by_expert(posb).rearrange("p e b -> p b e").unsqueeze(2).to_broadcast([BT, NB, 2, NEXP]), ALU.mult))
            link(v.tensor_reduce(slotf.rearrange("p (b k) -> p b k", k=2), prod, AX.X, ALU.add))
            link(v.tensor_copy(sloti, slotf))
            link(v.tensor_scalar(sloti, sloti, P.bit_length() - 1, None, ALU.logical_shift_right))
            link(v.tensor_copy(itemf, sloti))
            dve.wait_ge(quads_done, 2 * ER + QR)
            dve.wait_ge(xx_stored, (NB + 1) * DMA)
            dve.wait_ge(xh_stored, (NB + 1) * DMA)
            v.scalar_tensor_tensor(rowf, itemf, -float(P), slotf, ALU.mult, ALU.add).then_inc(slots_made, 1)
            dve.wait_ge(slots_made, 1)
            link(v.tensor_scalar(cmp2, pincl, iotap[:, :], None, ALU.is_le))
            link(v.tensor_reduce(scr[:, 2:3], cmp2, AX.X, ALU.add))
            v.tensor_scalar_min(scr[:, 0:1], scr[:, 2:3], float(NEXP - 1)).then_inc(item_cols, 1)
            for c in range(NG):
                js = slice(c * CH, (c + 1) * CH)
                if c >= 2:
                    dve.wait_ge(pv_made, 2 * (c - 1))
                v.tensor_tensor(eq[c % 2], iota[0:BT, 0:NITEM].unsqueeze(1).to_broadcast([BT, CH, NITEM]),
                                itemf[:, js].unsqueeze(2).to_broadcast([BT, CH, NITEM]), ALU.is_equal).then_inc(eq_made, 1)
                v.tensor_tensor(oh_row[:, js, :], iota[0:BT, :].unsqueeze(1).to_broadcast([BT, CH, P]),
                                rowf[:, js].unsqueeze(2).to_broadcast([BT, CH, P]), ALU.is_equal).then_inc(oh_row_made, 1)
                if c == 0:
                    dve.wait_ge(item_T, 1)
                    v.tensor_copy(items[:, 0:NITEM], p_item).then_inc(items_ready, 1)
            dve.wait_ge(chunk_done, NG)
            link(v.tensor_scalar(tok_of[:, 0:NITEM], p_meta[:, 0, :], -1.0, 0.0, ALU.add, ALU.max))
            v.tensor_scalar(tok_of[:, 0:NITEM], tok_of[:, 0:NITEM], 1, None, ALU.logical_shift_right).then_inc(tok_of_made, 1)
            link(v.tensor_scalar(skip, p_meta[:, 0, :], 0.5, float(SKIP), ALU.is_lt, ALU.mult))
            v.scalar_tensor_tensor(meta_of[:, 0:NITEM, 0].bitcast(i32), p_meta[:, 0, :], -1.0, skip, ALU.add, ALU.add).then_inc(meta_of_made, 1)
            v.tensor_copy(meta_of[:, 0:NITEM, 1], p_meta[:, 1, :]).then_inc(meta_of_made, 1)
            dve.wait_ge(w2_hi, NEXP)
            w = W2[:, NEXP - 1, :, :, :].rearrange("p a c d -> p a (c d)")
            v.scalar_tensor_tensor(w[:, 1, :], wstg3, WS2, w[:, 0, :], ALU.mult, ALU.subtract).then_inc(w2_lo, 1)
            dve.wait_ge(items_ready, 1)
            base2 = n0[0] + n1[0]

            def load_w(s, m):
                n = 4 * m + s
                e = dve.value_load(items[0:1, bass.ds(n, 1)], min_val=0, max_val=NEXP - 1)
                dve.wait_ge(l1_done, n + 1)
                dve.wait_ge(relu_done, n + 1)
                v.tensor_copy(b1e[:, s % 2, :], b1T[:, bass.ds(e * FC, FC)])
                v.tensor_copy(w1e[:, s % 2, :, :, :].rearrange("p a k f -> p (a k f)"),
                              W1[:, bass.ds(e, 1), :, :, :].rearrange("p e a k f -> p (e a k f)")).then_inc(w1_copied, 1)
                if not (isinstance(m, int) and m == 0):
                    dve.wait_ge(l2_done, 4 * (m - 1) + s + 3)
                v.tensor_copy(w2e[:, s, :, :, :].rearrange("p a c d -> p (a c d)"),
                              W2[:, bass.ds(e, 1), :, :, :].rearrange("p e a c d -> p (e a c d)")).then_inc(w2_copied, 1)

            def split(s, m):
                n = 4 * m + s
                dve.wait_ge(hi_split, n + 1)
                v.tensor_tensor(hl[:, s % 2, :], hr[:, s % 2, :], hh[:, s % 2, :], ALU.subtract).then_inc(h_split, 1)

            dve.wait_ge(gT_made, 1)
            dve.wait_ge(w2_lo, NEXP + 1)
            dve.sem_inc(h_split, 2)

            def dve_step_of(n, m=None):
                for job, ahead in ((load_w, 3), (split, 2)):
                    run_item(job, n, ahead, m)

            for n in range(-3, 4):
                dve_step_of(n)
            with dve.Fori(1, NITEM // 4 - 1) as m:
                for s in range(4):
                    dve_step_of(s, m)
            for n in range(NITEM - 4, NITEM):
                dve_step_of(n)

            dve.wait_ge(tail_loaded, 2 * DMA)
            link, _ = counted_link(dve, dve_step, base2)
            for q in range(NG + 1):
                if q < NG:
                    s = q % 2
                    for b in range(GB):
                        dve.wait_ge(summed, len(BANKED) * q + b // 2 + 1)
                        ins = v.bn_stats(stats3[0:BT, b, :], p_sum[s][:, b, :])
                    link(ins)
                    for b in range(GB):
                        ins = v.bn_aggr(mv3[s][:, b, :], stats3[0:BT, b, :])
                    link(ins)
                    rsqrt(v, link, mv3[s][:, :, 1], tmp3, rstd3[s])
                    v.scalar_tensor_tensor(nmr3[s], mv3[s][:, :, 0], -1.0, rstd3[s], ALU.mult, ALU.mult).then_inc(stats_made, 1)
                if q >= 1:
                    y = Y[q - 1][0:BT, :, :]
                    dve.wait_ge(normed, q)
                    v.tensor_tensor(y, y, gamma_b[:, :].unsqueeze(1).to_broadcast([BT, GB, D]), ALU.mult).then_inc(scaled, 1)
            dve.wait_ge(scaled, NG)
            dve.wait_ge(zx_loaded[NG - 1], 2 * DMA)
            v.tensor_tensor(y, y, XX3[NG - 1][0:BT, :, 0, :], ALU.add).then_inc(out_last, 1)


_INS = ["x", "src", "dst", "L0_gnn_W_self", "L0_gnn_W_neigh", "L0_gnn_b", "L0_ffn_gate_w", "L0_ffn_gate_b",
        "L0_ffn_w1", "L0_ffn_b1", "L0_ffn_w2", "L0_ffn_b2", "L0_ffn_gamma", "L0_ffn_beta"]


def kernel(**inputs):
    import numpy as np
    import concourse.bacc as bacc
    from concourse import mybir as mb
    from concourse.bass_utils import run_bass_kernel_spmd

    nc = bacc.Bacc("TRN2", target_bir_lowering=False, num_devices=1)
    arrays, args = {}, []
    for name in _INS:
        a = np.ascontiguousarray(inputs[name])
        arrays[f"in_{name}"] = a
        args.append(nc.dram_tensor(f"in_{name}", a.shape, mb.dt.from_np(a.dtype), kind="ExternalInput").ap())
    args.append(nc.dram_tensor("out_0", (N, D), mb.dt.float32, kind="ExternalOutput").ap())
    build(nc, *args)
    r = run_bass_kernel_spmd(nc, [arrays], core_ids=[0])
    return r.results[0]["out_0"]
```
